# Optimizing a Trainium2 kernel written in Bass

```python
import numpy as np
import jax
import jax.numpy as jnp

def _softmax(x, axis=-1):
    return jax.nn.softmax(x, axis=axis)

def _gelu(x):
    return jax.nn.gelu(x, approximate=True)

def _silu(x):
    return jax.nn.silu(x)

def _sigmoid(x):
    return jax.nn.sigmoid(x)

def _layernorm(x, axis=-1, eps=1e-05):
    m = jnp.mean(x, axis=axis, keepdims=True)
    v = jnp.var(x, axis=axis, keepdims=True)
    return (x - m) / jnp.sqrt(v + eps)

def _scatter_add(tgt, idx, src, axis=0):
    return tgt.at[idx].add(src)

def _segment_sum(src, seg, n):
    return jax.ops.segment_sum(src, seg, n)
kernel_name = 'mk_decoder_preln_d2_seqx_r8_3eb0c1'

def setup_inputs(seed: int=0):
    np.random.seed(seed)
    _w = jnp.asarray

    def _rec_inputs():
        import jax
        import jax.numpy as jnp
        _rk = jax.random.key(seed)
        x = -0.0002928 + 1 * jax.random.normal(jax.random.fold_in(_rk, 1), (4, 256, 128), jnp.float32)
        _lenS = 256 - jax.random.randint(jax.random.fold_in(_rk, 7), (4,), 0, max(1, 256 // 4) + 1, jnp.int32)
        _lenS2 = 256 - jax.random.randint(jax.random.fold_in(_rk, 8), (4,), 0, max(1, 256 // 4) + 1, jnp.int32)
        _ctx_1024P = jax.random.normal(jax.random.fold_in(_rk, 11), (4, 16, 128), jnp.float32)
        _ctx_1024c = jax.random.dirichlet(jax.random.fold_in(_rk, 511), 0.3 * jnp.ones((16,), jnp.float32), (4, 256))
        _ctx_1024t = jnp.einsum('bsk,bkd->bsd', _ctx_1024c, _ctx_1024P)
        _ctx_1024t = _ctx_1024t * jax.lax.rsqrt(jnp.mean(jnp.square(_ctx_1024t)) + 1e-12) * 0.953939
        ctx_1024 = -1.39393e-06 + 0.999914 * (_ctx_1024t + 0.3 * jax.random.normal(jax.random.fold_in(_rk, 611), (4, 256, 128), jnp.float32))
        fside_SxS2_0 = 0.000675642 + 1.00031 * jax.random.normal(jax.random.fold_in(_rk, 13), (256, 256), jnp.float32)
        _validS = jnp.arange(256)[None, :] < _lenS[:, None]
        _validS2 = jnp.arange(256)[None, :] < _lenS2[:, None]
        _causal = jnp.tril(jnp.ones((256, 256), dtype=bool))
        mask_B_ik0 = jnp.where(jnp.ones((4,), dtype=bool), 69, 1564).astype(jnp.int32)
        mask_BxS2_bk0 = jnp.logical_not(jnp.broadcast_to(_validS2[:, :], (4, 256)))
        return (x, ctx_1024, fside_SxS2_0, mask_B_ik0, mask_BxS2_bk0)
    x, ctx_1024, fside_SxS2_0, mask_B_ik0, mask_BxS2_bk0 = _rec_inputs()

    def _L0_attn_setup():
        import jax, jax.numpy as jnp
        import numpy as np
        N_HEADS = 16

        def _heads(x, h):
            B, T, D = x.shape
            return x.reshape(B, T, h, D // h).transpose(0, 2, 1, 3)

        def _reference_tuple_inner(x, Wq, Wk, Wv, Wo, Wg, bg):
            h = N_HEADS
            q = _heads(x @ Wq.T, h)
            k = _heads(x @ Wk.T, h)
            v = _heads(x @ Wv.T, h)
            g = _heads(jax.nn.sigmoid(x @ Wg.T + bg), h)
            qf = jax.nn.softplus(q) * (g + 1e-06)
            kf = jax.nn.softplus(k)
            kv = kf[..., :, None] * v[..., None, :]
            kv_cum = jnp.cumsum(kv, axis=2)
            z_cum = jnp.cumsum(kf, axis=2)
            num = jnp.einsum('bhtd,bhtde->bhte', qf, kv_cum)
            den = jnp.einsum('bhtd,bhtd->bht', qf, z_cum) + 1e-06
            out = num / den[..., None]
            B, _, T, dh = out.shape
            out = out.transpose(0, 2, 1, 3).reshape(B, T, h * dh)
            out = out @ Wo.T
            return (out, kv_cum[:, :, -1], z_cum[:, :, -1])
        key = jax.random.key(seed)
        B, T, D = (1, 256, 128)
        ks = jax.random.split(key, 7)
        s = 0.02
        return {'x': jax.random.normal(ks[0], (B, T, D), jnp.float32), 'Wq': jax.random.normal(ks[1], (D, D), jnp.float32) * s, 'Wk': jax.random.normal(ks[2], (D, D), jnp.float32) * s, 'Wv': jax.random.normal(ks[3], (D, D), jnp.float32) * s, 'Wo': jax.random.normal(ks[4], (D, D), jnp.float32) * s, 'Wg': jax.random.normal(ks[5], (D, D), jnp.float32) * s, 'bg': jax.random.normal(ks[6], (D,), jnp.float32) * s}
    _L0_attn_all = _L0_attn_setup()
    _L0_attn_in = {k: v for k, v in _L0_attn_all.items() if k in ('Wq', 'Wk', 'Wv', 'Wo', 'Wg', 'bg')}
    del _L0_attn_all

    def _L0_xattn_setup():
        import jax, jax.numpy as jnp
        import numpy as np
        NEG = -1000000.0
        key = jax.random.key(seed)
        ks = jax.random.split(key, 8)
        B, S, D = (2, 256, 128)
        query = jax.random.normal(ks[0], (B, S, D), jnp.float32)
        key_t = jax.random.normal(ks[1], (B, S, D), jnp.float32)
        value = jax.random.normal(ks[2], (B, S, D), jnp.float32)
        valid_len = jax.random.randint(ks[3], (B,), 1, S + 1, jnp.int32)
        s = 1.0 / np.sqrt(D)
        W_q = jax.random.normal(ks[4], (D, D), jnp.float32) * s
        W_k = jax.random.normal(ks[5], (D, D), jnp.float32) * s
        W_v = jax.random.normal(ks[6], (D, D), jnp.float32) * s
        W_o = jax.random.normal(ks[7], (D, D), jnp.float32) * s
        return {'query': query, 'key': key_t, 'value': value, 'valid_len': valid_len, 'W_q': W_q, 'W_k': W_k, 'W_v': W_v, 'W_o': W_o}
    _L0_xattn_all = _L0_xattn_setup()
    _L0_xattn_in = {k: v for k, v in _L0_xattn_all.items() if k in ('W_q', 'W_k', 'W_v', 'W_o')}
    del _L0_xattn_all

    def _L0_ffn_setup():
        import jax, jax.numpy as jnp
        import numpy as np
        EPS = 1e-09
        RMS_EPS = 1e-06
        TOP_K = 2
        LOOPS = 2

        def _rmsnorm(x, w):
            var = jnp.mean(x * x, axis=-1, keepdims=True)
            return x * jax.lax.rsqrt(var + RMS_EPS) * w

        def _swiglu(x, w1, w3, w2):
            h = jax.nn.silu(x @ w1) * (x @ w3)
            return h @ w2
        key = jax.random.key(seed)
        ks = jax.random.split(key, 5)
        B, S, D, F, E = (4, 256, 128, 256, 8)
        z = jax.random.normal(ks[0], (B, S, D), dtype=jnp.float32)
        norm_w = jnp.ones((D,), dtype=jnp.float32)
        router_w = jax.random.normal(ks[1], (D, E), dtype=jnp.float32) * 0.02
        w1 = jax.random.normal(ks[2], (E, D, F), dtype=jnp.float32) * 0.02
        w3 = jax.random.normal(ks[3], (E, D, F), dtype=jnp.float32) * 0.02
        w2 = jax.random.normal(ks[4], (E, F, D), dtype=jnp.float32) * 0.02
        return {'z': z, 'norm_w': norm_w, 'router_w': router_w, 'w1': w1, 'w3': w3, 'w2': w2}
    _L0_ffn_all = _L0_ffn_setup()
    _L0_ffn_in = {k: v for k, v in _L0_ffn_all.items() if k in ('norm_w', 'router_w', 'w1', 'w3', 'w2')}
    del _L0_ffn_all

    def _L1_attn_setup():
        import jax, jax.numpy as jnp
        import numpy as np
        D_INNER = 128
        STATE = 16
        DT_RANK = 64
        LOG_EPS = -7.0
        CLAMP = 20.0
        key = jax.random.key(seed)
        ks = jax.random.split(key, 4)
        B, L = (2, 128)
        x = jax.random.normal(ks[0], (B, L, D_INNER), jnp.float32)
        W_xproj = jax.random.normal(ks[1], (D_INNER, DT_RANK + 2 * STATE), jnp.float32) * 0.02
        W_dt = jax.random.normal(ks[2], (DT_RANK, D_INNER), jnp.float32) * 0.02
        b_dt = jax.random.normal(ks[3], (D_INNER,), jnp.float32) * 0.02
        A_log = jnp.log(jnp.tile(jnp.arange(1, STATE + 1, dtype=jnp.float32), (D_INNER, 1)))
        D = jnp.ones((D_INNER,), jnp.float32)
        return {'x': x, 'W_xproj': W_xproj, 'W_dt': W_dt, 'b_dt': b_dt, 'A_log': A_log, 'D': D}
    _L1_attn_all = _L1_attn_setup()
    _L1_attn_in = {k: v for k, v in _L1_attn_all.items() if k in ('W_xproj', 'W_dt', 'b_dt', 'A_log', 'D')}
    del _L1_attn_all

    def _L1_xattn_setup():
        import jax, jax.numpy as jnp
        import numpy as np
        B, L, S, E, H = (4, 256, 256, 128, 16)
        DH = E // H
        SCALING = DH ** (-0.5)

        def _split_heads(x):
            b, t, _ = x.shape
            return x.reshape(b, t, H, DH).transpose(0, 2, 1, 3)
        key = jax.random.key(seed)
        ks = jax.random.split(key, 14)
        std = 0.02
        return {'query': jax.random.normal(ks[0], (B, L, E), jnp.float32), 'key': jax.random.normal(ks[1], (B, S, E), jnp.float32), 'value': jax.random.normal(ks[2], (B, S, E), jnp.float32), 'attn_mask': jax.random.normal(ks[3], (L, S), jnp.float32), 'key_padding_mask': jax.random.randint(ks[4], (B, S), 0, 2).astype(bool), 'Wq': jax.random.normal(ks[5], (E, E), jnp.float32) * std, 'bq': jax.random.normal(ks[6], (E,), jnp.float32) * std, 'Wk': jax.random.normal(ks[7], (E, E), jnp.float32) * std, 'bk': jax.random.normal(ks[8], (E,), jnp.float32) * std, 'Wv': jax.random.normal(ks[9], (E, E), jnp.float32) * std, 'bv': jax.random.normal(ks[10], (E,), jnp.float32) * std, 'Wo': jax.random.normal(ks[11], (E, E), jnp.float32) * std, 'bo': jax.random.normal(ks[12], (E,), jnp.float32) * std}
    _L1_xattn_all = _L1_xattn_setup()
    _L1_xattn_in = {k: v for k, v in _L1_xattn_all.items() if k in ('Wq', 'bq', 'Wk', 'bk', 'Wv', 'bv', 'Wo', 'bo')}
    del _L1_xattn_all

    def _L1_ffn_setup():
        import jax, jax.numpy as jnp
        import numpy as np
        EPS = 1e-05

        def rmsnorm(x):
            return x * jax.lax.rsqrt(jnp.mean(x * x, axis=-1, keepdims=True) + EPS)

        def act_quant(x):
            scale = 127.0 / jnp.clip(jnp.max(jnp.abs(x), axis=-1, keepdims=True), 1e-05)
            q = jnp.clip(jnp.round(x * scale), -128.0, 127.0) / scale
            return x + jax.lax.stop_gradient(q - x)

        def weight_quant(w):
            scale = 1.0 / jnp.clip(jnp.mean(jnp.abs(w)), 1e-05)
            q = jnp.clip(jnp.round(w * scale), -1.0, 1.0) / scale
            return w + jax.lax.stop_gradient(q - w)

        def bitlinear(x, w, b):
            xq = act_quant(rmsnorm(x))
            wq = weight_quant(w)
            return jnp.einsum('bsd,fd->bsf', xq, wq) + b
        key = jax.random.key(seed)
        k0, k1, k2 = jax.random.split(key, 3)
        B, S, D, F = (2, 1024, 128, 512)
        x = jax.random.normal(k0, (B, S, D), dtype=jnp.float32)
        w1 = jax.random.normal(k1, (F, D), dtype=jnp.float32) * (1.0 / np.sqrt(D))
        b1 = jnp.zeros((F,), dtype=jnp.float32)
        w2 = jax.random.normal(k2, (D, F), dtype=jnp.float32) * (1.0 / np.sqrt(F))
        b2 = jnp.zeros((D,), dtype=jnp.float32)
        return {'x': x, 'w1': w1, 'b1': b1, 'w2': w2, 'b2': b2}
    _L1_ffn_all = _L1_ffn_setup()
    _L1_ffn_in = {k: v for k, v in _L1_ffn_all.items() if k in ('w1', 'b1', 'w2', 'b2')}
    del _L1_ffn_all
    return {'x': x, 'ctx_1024': ctx_1024, 'fside_SxS2_0': fside_SxS2_0, 'mask_B_ik0': mask_B_ik0, 'mask_BxS2_bk0': mask_BxS2_bk0, 'L0_attn_Wq': _L0_attn_in['Wq'], 'L0_attn_Wk': _L0_attn_in['Wk'], 'L0_attn_Wv': _L0_attn_in['Wv'], 'L0_attn_Wo': _L0_attn_in['Wo'], 'L0_attn_Wg': _L0_attn_in['Wg'], 'L0_attn_bg': _L0_attn_in['bg'], 'L0_xattn_W_q': _L0_xattn_in['W_q'], 'L0_xattn_W_k': _L0_xattn_in['W_k'], 'L0_xattn_W_v': _L0_xattn_in['W_v'], 'L0_xattn_W_o': _L0_xattn_in['W_o'], 'L0_ffn_norm_w': _L0_ffn_in['norm_w'], 'L0_ffn_router_w': _L0_ffn_in['router_w'], 'L0_ffn_w1': _L0_ffn_in['w1'], 'L0_ffn_w3': _L0_ffn_in['w3'], 'L0_ffn_w2': _L0_ffn_in['w2'], 'L1_attn_W_xproj': _L1_attn_in['W_xproj'], 'L1_attn_W_dt': _L1_attn_in['W_dt'], 'L1_attn_b_dt': _L1_attn_in['b_dt'], 'L1_attn_A_log': _L1_attn_in['A_log'], 'L1_attn_D': _L1_attn_in['D'], 'L1_xattn_Wq': _L1_xattn_in['Wq'], 'L1_xattn_bq': _L1_xattn_in['bq'], 'L1_xattn_Wk': _L1_xattn_in['Wk'], 'L1_xattn_bk': _L1_xattn_in['bk'], 'L1_xattn_Wv': _L1_xattn_in['Wv'], 'L1_xattn_bv': _L1_xattn_in['bv'], 'L1_xattn_Wo': _L1_xattn_in['Wo'], 'L1_xattn_bo': _L1_xattn_in['bo'], 'L1_ffn_w1': _L1_ffn_in['w1'], 'L1_ffn_b1': _L1_ffn_in['b1'], 'L1_ffn_w2': _L1_ffn_in['w2'], 'L1_ffn_b2': _L1_ffn_in['b2']}

def reference(x, ctx_1024, fside_SxS2_0, mask_B_ik0, mask_BxS2_bk0, L0_attn_Wq, L0_attn_Wk, L0_attn_Wv, L0_attn_Wo, L0_attn_Wg, L0_attn_bg, L0_xattn_W_q, L0_xattn_W_k, L0_xattn_W_v, L0_xattn_W_o, L0_ffn_norm_w, L0_ffn_router_w, L0_ffn_w1, L0_ffn_w3, L0_ffn_w2, L1_attn_W_xproj, L1_attn_W_dt, L1_attn_b_dt, L1_attn_A_log, L1_attn_D, L1_xattn_Wq, L1_xattn_bq, L1_xattn_Wk, L1_xattn_bk, L1_xattn_Wv, L1_xattn_bv, L1_xattn_Wo, L1_xattn_bo, L1_ffn_w1, L1_ffn_b1, L1_ffn_w2, L1_ffn_b2):
    import jax
    import jax.numpy as jnp

    def _L0_attn_ref(x, Wq, Wk, Wv, Wo, Wg, bg):
        import jax, jax.numpy as jnp
        import numpy as np
        N_HEADS = 16

        def _heads(x, h):
            B, T, D = x.shape
            return x.reshape(B, T, h, D // h).transpose(0, 2, 1, 3)

        def _reference_tuple_inner(x, Wq, Wk, Wv, Wo, Wg, bg):
            h = N_HEADS
            q = _heads(x @ Wq.T, h)
            k = _heads(x @ Wk.T, h)
            v = _heads(x @ Wv.T, h)
            g = _heads(jax.nn.sigmoid(x @ Wg.T + bg), h)
            qf = jax.nn.softplus(q) * (g + 1e-06)
            kf = jax.nn.softplus(k)
            kv = kf[..., :, None] * v[..., None, :]
            kv_cum = jnp.cumsum(kv, axis=2)
            z_cum = jnp.cumsum(kf, axis=2)
            num = jnp.einsum('bhtd,bhtde->bhte', qf, kv_cum)
            den = jnp.einsum('bhtd,bhtd->bht', qf, z_cum) + 1e-06
            out = num / den[..., None]
            B, _, T, dh = out.shape
            out = out.transpose(0, 2, 1, 3).reshape(B, T, h * dh)
            out = out @ Wo.T
            return (out, kv_cum[:, :, -1], z_cum[:, :, -1])
        return _reference_tuple_inner(x, Wq, Wk, Wv, Wo, Wg, bg)[0]

    def _L0_xattn_ref(query, key, value, valid_len, W_q, W_k, W_v, W_o):
        import jax, jax.numpy as jnp
        import numpy as np
        NEG = -1000000.0
        B, S, D = query.shape
        H = 16
        hd = D // H

        def split_heads(x, W):
            return (x @ W.T).reshape(B, S, H, hd)
        q = split_heads(query, W_q)
        k = split_heads(key, W_k)
        v = split_heads(value, W_v)
        scores = jnp.einsum('bqhd,bkhd->bhqk', q, k) / np.sqrt(hd)
        kmask = jnp.arange(S)[None, None, None, :] < valid_len[:, None, None, None]
        scores = jnp.where(kmask, scores, NEG)
        attn = jax.nn.softmax(scores, axis=-1)
        out = jnp.einsum('bhqk,bkhd->bqhd', attn, v).reshape(B, S, D)
        return out @ W_o.T

    def _L0_ffn_ref(z, norm_w, router_w, w1, w3, w2):
        import jax, jax.numpy as jnp
        import numpy as np
        EPS = 1e-09
        RMS_EPS = 1e-06
        TOP_K = 2
        LOOPS = 2

        def _rmsnorm(x, w):
            var = jnp.mean(x * x, axis=-1, keepdims=True)
            return x * jax.lax.rsqrt(var + RMS_EPS) * w

        def _swiglu(x, w1, w3, w2):
            h = jax.nn.silu(x @ w1) * (x @ w3)
            return h @ w2
        B, S, D = z.shape
        E = router_w.shape[-1]
        T = B * S
        for _ in range(LOOPS):
            z_norm = _rmsnorm(z, norm_w)
            logits = z_norm @ router_w
            scores = jax.nn.softmax(logits, axis=-1)
            topk_vals, topk_idx = jax.lax.top_k(scores, TOP_K)
            topk_vals = topk_vals / (jnp.sum(topk_vals, axis=-1, keepdims=True) + EPS)
            cw = jnp.sum(jax.nn.one_hot(topk_idx, E, dtype=z.dtype) * topk_vals[..., None], axis=-2)
            flat_z = z_norm.reshape(T, D)
            flat_cw = cw.reshape(T, E)
            mixed = jnp.zeros((T, D), dtype=z.dtype)
            for e in range(E):
                mixed = mixed + flat_cw[:, e:e + 1] * _swiglu(flat_z, w1[e], w3[e], w2[e])
            z = z + mixed.reshape(B, S, D)
        return z

    def _L1_attn_ref(x, W_xproj, W_dt, b_dt, A_log, D):
        import jax, jax.numpy as jnp
        import numpy as np
        D_INNER = 128
        STATE = 16
        DT_RANK = 64
        LOG_EPS = -7.0
        CLAMP = 20.0
        proj = x @ W_xproj
        dt_inter = proj[..., :DT_RANK]
        B_ssm = proj[..., DT_RANK:DT_RANK + STATE]
        C_ssm = proj[..., DT_RANK + STATE:]
        delta = jax.nn.softplus(dt_inter @ W_dt + b_dt)
        A = -jnp.exp(A_log)
        log_delta_A = jnp.clip(delta[..., None] * A[None, None], LOG_EPS, CLAMP)
        delta_A = jnp.exp(log_delta_A)
        delta_B_u = delta[..., None] * B_ssm[:, :, None, :] * x[..., None]
        log_dA = jnp.log(jnp.clip(delta_A, 1e-07, None))
        log_R = jnp.cumsum(log_dA, axis=1)
        R = jnp.exp(jnp.minimum(log_R, CLAMP))
        exp_neg_log_R = jnp.exp(jnp.minimum(-log_R, CLAMP))
        S = jnp.cumsum(delta_B_u * exp_neg_log_R, axis=1)
        h = R * S
        y = jnp.einsum('bln,bldn->bld', C_ssm, h) + x * D
        return y

    def _L1_xattn_ref(query, key, value, attn_mask, key_padding_mask, Wq, bq, Wk, bk, Wv, bv, Wo, bo):
        import jax, jax.numpy as jnp
        import numpy as np
        B, L, S, E, H = (4, 256, 256, 128, 16)
        DH = E // H
        SCALING = DH ** (-0.5)

        def _split_heads(x):
            b, t, _ = x.shape
            return x.reshape(b, t, H, DH).transpose(0, 2, 1, 3)
        q = (query @ Wq.T + bq) * SCALING
        k = key @ Wk.T + bk
        v = value @ Wv.T + bv
        q, k, v = (_split_heads(q), _split_heads(k), _split_heads(v))
        scores = jnp.einsum('bhld,bhsd->bhls', q, k)
        scores = scores + attn_mask[None, None, :, :]
        scores = jnp.where(key_padding_mask[:, None, None, :], -jnp.inf, scores)
        probs = jax.nn.softmax(scores.astype(jnp.float32), axis=-1).astype(scores.dtype)
        attn = jnp.einsum('bhls,bhsd->bhld', probs, v)
        attn = attn.transpose(0, 2, 1, 3).reshape(query.shape[0], query.shape[1], E)
        return attn @ Wo.T + bo

    def _L1_ffn_ref(x, w1, b1, w2, b2):
        import jax, jax.numpy as jnp
        import numpy as np
        EPS = 1e-05

        def rmsnorm(x):
            return x * jax.lax.rsqrt(jnp.mean(x * x, axis=-1, keepdims=True) + EPS)

        def act_quant(x):
            scale = 127.0 / jnp.clip(jnp.max(jnp.abs(x), axis=-1, keepdims=True), 1e-05)
            q = jnp.clip(jnp.round(x * scale), -128.0, 127.0) / scale
            return x + jax.lax.stop_gradient(q - x)

        def weight_quant(w):
            scale = 1.0 / jnp.clip(jnp.mean(jnp.abs(w)), 1e-05)
            q = jnp.clip(jnp.round(w * scale), -1.0, 1.0) / scale
            return w + jax.lax.stop_gradient(q - w)

        def bitlinear(x, w, b):
            xq = act_quant(rmsnorm(x))
            wq = weight_quant(w)
            return jnp.einsum('bsd,fd->bsf', xq, wq) + b
        h = bitlinear(x, w1, b1)
        h = jax.nn.gelu(h, approximate=False)
        return bitlinear(h, w2, b2)
    x = x + _L0_attn_ref(_layernorm(x, axis=-1), L0_attn_Wq, L0_attn_Wk, L0_attn_Wv, L0_attn_Wo, L0_attn_Wg, L0_attn_bg)
    x = x + _L0_xattn_ref(_layernorm(x, axis=-1), ctx_1024, ctx_1024, mask_B_ik0, L0_xattn_W_q, L0_xattn_W_k, L0_xattn_W_v, L0_xattn_W_o)
    x = x + _L0_ffn_ref(_layernorm(x, axis=-1), L0_ffn_norm_w, L0_ffn_router_w, L0_ffn_w1, L0_ffn_w3, L0_ffn_w2)
    x = x + _L1_attn_ref(_layernorm(x, axis=-1), L1_attn_W_xproj, L1_attn_W_dt, L1_attn_b_dt, L1_attn_A_log, L1_attn_D)
    x = x + _L1_xattn_ref(_layernorm(x, axis=-1), ctx_1024, ctx_1024, fside_SxS2_0, mask_BxS2_bk0, L1_xattn_Wq, L1_xattn_bq, L1_xattn_Wk, L1_xattn_bk, L1_xattn_Wv, L1_xattn_bv, L1_xattn_Wo, L1_xattn_bo)
    x = x + _L1_ffn_ref(_layernorm(x, axis=-1), L1_ffn_w1, L1_ffn_b1, L1_ffn_w2, L1_ffn_b2)
    return x

_drawn_inputs = setup_inputs


def setup_inputs(seed=0):
    import zlib

    import numpy as np

    out = dict(_drawn_inputs(seed))
    spreads = {'L0_ffn_norm_w': (1.0, 0.6),
     'L1_attn_D': (1.0, 0.6),
     'L1_ffn_b1': (0.0, 0.8),
     'L1_ffn_b2': (0.0, 0.8)}
    factors = {'fside_SxS2_0': 8.0,
     'L0_attn_Wq': 8.0,
     'L0_attn_Wk': 8.0,
     'L0_attn_Wv': 7.114,
     'L0_attn_Wo': 7.275,
     'L0_attn_Wg': 8.0,
     'L0_attn_bg': 8.0,
     'L0_ffn_router_w': 8.0,
     'L0_ffn_w1': 8.0,
     'L0_ffn_w3': 8.0,
     'L0_ffn_w2': 8.0,
     'L1_attn_W_xproj': 7.631,
     'L1_attn_W_dt': 8.0,
     'L1_attn_b_dt': 26.903,
     'L1_attn_A_log': 8.0,
     'L1_xattn_Wq': 8.0,
     'L1_xattn_bq': 48.048,
     'L1_xattn_Wk': 8.0,
     'L1_xattn_bk': 64.0,
     'L1_xattn_Wv': 6.693,
     'L1_xattn_bv': 29.466,
     'L1_xattn_Wo': 6.739,
     'L1_xattn_bo': 55.693}
    for name, (base, spread) in spreads.items():
        noise = np.random.default_rng([zlib.crc32(name.encode()), seed]).standard_normal(out[name].shape)
        drawn = base * np.exp(spread * noise) if base else spread * noise
        out[name] = jnp.asarray(drawn.astype(out[name].dtype))
    for name, factor in factors.items():
        out[name] = (out[name] * factor).astype(out[name].dtype)
    return out
```

```python
from contextlib import ExitStack

import concourse.bass as bass
from concourse import mybir

F32 = mybir.dt.float32
BF16 = mybir.dt.bfloat16
I32 = mybir.dt.int32
U8 = mybir.dt.uint8
ALU = mybir.AluOpType
ACT = mybir.ActivationFunctionType
AX = mybir.AxisListType.X

P = 128
B, S, D = 4, 256, 128
T = B * S
NT = T // P
QT = S // P
H = 16
DH = D // H
HG = 4
NG = H // HG
NE, FE = 8, 256
NS = 16
DTR = 64
FF = 512
HALF = 512
PAIRS = H // 2
UNITS = B * PAIRS
ROUND = 12582912.0
CLAMP_EXP = 485165195.40979
NEG_X0 = 1.0e6
NEG_X1 = 1.0e30
MAX_ROW = 96
NEG_ROW = 72


def build(nc, inp, out, last_stage=6):
    ctx = ExitStack()
    with ctx:
        def sb(name, shape, dt=F32):
            return ctx.enter_context(nc.sbuf_tensor(name, shape, dt))

        signals = {}

        def sig(name):
            if name not in signals:
                signals[name] = ctx.enter_context(nc.semaphore(name))
            return signals[name]

        PS = ctx.enter_context(nc.psum_tensor("PS", [P, 8, HALF], F32))

        X = sb("X", [P, NT, D])
        XN = sb("XN", [P, NT, D])
        XNT = sb("XNT", [P, T])
        QS = sb("QS", [P, H, T], BF16)
        KSA = sb("KSA", [P, H, T], BF16)
        KX = sb("KX", [P, H, T], BF16)
        VA = sb("VA", [P, NT, H, 32])
        VX = sb("VX", [P, NT, H, 32])
        SCR = sb("SCR", [P, 4, T])
        OT = sb("OT", [P, NG, T])
        E = sb("E", [P, 3, 2, HALF])
        wself = sb("wself", [P, 4, D])
        wox = sb("wox", [P, 3, NG, D])
        wx = sb("wx", [P, 2, 3, D])
        ident = sb("ident", [P, P])
        identb = sb("identb", [P, P], BF16)
        causal = sb("causal", [P, P])
        spread = sb("spread", [P, P])
        onesf = sb("onesf", [P, P])
        den_eps = sb("den_eps", [P, 1])
        bg = sb("bg", [P, 2])
        bqk = sb("bqk", [P, 3])
        brow = sb("brow", [1, 2, D])
        st = sb("st", [P, NT, 6])
        mv = sb("mv", [P, NT, 2])
        ve = sb("ve", [P, NT])
        lnv = sb("lnv", [P, NT])
        rs = sb("rs", [P, NT])
        rt = sb("rt", [P, NT])
        rstd = sb("rstd", [P, NT])
        lens = sb("lens", [P, B], I32)
        lensf = sb("lensf", [P, B])
        mx = sb("mx", [P, 2, QT, H])
        mxr = sb("mxr", [32, 2, P])
        mxp = sb("mxp", [32, B, 3, P], BF16)

        QP = E[:, 0:2].rearrange("p a b c -> p (a b c)").bitcast(BF16)[:, 0:3 * T].rearrange("p (a t) -> p a t", a=3)
        EF = E[:, :, :, :].rearrange("p a b c -> p (a b c)").bitcast(BF16)
        KP = EF[:, 3 * T:6 * T].rearrange("p (a t) -> p a t", a=3)
        OTf = OT[:, :, :].rearrange("p g t -> p (g t)")
        KXP = OTf[:, 0:3 * T // 2].bitcast(BF16).rearrange("p (a t) -> p a t", a=3)
        KX32 = OTf[:, 3 * T // 2:5 * T // 2]
        KXR = OTf[:, 5 * T // 2:7 * T // 2]
        iota = OTf[:, 7 * T // 2:7 * T // 2 + S].bitcast(I32)
        iotaf = OTf[:, 7 * T // 2 + S:4 * T]
        VMASK = SCR[:, 2, :]
        CT = SCR[:, 3, :]
        KSf = KSA[:, :, :].rearrange("p h t -> p (h t)").bitcast(F32)
        W1 = KSf[:, 0:2048].rearrange("p (e f) -> p e f", e=NE)
        W3 = KSf[:, 2048:4096].rearrange("p (e f) -> p e f", e=NE)
        W2 = KSf[:, 4096:6144].rearrange("p (e c d) -> p e c d", e=NE, c=2)
        FPART = KSf[:, 6144:7680].bitcast(BF16).rearrange("p (w c n) -> p w c n", w=4, c=3)
        VAf = VA[:, :, :, :].rearrange("p a b c -> p (a b c)")
        XN1 = XN[:, :, :].rearrange("p j d -> p (j d)")
        E6 = E[:, :, :, :].rearrange("p a b c -> p (a b) c")
        PAD = SCR[:, 0, 0:T // 4].bitcast(U8)
        FRAW = SCR[:, 1, :].rearrange("p (w n) -> p w n", w=4)
        RDEN = SCR[:, 1, 0:HALF]

        router = sb("router", [P, NE])
        normw = sb("normw", [P, 1])
        tri = sb("tri", [P, NE, NE])
        logits = sb("logits", [P, NT, NE])
        gates = sb("gates", [P, NT, NE])
        chosen = sb("chosen", [P, NT, NE])
        tok1 = sb("tok1", [P, NT])
        tok2 = sb("tok2", [P, NT])
        wssm = sb("wssm", [P, DTR + 2 * NS])
        wdt = sb("wdt", [DTR, P])
        ssmc = sb("ssmc", [P, 2])
        amat = sb("amat", [P, NS])
        wraw = KSf[:, 6144:6144 + 2 * FF].rearrange("p (w f) -> p w f", w=2)
        wq1 = sb("wq1", [P, FF], BF16)
        wq2 = sb("wq2", [P, FF // P, D], BF16)
        b1bc = KSf[:, 0:FF]
        b2bc = KSf[:, FF:FF + D]
        wsum = sb("wsum", [P, 2])
        wmean = sb("wmean", [P, 2])
        wscale = sb("wscale", [P, 2])
        peak = sb("peak", [P, NT])
        fac = sb("fac", [P, NT])
        deq = sb("deq", [P, NT])
        sumsq = sb("sumsq", [P, NT])

        block = ctx.enter_context(nc.Block())

        def bank(i):
            return PS[:, i, :]

        class Chain:
            def __init__(self, eng, name):
                self.eng, self.sem, self.n = eng, sig(name), 0

            def link(self, ins):
                ins.then_inc(self.sem, 1)
                self.n += 1
                self.eng.wait_ge(self.sem, self.n)

            def mark(self, ins):
                ins.then_inc(self.sem, 1)
                self.n += 1

            def wait(self):
                self.eng.wait_ge(self.sem, self.n)

        def norm_stats(dve, ch, src, k, eps, mean_square=False):
            for j in range(NT):
                ins = dve.bn_stats(st[:, j, :], src[:, j, :])
            ch.link(ins)
            for j in range(NT):
                ins = dve.bn_aggr(mv[:, j, :], st[:, j, :])
            ch.link(ins)
            if mean_square:
                ch.link(dve.tensor_tensor(rt[:, :], mv[:, :, 0], mv[:, :, 0], ALU.mult))
                ch.link(dve.tensor_tensor(ve[:, :], rt[:, :], mv[:, :, 1], ALU.add))
                dve.tensor_scalar(ve[:, :], ve[:, :], eps, None, ALU.add).then_inc(sig("ve"), 1)
            else:
                dve.tensor_scalar(ve[:, :], mv[:, :, 1], eps, None, ALU.add).then_inc(sig("ve"), 1)

        def norm_root(act, ch, k):
            act.wait_ge(sig("ve"), k + 1)
            ch.link(act.activation(lnv[:, :], ve[:, :], ACT.Ln))
            act.activation(rs[:, :], lnv[:, :], ACT.Exp, scale=-0.5).then_inc(sig("root"), 1)

        def norm_refine(dve, ch, k):
            dve.wait_ge(sig("root"), k + 1)
            ch.link(dve.tensor_tensor(rt[:, :], rs[:, :], rs[:, :], ALU.mult))
            ch.link(dve.tensor_tensor(rt[:, :], rt[:, :], ve[:, :], ALU.mult))
            ch.link(dve.tensor_scalar(rt[:, :], rt[:, :], -0.5, 1.5, ALU.mult, ALU.add))
            ch.link(dve.tensor_tensor(rstd[:, :], rt[:, :], rs[:, :], ALU.mult))

        def norm_apply(dve, dst, src):
            for j in range(NT):
                ins = dve.tensor_scalar(dst[:, j, :], src[:, j, :], mv[:, j, 0:1], rstd[:, j:j + 1],
                                        ALU.subtract, ALU.mult)
                if j % 4 == 3:
                    ins.then_inc(sig("xn"), 1)

        def norm_turn(pe, src, o):
            for half in range(2):
                pe.wait_ge(sig("xn"), 2 * o + half + 1)
                for j in range(4):
                    ins = pe.transpose(bank(4 + half)[:, j * P:(j + 1) * P], src[:, 4 * half + j, :], ident[:, :])
                ins.then_inc(sig("turned"), 1)

        def norm_take(act, o, scale=None):
            for half in range(2):
                act.wait_ge(sig("turned"), 2 * o + half + 1)
                if scale is None:
                    ins = act.activation(XNT[:, half * HALF:(half + 1) * HALF], bank(4 + half), ACT.Copy)
                else:
                    ins = act.activation(XNT[:, half * HALF:(half + 1) * HALF], bank(4 + half), ACT.Copy, scale=scale)
                ins.then_inc(sig("xnt"), 1)

        def project(pe, first_bank, lhsT, rhs, signal):
            for half in range(2):
                ins = pe.matmul(bank(first_bank + half)[0:lhsT.shape[1], :], lhsT,
                                rhs[:, half * HALF:(half + 1) * HALF], start=True, stop=True)
            ins.then_inc(sig(signal), 1)

        def two(b):
            return PS[:, b:b + 2, :].rearrange("p a n -> p (a n)")

        def split(dve, ch, dst, src, tmp, signal):
            ch.link(dve.tensor_copy(dst[:, 0, :], src))
            ch.link(dve.tensor_tensor(tmp, src, dst[:, 0, :], ALU.subtract))
            ch.link(dve.tensor_copy(dst[:, 1, :], tmp))
            dve.tensor_tensor(dst[:, 2, :], tmp, dst[:, 1, :], ALU.subtract).then_inc(sig(signal), 1)

        def o_region(u):
            g = (u % PAIRS) // 2
            return bank(6)[:, (g % 2) * S:(g % 2) * S + S]

        def o_rows(u, i):
            r = 32 * ((2 * u + i) % HG)
            return slice(r, r + 32)

        NZ = UNITS // 4

        def out_evac(act, A, z, bias):
            act.wait_ge(sig("o_full"), A * NZ + z + 1)
            if A == 0 and z == 0:
                act.wait_ge(sig("stack_k"), 16 * 12)
            b, x = z // 2, z % 2
            dst = OT[:, 2 * x:2 * x + 2, b * S:(b + 1) * S]
            src = bank(6).rearrange("p (g t) -> p g t", g=2)
            if bias:
                ins = act.activation(dst, src, ACT.Identity, bias=den_eps[:, 0:1])
            else:
                ins = act.activation(dst, src, ACT.Copy)
            ins.then_inc(sig("o_taken"), 1)

        def den_spread(pe, A, z):
            pe.wait_ge(sig("o_taken"), A * NZ + z + 1)
            if z or A:
                pe.wait_ge(sig("o_normed"), A * NZ + z)
            b, x = z // 2, z % 2
            pe.matmul(bank(7).rearrange("p (g t) -> p g t", g=2), spread[:, :],
                      OT[:, 2 * x:2 * x + 2, b * S:(b + 1) * S], start=True, stop=True).then_inc(sig("den"), 1)

        def out_norm(dve, ch, A, z):
            b, x = z // 2, z % 2
            dve.wait_ge(sig("den"), A * NZ + z + 1)
            ch.link(dve.reciprocal(RDEN, bank(7)))
            o = OT[:, 2 * x:2 * x + 2, b * S:(b + 1) * S]
            dve.tensor_tensor(o, o, RDEN.rearrange("p (g t) -> p g t", g=2), ALU.mult).then_inc(sig("o_normed"), 1)

        def out_project(pe, A):
            pe.wait_ge(sig("o_normed"), (A + 1) * NZ)
            pe.wait_ge(sig("wox_in"), 16)
            for j in range(NT):
                o = bank(j // 4)[:, (j % 4) * P:(j % 4 + 1) * P]
                for g in range(NG):
                    ins = pe.matmul(o, OT[:, g, j * P:(j + 1) * P], wox[:, A, g, :],
                                    start=(g == 0), stop=(g == NG - 1 and A < 2))
                if A == 2:
                    ins = pe.matmul(o, onesf[0:1, :], brow[0:1, 1, :], start=False, stop=True)
                if j % 4 == 3:
                    ins.then_inc(sig("proj_out"), 1)

        def residual(dve, ch, A):
            for half in range(2):
                dve.wait_ge(sig("proj_out"), 2 * A + half + 1)
                x = X[:, 4 * half:4 * half + 4, :].rearrange("p j d -> p (j d)")
                ins = dve.tensor_tensor(x, x, bank(half), ALU.add)
            ins.then_inc(sig("x_res"), 1)


        def x_ready(eng, stage):
            eng.wait_ge(sig("x_res"), stage)

        def context_tensor(pe, L):
            if L == 0:
                pe.wait_ge(sig("ctx_in"), 16)
                pe.wait_ge(sig("wx_in"), 16)
            else:
                pe.wait_ge(sig("ctx_in"), 32)
                pe.wait_ge(sig("brow_in"), 16)
            project(pe, 0, wx[:, L, 1, :], CT, "kx_psum")
            for j in range(NT):
                o = bank(2 + j // 4)[:, (j % 4) * P:(j % 4 + 1) * P]
                ins = pe.matmul(o, CT[:, j * P:(j + 1) * P], wx[:, L, 2, :], start=True, stop=(L == 0))
                if L == 1:
                    ins = pe.matmul(o, onesf[0:1, :], brow[0:1, 0, :], start=False, stop=True)
            ins.then_inc(sig("vx_psum"), 1)

        def take_values(act, dst):
            for half in range(2):
                ins = act.activation(dst[:, 4 * half:4 * half + 4, :, 0:DH].rearrange("p j h e -> p (j h) e"),
                                     bank(2 + half).rearrange("p (a e) -> p a e", e=DH), ACT.Copy)
            return ins

        def context_scalar(act, L):
            act.wait_ge(sig("kx_psum"), L + 1)
            if L == 0:
                act.activation(KX32, two(0), ACT.Copy).then_inc(sig("kx_raw"), 1)
            else:
                act.wait_ge(sig("bqk_in"), 16)
                act.activation(KX32, two(0), ACT.Identity, bias=bqk[:, 1:2]).then_inc(sig("kx_raw"), 1)
            act.wait_ge(sig("vx_psum"), L + 1)
            act.wait_ge(sig("const"), 1)
            take_values(act, VX).then_inc(sig("vx_ready"), 1)

        def context_keys_pool(pool, ch, L, neg):
            if L == 0:
                for b in range(B):
                    ins = pool.tensor_scalar(VMASK[:, b * S:(b + 1) * S], iotaf, lensf[:, b:b + 1], None,
                                             ALU.is_lt)
                ch.link(ins)
            else:
                pool.wait_ge(sig("pad_in"), 16)
                ch.link(pool.tensor_scalar(VMASK, PAD, -1.0, 1.0, ALU.mult, ALU.add))
            pool.wait_ge(sig("kx_raw"), L + 1)
            ch.link(pool.tensor_tensor(KX32, KX32, VMASK, ALU.mult))

            def parts():
                ch.link(pool.tensor_scalar(KXP[:, 0, :], KX32, 1.0, 0.0, ALU.mult, ALU.add))
                ch.link(pool.tensor_tensor(KXR, KX32, KXP[:, 0, :], ALU.subtract))
                ch.link(pool.tensor_scalar(KXP[:, 1, :], KXR, 1.0, 0.0, ALU.mult, ALU.add))
                ch.link(pool.tensor_tensor(KXP[:, 2, :], KXR, KXP[:, 1, :], ALU.subtract))

            parts()
            for a in range(3):
                for b in range(3):
                    r = 24 * a + 8 * b
                    pool.dma_start(KX[r:r + 8, :, :], KXP[:, b, :]).then_inc(sig("stack_k"), 16)
            pool.wait_ge(sig("stack_k"), 16 * (12 * L + 9))
            ch.link(pool.tensor_scalar(KX32, VMASK, -1.0, neg, ALU.add, ALU.mult))
            parts()
            for c in range(3):
                pool.dma_start(KX[NEG_ROW + c:NEG_ROW + c + 1, :, :], KXP[0:H, c, :]).then_inc(sig("stack_k"), 16)

        def weighed(eng, A, v):
            if v % 4 == 3:
                eng.wait_ge(sig("o_full"), A * NZ + v // 4 + 1)
            else:
                eng.wait_ge(sig("weighed"), A * (UNITS - NZ) + v + 1 - (v + 1) // 4)

        def o_free(pe, A, u):
            if u % 4 == 0 and (A or u):
                pe.wait_ge(sig("o_taken"), A * NZ + u // 4)

        def self_tensor(pe):
            pe.wait_ge(sig("wself_in"), 16)
            pe.wait_ge(sig("xnt"), 2)
            pe.wait_ge(sig("kx_raw"), 1)
            project(pe, 0, wself[:, 0, :], XNT, "self_proj")
            pe.wait_ge(sig("vx_ready"), 1)
            project(pe, 2, wself[:, 1, :], XNT, "self_proj")
            project(pe, 6, wself[:, 2, :], XNT, "self_proj")
            pe.wait_ge(sig("ka32"), 1)
            for j in range(NT):
                ins = pe.matmul(bank(2 + j // 4)[:, (j % 4) * P:(j % 4 + 1) * P], XNT[:, j * P:(j + 1) * P],
                                wself[:, 3, :], start=True, stop=True)
            ins.then_inc(sig("self_proj"), 1)
            pe.wait_ge(sig("stack_a"), 16 * 18)
            pe.wait_ge(sig("stack_clear"), 1)
            pe.wait_ge(sig("va_ready"), 1)

            def scores(u):
                if u >= 2:
                    pe.wait_ge(sig("a_masked"), u - 1)
                    pe.wait_ge(sig("a_off"), u - 1)
                b, hp = divmod(u, PAIRS)
                diagonal, off = bank(2 * (u % 2)), bank(2 * (u % 2) + 1)
                for i in range(2):
                    h = 2 * hp + i
                    for o, kt, qt in ((diagonal[:, 2 * i * P:], 0, 0), (diagonal[:, (2 * i + 1) * P:], 1, 1),
                                      (off[:, i * P:], 0, 1)):
                        ins = pe.matmul(o[:, 0:P], KSA[:, h, b * S + kt * P:b * S + (kt + 1) * P],
                                        QS[:, h, b * S + qt * P:b * S + (qt + 1) * P], start=True, stop=True)
                ins.then_inc(sig("a_scores"), 1)

            def weigh(u):
                b, hp = divmod(u, PAIRS)
                pe.wait_ge(sig("a_masked"), u + 1)
                pe.wait_ge(sig("a_off"), u + 1)
                o_free(pe, 0, u)
                for tile, cols, kind, step, off, start, stop in (
                        (0, slice(0, P), 0, 2, 0, True, True),
                        (0, slice(P, S), 1, 1, 0, True, False),
                        (1, slice(P, S), 0, 2, 1, False, True)):
                    for i in range(2):
                        h = 2 * hp + i
                        c = (step * i + off) * P
                        ins = pe.matmul(o_region(u)[o_rows(u, i), cols], VA[:, 2 * b + tile, h, :],
                                        E[:, u % 3, kind, c:c + P], start=start, stop=stop, skip_group_check=True)
                ins.then_inc(sig("o_full" if u % 4 == 3 else "weighed"), 1)

            scores(0)
            for u in range(UNITS):
                if u + 1 < UNITS:
                    scores(u + 1)
                weigh(u)
                if u % 4 == 1 and u > 4:
                    den_spread(pe, 0, u // 4 - 1)
            den_spread(pe, 0, NZ - 1)
            out_project(pe, 0)

        EG = SCR[:, 0, :]
        SPQ = SCR[:, 3, :]

        def self_scalar(act, ch):
            act.wait_ge(sig("self_proj"), 1)
            for n, dst in enumerate((SPQ, XN1)):
                act.wait_ge(sig("self_proj"), n + 1)
                ch.link(act.activation(dst, two(2 * n), ACT.Abs))
                ch.link(act.activation(dst, dst, ACT.Exp, scale=-1.0))
                act.activation(dst, dst, ACT.Ln, bias=1.0).then_inc(sig("self_sp"), 1)
            act.wait_ge(sig("self_proj"), 3)
            act.wait_ge(sig("bg_neg"), 1)
            act.activation(EG, two(6), ACT.Exp, bias=bg[:, 1:2], scale=-1.0).then_inc(sig("self_gate"), 1)
            act.wait_ge(sig("self_proj"), 4)
            take_values(act, VA).then_inc(sig("va_ready"), 1)
            act.wait_ge(sig("den_eps"), 1)
            act.wait_ge(sig("stack_a"), 16 * 18)
            for u in range(UNITS):
                act.wait_ge(sig("a_scores"), u + 1)
                if u >= 3:
                    weighed(act, 0, u - 3)
                act.activation(E[:, u % 3, 1, 0:S], bank(2 * (u % 2) + 1)[:, 0:S], ACT.Copy).then_inc(sig("a_off"), 1)
                if u % 4 == 0 and u:
                    out_evac(act, 0, u // 4 - 1, True)
            out_evac(act, 0, NZ - 1, True)

        def self_vector(dve, ch):
            R = SCR[:, 1, :]
            dve.wait_ge(sig("bg_in"), 16)
            dve.tensor_scalar(bg[:, 1:2], bg[:, 0:1], -1.0, None, ALU.mult).then_inc(sig("bg_neg"), 1)
            dve.wait_ge(sig("const"), 1)
            ch.link(dve.tensor_reduce(den_eps[:, :], spread[:, :], AX, ALU.max))
            dve.tensor_scalar(den_eps[:, :], den_eps[:, :], 1e-6, None, ALU.mult).then_inc(sig("den_eps"), 1)
            dve.wait_ge(sig("self_sp"), 2)
            dve.scalar_tensor_tensor(XN1, two(2), 0.0, XN1, ALU.max, ALU.add).then_inc(sig("ka32"), 1)
            dve.wait_ge(sig("ka32"), 1)
            split(dve, ch, KP, XN1, R, "ka_parts")
            dve.wait_ge(sig("ka_parts"), 1)
            ch.link(dve.scalar_tensor_tensor(SPQ, two(0), 0.0, SPQ, ALU.max, ALU.add))
            dve.wait_ge(sig("self_gate"), 1)
            ch.link(dve.tensor_scalar(EG, EG, 1.0, None, ALU.add))
            ch.link(dve.reciprocal(EG, EG))
            ch.link(dve.scalar_tensor_tensor(SPQ, EG, 1e-6, SPQ, ALU.add, ALU.mult))
            split(dve, ch, QP, SPQ, R, "qa_parts")
            mask = causal[:, :].unsqueeze(1).to_broadcast([P, 4, P])
            dve.wait_ge(sig("stack_a"), 16 * 18)
            for u in range(UNITS):
                dve.wait_ge(sig("a_scores"), u + 1)
                if u >= 3:
                    weighed(dve, 0, u - 3)
                dve.tensor_tensor(E[:, u % 3, 0, :].rearrange("p (a n) -> p a n", a=4),
                                  bank(2 * (u % 2)).rearrange("p (a n) -> p a n", a=4), mask, ALU.mult)\
                    .then_inc(sig("a_masked"), 1)
                if u % 4 == 2 and u > 4:
                    out_norm(dve, ch, 0, u // 4 - 1)
            out_norm(dve, ch, 0, NZ - 1)
            residual(dve, ch, 0)

        STEPS = QT * PAIRS + 1
        CHUNKS = (3, 3, 3, 3, 3, 2, 0, 0)

        def steps_before(u):
            b, hp = divmod(u, PAIRS)
            if b + 1 < B:
                k0 = sum(CHUNKS[:hp])
                for k in range(k0, k0 + CHUNKS[hp]):
                    yield b + 1, k

        def cross_tensor(pe, L):
            A = L + 1
            pe.wait_ge(sig("xnt"), 2 * ((1, 5)[L] + 1))
            project(pe, 0, wx[:, L, 0, :], XNT, "qx_psum")
            pe.wait_ge(sig("qx_raw"), L + 1)
            pe.wait_ge(sig("stack_q"), 16 * 9 * (L + 1))
            pe.wait_ge(sig("stack_k"), 16 * 12 * (L + 1))
            pe.wait_ge(sig("stack_clear"), 2 + L)
            pe.wait_ge(sig("vx_ready"), L + 1)
            if L == 1:
                pe.wait_ge(sig("bias_parts"), 1)

            def max_step(b, k):
                n = b * STEPS + k
                if n >= 2 or L:
                    pe.wait_ge(sig("maxed"), L * B * STEPS + max(n - 1, 0))
                o = bank(4 + n % 2)
                if k == STEPS - 1:
                    pe.wait_ge(sig("maxed"), L * B * STEPS + n)
                    ins = pe.transpose(o[0:32, 0:P], mx[:, b % 2, :, :].rearrange("p q h -> p (q h)"), ident[:, :])
                else:
                    q, hp = divmod(k, PAIRS)
                    if L == 1:
                        for c in range(2):
                            pe.matmul(o.rearrange("p (i n) -> p i n", i=2), identb[:, :],
                                      FPART[:, q, c, :].unsqueeze(1).to_broadcast([P, 2, S]),
                                      start=(c == 0), stop=False, skip_group_check=True)
                    for i in range(2):
                        h = 2 * hp + i
                        ins = pe.matmul(o[:, i * S:(i + 1) * S], QS[:, h, b * S + q * P:b * S + (q + 1) * P],
                                        KX[:, h, b * S:(b + 1) * S], start=(L == 0), stop=True, skip_group_check=True)
                ins.then_inc(sig("max_scores"), 1)

            def scores(u):
                b, hp = divmod(u, PAIRS)
                if hp == 0:
                    pe.wait_ge(sig("max_in%d" % b), 16 * 3 * QT * (L + 1))
                if u >= 2 or L:
                    pe.wait_ge(sig("x_exp"), L * UNITS + max(u - 1, 0))
                for i in range(2):
                    h = 2 * hp + i
                    for kt in range(QT):
                        o = bank(2 * (u % 2) + i)[:, kt * S:(kt + 1) * S]
                        if L == 1:
                            for c in range(3):
                                pe.matmul(o, identb[:, :], FPART[:, 2 + kt, c, :], start=(c == 0), stop=False,
                                          skip_group_check=True)
                        ins = pe.matmul(o, KX[:, h, b * S + kt * P:b * S + (kt + 1) * P],
                                        QS[:, h, b * S:(b + 1) * S], start=(L == 0), stop=True, skip_group_check=True)
                ins.then_inc(sig("x_scores"), 1)

            def weigh(u):
                b, hp = divmod(u, PAIRS)
                pe.wait_ge(sig("x_exp"), L * UNITS + u + 1)
                o_free(pe, A, u)
                for kt in range(QT):
                    for i in range(2):
                        ins = pe.matmul(o_region(u)[o_rows(u, i), :], VX[:, 2 * b + kt, 2 * hp + i, :],
                                        E[:, u % 3, i, kt * S:(kt + 1) * S], start=(kt == 0), stop=(kt == QT - 1),
                                        skip_group_check=True)
                ins.then_inc(sig("o_full" if u % 4 == 3 else "weighed"), 1)

            for k in range(STEPS):
                max_step(0, k)
            for u in range(UNITS):
                for b, k in steps_before(u):
                    max_step(b, k)
                scores(u)
                if u:
                    weigh(u - 1)
                if u % 4 == 2 and u > 4:
                    den_spread(pe, A, u // 4 - 1)
            weigh(UNITS - 1)
            den_spread(pe, A, NZ - 1)
            out_project(pe, A)

        def cross_scalar(act, ch, L):
            A = L + 1
            act.wait_ge(sig("qx_psum"), L + 1)
            if L == 0:
                ins = act.activation(EG, two(0), ACT.Copy, scale=DH ** -0.5)
            else:
                act.wait_ge(sig("bq_scaled"), 1)
                ins = act.activation(EG, two(0), ACT.Identity, bias=bqk[:, 2:3], scale=DH ** -0.5)
            ins.then_inc(sig("qx_raw"), 1)
            act.wait_ge(sig("stack_q"), 16 * 9 * (L + 1))
            act.wait_ge(sig("stack_k"), 16 * 12 * (L + 1))
            for u in range(UNITS):
                act.wait_ge(sig("x_scores"), L * UNITS + u + 1)
                if u >= 3:
                    weighed(act, A, u - 3)
                bk = 2 * (u % 2)
                act.activation(E[:, u % 3, :, :], PS[:, bk:bk + 2, :], ACT.Exp).then_inc(sig("x_exp"), 1)
                if u % 4 == 0 and u:
                    out_evac(act, A, u // 4 - 1, False)
            out_evac(act, A, NZ - 1, False)

        def cross_vector(dve, ch, L):
            A = L + 1
            if L == 1:
                dve.wait_ge(sig("bqk_in"), 16)
                dve.tensor_scalar(bqk[:, 2:3], bqk[:, 0:1], DH ** -0.5, None, ALU.mult).then_inc(sig("bq_scaled"), 1)
            dve.wait_ge(sig("qx_raw"), L + 1)
            split(dve, ch, QP, EG, SCR[:, 1, :], "qx_parts")

            def max_step(b, k):
                n = b * STEPS + k
                dve.wait_ge(sig("max_scores"), L * B * STEPS + n + 1)
                o = bank(4 + n % 2)
                if k < STEPS - 1:
                    q, hp = divmod(k, PAIRS)
                    dve.tensor_reduce(mx[:, b % 2, q, 2 * hp:2 * hp + 2], o.rearrange("p (i n) -> p i n", i=2),
                                      AX, ALU.max, negate=True).then_inc(sig("maxed"), 1)
                else:
                    o = o[0:32, 0:P]
                    ch.link(dve.tensor_copy(mxp[:, b, 0, :], o))
                    dve.tensor_tensor(mxr[:, 0, :], o, mxp[:, b, 0, :], ALU.subtract).then_inc(sig("maxed"), 1)
                    dve.wait_ge(sig("maxed"), L * B * STEPS + n + 1)
                    ch.link(dve.tensor_copy(mxp[:, b, 1, :], mxr[:, 0, :]))
                    dve.tensor_tensor(mxp[:, b, 2, :], mxr[:, 0, :], mxp[:, b, 1, :], ALU.subtract)\
                        .then_inc(sig("max_parts"), 1)

            for k in range(STEPS):
                max_step(0, k)
            for u in range(UNITS):
                for b, k in steps_before(u):
                    max_step(b, k)
                if u % 4 == 3 and u > 4:
                    out_norm(dve, ch, A, u // 4 - 1)
            out_norm(dve, ch, A, NZ - 1)
            residual(dve, ch, A)

        ZN = VAf[:, 0:T].rearrange("p (j d) -> p j d", j=NT)
        RANK = VAf[:, T:T + NT * NE * NE].rearrange("p (j a b) -> p j a b", j=NT, a=NE)
        SAME = VAf[:, T + 512:T + 1024].rearrange("p (j a b) -> p j a b", j=NT, a=NE)
        LOOPS = 2
        UPS = NE * 4

        def experts_tensor(pe, r):
            pe.wait_ge(sig("xnt"), 2 * (2 + r + 1))
            if r == 0:
                pe.wait_ge(sig("experts_in"), 16 * 3)
            for j in range(NT):
                ins = pe.matmul(bank(7)[:, j * NE:(j + 1) * NE], XNT[:, j * P:(j + 1) * P], router[:, :],
                                start=True, stop=True)
            ins.then_inc(sig("logits"), 1)

            def up(n):
                g = r * UPS + n
                e, half, c = n // 4, n // 2 % 2, n % 2
                if g >= 3:
                    pe.wait_ge(sig("gated"), g - 2)
                for w, o in ((W1, 0), (W3, 1)):
                    ins = pe.matmul(bank(2 * (g % 3) + o), w[:, e, c * P:(c + 1) * P],
                                    XNT[:, half * HALF:(half + 1) * HALF], start=True, stop=True)
                ins.then_inc(sig("up"), 1)

            def down(m):
                g = r * UPS // 2 + m
                pe.wait_ge(sig("gated"), 2 * g + 2)
                if g >= 2:
                    pe.wait_ge(sig("mixed"), g - 1)
                if m == 1:
                    pe.wait_ge(sig("logits_read"), r + 1)
                for j in range(4):
                    for c in range(2):
                        ins = pe.matmul(bank(6 + g % 2)[:, j * P:(j + 1) * P],
                                        E6[:, (2 * g + c) % 4, j * P:(j + 1) * P], W2[:, m // 2, c, :],
                                        start=(c == 0), stop=(c == 1))
                ins.then_inc(sig("down"), 1)

            for n in range(UPS):
                up(n)
                if n >= 2 and n % 2 == 0:
                    down(n // 2 - 1)
            down(UPS // 2 - 1)

        def experts_scalar(act, r):
            act.wait_ge(sig("logits_shifted"), r + 1)
            act.activation(gates[:, :, :], gates[:, :, :], ACT.Exp).then_inc(sig("gate_exp"), 1)
            for n in range(UPS):
                g = r * UPS + n
                act.wait_ge(sig("up"), g + 1)
                if g >= 2:
                    act.wait_ge(sig("gated"), g - 1)
                act.activation(E6[:, 4 + g % 2, :], bank(2 * (g % 3)), ACT.Silu).then_inc(sig("silu"), 1)

        def experts_vector(dve, ch, r):
            dve.wait_ge(sig("logits"), r + 1)
            dve.tensor_copy(logits[:, :, :], bank(7)[:, 0:NT * NE].rearrange("p (j e) -> p j e", j=NT))\
                .then_inc(sig("logits_read"), 1)
            dve.wait_ge(sig("logits_read"), r + 1)
            ch.link(dve.tensor_reduce(tok1[:, :], logits[:, :, :], AX, ALU.max))
            dve.tensor_tensor(gates[:, :, :], logits[:, :, :], tok1[:, :].unsqueeze(2).to_broadcast([P, NT, NE]),
                              ALU.subtract).then_inc(sig("logits_shifted"), 1)
            other = logits[:, :, :].unsqueeze(2).to_broadcast([P, NT, NE, NE])
            own = logits[:, :, :].unsqueeze(3).to_broadcast([P, NT, NE, NE])
            dve.tensor_tensor(RANK, other, own, ALU.is_gt)
            ch.link(dve.tensor_tensor(SAME, other, own, ALU.is_equal))
            ch.link(dve.tensor_tensor(SAME, SAME, tri[:, :, :].unsqueeze(1).to_broadcast([P, NT, NE, NE]), ALU.mult))
            ch.link(dve.tensor_tensor(RANK, RANK, SAME, ALU.add))
            ch.link(dve.tensor_reduce(chosen[:, :, :], RANK, AX, ALU.add))
            ch.link(dve.tensor_scalar(chosen[:, :, :], chosen[:, :, :], 1.5, None, ALU.is_lt))
            dve.wait_ge(sig("gate_exp"), r + 1)
            ch.link(dve.tensor_reduce(tok1[:, :], gates[:, :, :], AX, ALU.add))
            ch.link(dve.reciprocal(tok1[:, :], tok1[:, :]))
            ch.link(dve.tensor_tensor(gates[:, :, :], gates[:, :, :], chosen[:, :, :], ALU.mult))
            ch.link(dve.tensor_tensor(gates[:, :, :], gates[:, :, :],
                                      tok1[:, :].unsqueeze(2).to_broadcast([P, NT, NE]), ALU.mult))
            ch.link(dve.tensor_reduce(tok2[:, :], gates[:, :, :], AX, ALU.add))
            ch.link(dve.tensor_scalar(tok2[:, :], tok2[:, :], 1e-9, None, ALU.add))
            ch.link(dve.reciprocal(tok2[:, :], tok2[:, :]))
            ch.link(dve.tensor_tensor(gates[:, :, :], gates[:, :, :],
                                      tok2[:, :].unsqueeze(2).to_broadcast([P, NT, NE]), ALU.mult))

            def mix(m):
                g = r * UPS // 2 + m
                e, half = divmod(m, 2)
                dve.wait_ge(sig("down"), g + 1)
                if g >= 2:
                    dve.wait_ge(sig("mixed"), g - 1)
                for t in range(4):
                    j = 4 * half + t
                    ins = dve.scalar_tensor_tensor(XN[:, j, :], bank(6 + g % 2)[:, t * P:(t + 1) * P],
                                                   gates[:, j, e:e + 1], XN[:, j, :], ALU.mult, ALU.add)
                ins.then_inc(sig("mixed"), 1)

            for n in range(UPS):
                g = r * UPS + n
                dve.wait_ge(sig("silu"), g + 1)
                if g >= 4:
                    dve.wait_ge(sig("down"), (g - 4) // 2 + 1)
                dve.tensor_tensor(E6[:, g % 4, :], E6[:, 4 + g % 2, :], bank(2 * (g % 3) + 1), ALU.mult)\
                    .then_inc(sig("gated"), 1)
                if n >= 3 and n % 2 == 1:
                    mix((n - 3) // 2)
            mix(UPS // 2 - 1)
            dve.wait_ge(sig("mixed"), (r + 1) * UPS // 2)

        def tiles(ap, n):
            return [ap[:, i * T:(i + 1) * T] for i in range(n)]

        ot, va, ks, ee = tiles(OTf, 4), tiles(VAf, 4), tiles(KSf, 6), \
            tiles(E[:, :, :, :].rearrange("p a b c -> p (a b c)"), 3)
        LOGR, FLOOR, RR, EN = ot[0:2], ot[2:4], va[0:2], va[2:4]
        BCOL, DXB, SS, HH, HC = ee[0], ks[0:2], ks[2:4], ks[4:6], (ee[1], ee[2])
        DELTA, DX, LA, DTI = SCR[:, 1, :], SCR[:, 2, :], SCR[:, 0, :], SCR[0:DTR, 3, :]
        WW = SCR[:, 3, :]
        CARRY = XN1

        def scan_tensor(pe):
            pe.wait_ge(sig("ssm_in"), 16 * 5)
            pe.wait_ge(sig("xnt"), 2 * 5)
            project(pe, 0, wssm[:, 0:DTR], XNT, "dti_psum")
            pe.wait_ge(sig("dti"), 1)
            for half in range(2):
                ins = pe.matmul(bank(2 + half), wdt[:, :], DTI[:, half * HALF:(half + 1) * HALF], start=True, stop=True)
            ins.then_inc(sig("delta_psum"), 1)

            def rows(n):
                if n >= 1:
                    pe.wait_ge(sig("b_read"), n)
                project(pe, 0, wssm[:, DTR + n:DTR + n + 1].to_broadcast([P, P]), XNT, "b_psum")
                if n == 0:
                    pe.wait_ge(sig("delta"), 1)
                if n >= 2:
                    pe.wait_ge(sig("c_read"), n - 1)
                project(pe, 2 + 2 * (n % 2), wssm[:, DTR + NS + n:DTR + NS + n + 1].to_broadcast([P, P]), XNT, "c_psum")

            def gather(n):
                pe.wait_ge(sig("c_read"), n + 1)
                for half in range(2):
                    ins = pe.matmul(bank(6 + half), ident[:, :], HC[n % 2][:, half * HALF:(half + 1) * HALF],
                                    start=(n == 0), stop=(n == NS - 1), skip_group_check=True)
                ins.then_inc(sig("summed"), 1)

            for n in range(NS):
                rows(n)
                if n >= 2:
                    gather(n - 2)
            gather(NS - 2)
            gather(NS - 1)
            pe.wait_ge(sig("y_ready"), 1)
            for half in range(2):
                for j in range(4):
                    t = 4 * half + j
                    ins = pe.transpose(bank(half)[:, j * P:(j + 1) * P], LA[:, t * P:(t + 1) * P], ident[:, :])
                ins.then_inc(sig("y_turned"), 1)

        def scan_scalar(act, ch):
            act.wait_ge(sig("stack_k"), 16 * 24)
            act.wait_ge(sig("dti_psum"), 1)
            act.activation(DTI, two(0)[0:DTR, :], ACT.Copy).then_inc(sig("dti"), 1)
            act.wait_ge(sig("ssm_in"), 16 * 5)
            act.activation(amat[:, :], amat[:, :], ACT.Exp).then_inc(sig("a_exp"), 1)
            act.wait_ge(sig("delta_psum"), 1)
            ch.link(act.activation(DX, two(2), ACT.Abs, bias=ssmc[:, 0:1]))
            ch.link(act.activation(DX, DX, ACT.Exp, scale=-1.0))
            act.activation(DX, DX, ACT.Ln, bias=1.0).then_inc(sig("delta_ln"), 1)

            def b_copy(n):
                act.wait_ge(sig("b_psum"), n + 1)
                if n >= 1:
                    act.wait_ge(sig("dxb"), n)
                act.activation(BCOL, two(0), ACT.Copy).then_inc(sig("b_read"), 1)

            b_copy(0)
            for n in range(NS):
                act.wait_ge(sig("logr"), n + 1)
                if n >= 2:
                    act.wait_ge(sig("state"), n - 1)
                act.activation(RR[n % 2], LOGR[n % 2], ACT.Exp).then_inc(sig("rr"), 1)
                act.wait_ge(sig("floored"), n + 1)
                if n >= 2:
                    act.wait_ge(sig("input"), n - 1)
                act.activation(EN[n % 2], FLOOR[n % 2], ACT.Exp, scale=-1.0).then_inc(sig("en"), 1)
                if n + 1 < NS:
                    b_copy(n + 1)

        def scan_pool(pool):
            def dxb(n):
                pool.wait_ge(sig("b_read"), n + 1)
                if n == 0:
                    pool.wait_ge(sig("dx"), 1)
                if n >= 2:
                    pool.wait_ge(sig("input"), n - 1)
                pool.tensor_tensor(DXB[n % 2], DX, BCOL, ALU.mult).then_inc(sig("dxb"), 1)

            def state(n):
                pool.wait_ge(sig("s_sum"), n + 1)
                pool.wait_ge(sig("rr"), n + 1)
                if n >= 2:
                    pool.wait_ge(sig("c_read"), n - 1)
                pool.tensor_tensor(HH[n % 2], RR[n % 2], SS[n % 2], ALU.mult).then_inc(sig("state"), 1)

            dxb(0)
            dxb(1)
            for n in range(NS):
                state(n)
                if n + 2 < NS:
                    dxb(n + 2)

        def scan_vector(dve, ch):
            dve.wait_ge(sig("stack_k"), 16 * 24)
            dve.wait_ge(sig("turned"), 2 * 5)
            ch.link(dve.memset(XN1, 1.0))
            dve.memset(XN1.rearrange("p (b s) -> p b s", b=B)[:, :, 0:1], 0.0)
            dve.wait_ge(sig("a_exp"), 1)
            ch.link(dve.tensor_scalar(amat[:, :], amat[:, :], -1.0, None, ALU.mult))
            dve.wait_ge(sig("delta_ln"), 1)
            ch.link(dve.tensor_scalar(DELTA, two(2), ssmc[:, 0:1], 0.0, ALU.add, ALU.max))
            dve.tensor_tensor(DELTA, DELTA, DX, ALU.add).then_inc(sig("delta"), 1)
            dve.wait_ge(sig("delta"), 1)
            dve.tensor_tensor(DX, DELTA, XNT[:, :], ALU.mult).then_inc(sig("dx"), 1)

            def decay(n):
                ch.link(dve.tensor_scalar(LA, DELTA, amat[:, n:n + 1], -7.0, ALU.mult, ALU.max))
                if n >= 2:
                    dve.wait_ge(sig("rr"), n - 1)
                dve.tensor_tensor_scan(LOGR[n % 2], CARRY, LA, 0.0, ALU.mult, ALU.add).then_inc(sig("logr"), 1)
                dve.wait_ge(sig("logr"), n + 1)
                if n >= 2:
                    dve.wait_ge(sig("en"), n - 1)
                dve.tensor_scalar(FLOOR[n % 2], LOGR[n % 2], -20.0, None, ALU.max).then_inc(sig("floored"), 1)

            def accumulate(n):
                dve.wait_ge(sig("en"), n + 1)
                dve.wait_ge(sig("dxb"), n + 1)
                if n:
                    dve.wait_ge(sig("s_sum"), n)
                dve.tensor_tensor(WW, EN[n % 2], DXB[n % 2], ALU.mult).then_inc(sig("input"), 1)
                dve.wait_ge(sig("input"), n + 1)
                if n >= 2:
                    dve.wait_ge(sig("state"), n - 1)
                dve.tensor_tensor_scan(SS[n % 2], CARRY, WW, 0.0, ALU.mult, ALU.add).then_inc(sig("s_sum"), 1)

            def output(n):
                dve.wait_ge(sig("state"), n + 1)
                dve.wait_ge(sig("c_psum"), n + 1)
                if n >= 2:
                    dve.wait_ge(sig("summed"), n - 1)
                dve.tensor_tensor(HC[n % 2], HH[n % 2], two(2 + 2 * (n % 2)), ALU.mult).then_inc(sig("c_read"), 1)

            decay(0)
            for n in range(NS):
                if n + 1 < NS:
                    decay(n + 1)
                accumulate(n)
                if n:
                    output(n - 1)
            output(NS - 1)
            dve.wait_ge(sig("summed"), NS)
            dve.scalar_tensor_tensor(LA, XNT[:, :], ssmc[:, 1:2], two(6), ALU.mult, ALU.add).then_inc(sig("y_ready"), 1)
            for half in range(2):
                dve.wait_ge(sig("y_turned"), half + 1)
                x = X[:, 4 * half:4 * half + 4, :].rearrange("p j d -> p (j d)")
                ins = dve.tensor_tensor(x, x, bank(half), ALU.add)
            ins.then_inc(sig("x_res"), 1)

        HB = OTf.rearrange("p (j f) -> p j f", j=NT)
        GG = VAf.rearrange("p (j f) -> p j f", j=NT)
        ROUNDED = SCR[:, 0, :]
        QB = SCR[:, 1, 0:T // 2].bitcast(BF16)
        QTB = SCR[:, 1, T // 2:T].bitcast(BF16)
        GQ = SCR[:, 2, 0:T // 2].bitcast(BF16).rearrange("p (s f) -> p s f", s=2)
        GQT = SCR[:, 2, T // 2:T].bitcast(BF16).rearrange("p (s f) -> p s f", s=2)
        SQ = SCR[:, 3, 0:HALF]

        def halfbank(i):
            return bank(i).bitcast(BF16)

        def feed_vector_weights(dve, ch):
            dve.wait_ge(sig("ffn_in"), 16 * 2)
            ch.link(dve.tensor_reduce(wsum[:, :], wraw[:, :, :], AX, ALU.add, apply_absolute_value=True))
            dve.tensor_copy(wscale[:, :], wsum[:, :]).then_inc(sig("w_sums"), 1)
            dve.wait_ge(sig("w_total"), 1)
            ch.link(dve.tensor_scalar(wmean[:, :], bank(6)[:, 0:2], 1.0 / (FF * D), 1e-5, ALU.mult, ALU.max))
            ch.link(dve.reciprocal(wscale[:, :], wmean[:, :]))
            for w, dst in ((0, wq1[:, :]), (1, wq2[:, :, :].rearrange("p c d -> p (c d)"))):
                raw = wraw[:, w, :]
                ch.link(dve.tensor_scalar(raw, raw, wscale[:, w:w + 1], ROUND, ALU.mult, ALU.add))
                ch.link(dve.tensor_scalar(raw, raw, -ROUND, 1.0, ALU.add, ALU.min))
                dve.tensor_scalar(dst, raw, -1.0, None, ALU.max).then_inc(sig("w_quantised"), 1)

        def quant_factors(dve, ch, w):
            ch.link(dve.tensor_tensor(peak[:, :], peak[:, :], rstd[:, :], ALU.mult))
            ch.link(dve.tensor_scalar(peak[:, :], peak[:, :], 1e-5, None, ALU.max))
            ch.link(dve.reciprocal(fac[:, :], peak[:, :]))
            dve.tensor_scalar(deq[:, :], peak[:, :], 1.0 / 127.0, wmean[:, w:w + 1], ALU.mult, ALU.mult)
            ch.link(dve.scalar_tensor_tensor(fac[:, :], fac[:, :], 127.0, rstd[:, :], ALU.mult, ALU.mult))

        def feed_vector(dve, ch):
            dve.wait_ge(sig("xn"), 2 * 7)
            norm_stats(dve, ch, XN, 8, 1e-5, mean_square=True)
            ch.link(dve.tensor_reduce(peak[:, :], XN[:, :, :], AX, ALU.max, apply_absolute_value=True))
            norm_refine(dve, ch, 8)
            quant_factors(dve, ch, 0)
            for j in range(NT):
                ins = dve.tensor_scalar(ROUNDED[:, j * P:(j + 1) * P], XN[:, j, :], fac[:, j:j + 1], ROUND,
                                        ALU.mult, ALU.add)
            ch.link(ins)
            dve.tensor_scalar(QB, ROUNDED, -ROUND, 127.0, ALU.add, ALU.min).then_inc(sig("q1"), 1)
            dve.wait_ge(sig("bias_in"), 32)
            for j in range(NT):
                dve.wait_ge(sig("h1"), j + 1)
                dve.scalar_tensor_tensor(HB[:, j, :], bank(1 + j % 2), deq[:, j:j + 1], b1bc, ALU.mult, ALU.add)\
                    .then_inc(sig("h1_read"), 1)
                if j:
                    dve.wait_ge(sig("gelu"), j)
                    dve.tensor_reduce(peak[:, j - 1:j], GG[:, j - 1, :], AX, ALU.max, apply_absolute_value=True)
            dve.wait_ge(sig("gelu"), NT)
            ch.link(dve.tensor_reduce(peak[:, NT - 1:NT], GG[:, NT - 1, :], AX, ALU.max, apply_absolute_value=True))
            dve.wait_ge(sig("sumsq"), 1)
            dve.tensor_scalar(ve[:, :], sumsq[:, :], 1.0 / FF, 1e-5, ALU.mult, ALU.add).then_inc(sig("ve"), 1)
            norm_refine(dve, ch, 9)
            quant_factors(dve, ch, 1)
            b2 = b2bc.unsqueeze(1).to_broadcast([P, NT, D])
            ch.link(dve.tensor_tensor(X[:, :, :], X[:, :, :], b2, ALU.add))

            def finish(j):
                dve.wait_ge(sig("h2"), j + 1)
                dve.scalar_tensor_tensor(X[:, j, :], bank(6 + j % 2)[:, 0:D], deq[:, j:j + 1], X[:, j, :],
                                         ALU.mult, ALU.add).then_inc(sig("x_tile"), 1)

            for j in range(NT):
                ch.link(dve.tensor_scalar(HB[:, j, :], GG[:, j, :], fac[:, j:j + 1], ROUND, ALU.mult, ALU.add))
                if j >= 2:
                    dve.wait_ge(sig("g_turned"), j - 1)
                dve.tensor_scalar(GQ[:, j % 2, :], HB[:, j, :], -ROUND, 127.0, ALU.add, ALU.min)\
                    .then_inc(sig("q2"), 1)
                if j >= 2:
                    finish(j - 2)
            finish(NT - 2)
            finish(NT - 1)

        def feed_tensor(pe):
            pe.wait_ge(sig("q1"), 1)
            for j in range(NT):
                ins = pe.transpose(halfbank(3)[:, j * P:(j + 1) * P], QB[:, j * P:(j + 1) * P], identb[:, :])
            ins.then_inc(sig("q_turned"), 1)
            pe.wait_ge(sig("qt1"), 1)
            for j in range(NT):
                if j >= 2:
                    pe.wait_ge(sig("h1_read"), j - 1)
                pe.matmul(bank(1 + j % 2), QTB[:, j * P:(j + 1) * P], wq1[:, :], start=True, stop=True)\
                    .then_inc(sig("h1"), 1)

            def second(j):
                pe.wait_ge(sig("gt"), j + 1)
                if j >= 2:
                    pe.wait_ge(sig("x_tile"), j - 1)
                for c in range(FF // P):
                    ins = pe.matmul(bank(6 + j % 2)[:, 0:D], GQT[:, j % 2, c * P:(c + 1) * P], wq2[:, c, :],
                                    start=(c == 0), stop=(c == FF // P - 1))
                ins.then_inc(sig("h2"), 1)

            for j in range(NT):
                pe.wait_ge(sig("q2"), j + 1)
                if j >= 2:
                    pe.wait_ge(sig("gt"), j - 1)
                for c in range(FF // P):
                    ins = pe.transpose(halfbank(4 + j % 2)[:, c * P:(c + 1) * P], GQ[:, j % 2, c * P:(c + 1) * P],
                                       identb[:, :])
                ins.then_inc(sig("g_turned"), 1)
                if j:
                    second(j - 1)
            second(NT - 1)

        def feed_scalar(act, ch):
            norm_root(act, ch, 8)
            act.wait_ge(sig("q_turned"), 1)
            act.activation(QTB, halfbank(3)[:, 0:T], ACT.Copy).then_inc(sig("qt1"), 1)
            for j in range(NT):
                act.wait_ge(sig("h1_read"), j + 1)
                act.activation(GG[:, j, :], HB[:, j, :], ACT.Gelu).then_inc(sig("gelu"), 1)
                act.wait_ge(sig("gelu"), j + 1)
                ins = act.activation(SQ, GG[:, j, :], ACT.Square, accum_out=sumsq[:, j:j + 1])
            ins.then_inc(sig("sumsq"), 1)
            norm_root(act, ch, 9)
            for j in range(NT):
                act.wait_ge(sig("g_turned"), j + 1)
                if j >= 2:
                    act.wait_ge(sig("h2"), j - 1)
                act.activation(GQT[:, j % 2, :], halfbank(4 + j % 2)[:, 0:FF], ACT.Copy).then_inc(sig("gt"), 1)

        @block.sync
        def _(sp):
            def load(dst, src, signal):
                sp.dma_start(dst, src).then_inc(sig(signal), 16)

            load(X[:, :, :], inp["x"].rearrange("(j p) d -> p j d", p=P), "x_in")
            load(CT, inp["ctxT"], "ctx_in")
            load(wx[:, :, :, :], inp["w_x"].rearrange("l w p d -> p l w d"), "wx_in")
            load(wself[:, :, :], inp["w_self"].rearrange("w p d -> p w d"), "wself_in")
            load(bg[:, 0:1], inp["bg"].rearrange("(p o) -> p o", o=1), "bg_in")
            load(lens[:, :], inp["lens"].partition_broadcast(P), "lens_in")
            load(wox[:, :, :, :], inp["w_out"].rearrange("l g p d -> p l g d"), "wox_in")
            load(router[:, :], inp["router"], "router_in")
            load(normw[:, :], inp["normw"].rearrange("(p o) -> p o", o=1), "router_in")
            load(bqk[:, 0:2], inp["bqk"], "bqk_in")
            load(brow[0:1, :, :], inp["brow"].rearrange("(o w) d -> o w d", o=1), "brow_in")
            load(wssm[:, :], inp["w_ssm"], "ssm_in")
            load(wdt[:, :], inp["w_dt"], "ssm_in")
            load(ssmc[:, 0:1], inp["b_dt"].rearrange("(p o) -> p o", o=1), "ssm_in")
            load(ssmc[:, 1:2], inp["Dskip"].rearrange("(p o) -> p o", o=1), "ssm_in")
            load(amat[:, :], inp["A_log"], "ssm_in")
            for parts, stack, ready in ((KP, KSA, "ka_parts"), (QP, QS, "qa_parts")):
                sp.wait_ge(sig(ready), 1)
                sp.wait_ge(sig("stack_clear"), 1)
                for a in range(3):
                    for b in range(3):
                        r = 24 * a + 8 * b
                        part = a if stack is QS else b
                        sp.dma_start(stack[r:r + 8, :, :], parts[:, part, :]).then_inc(sig("stack_a"), 16)

            def cross_sync(L):
                sp.wait_ge(sig("qx_parts"), L + 1)
                for a in range(3):
                    for b in range(3):
                        r = 24 * a + 8 * b
                        sp.dma_start(QS[r:r + 8, :, :], QP[:, a, :]).then_inc(sig("stack_q"), 16)
                for b in range(B):
                    sp.wait_ge(sig("max_parts"), L * B + b + 1)
                    for c in range(3):
                        for q in range(QT):
                            t0 = b * S + q * P
                            sp.dma_start(QS[MAX_ROW + c:MAX_ROW + c + 1, :, t0:t0 + P],
                                         mxp[16 * q:16 * q + 16, b, c, :]).then_inc(sig("max_in%d" % b), 16)

            if last_stage >= 2:
                cross_sync(0)
            if last_stage >= 3:
                load(KSf[:, 0:2048], inp["w1"].rearrange("e p f -> p e f"), "experts_in")
                load(KSf[:, 2048:4096], inp["w3"].rearrange("e p f -> p e f"), "experts_in")
                load(W2, inp["w2"].rearrange("e (c p) d -> p e c d", p=P), "experts_in")
                load(wraw[:, 0, :], inp["w1T"], "ffn_in")
                load(wraw[:, 1, :].rearrange("p (c d) -> p c d", c=FF // P),
                     inp["w2T"].rearrange("(c p) d -> p c d", p=P), "ffn_in")
                x_ready(sp, 2)
                load(CT, inp["ctxT"], "ctx_in")
                load(PAD, inp["pad"].partition_broadcast(P), "pad_in")
                load(FRAW, inp["fside"].rearrange("w p n -> p w n"), "fside_in")
            if last_stage >= 5:
                x_ready(sp, 4)
                load(b1bc, inp["b1"].partition_broadcast(P), "bias_in")
                load(b2bc, inp["b2"].partition_broadcast(P), "bias_in")
                cross_sync(1)
            if last_stage == 6:
                for j in range(NT):
                    sp.wait_ge(sig("x_tile"), j + 1)
                    sp.dma_start(out[j * P:(j + 1) * P, :], X[:, j, :]).then_inc(sig("stored"), 16)
                sp.wait_ge(sig("stored"), 16 * NT)
            else:
                x_ready(sp, last_stage)
                sp.dma_start(out.rearrange("(j p) d -> p j d", p=P), X[:, :, :]).then_inc(sig("stored"), 16)
                sp.wait_ge(sig("stored"), 16)

        @block.gpsimd
        def _(pool):
            ch = Chain(pool, "pool_step")
            pool.memset(ident[:, :], 0.0)
            pool.memset(spread[:, :], 0.0)
            pool.memset(onesf[:, :], 1.0)
            pool.memset(causal[:, :], 1.0)
            ch.link(pool.memset(tri[:, :, :], 1.0))
            pool.affine_select(out=ident[:, :], in_=ident[:, :], compare_op=ALU.not_equal, fill=1.0,
                               base=0, pattern=[[-1, P]], channel_multiplier=1)
            heads = spread[:, :].rearrange("p (i e) -> p i e", i=HG)
            pool.affine_select(out=heads, in_=heads, compare_op=ALU.not_equal, fill=1.0, base=-DH,
                               pattern=[[-32, HG], [0, 32]], channel_multiplier=1)
            pool.affine_select(out=causal[:, :], in_=causal[:, :], compare_op=ALU.is_ge, fill=0.0,
                               base=0, pattern=[[1, P]], channel_multiplier=-1)
            ch.link(pool.affine_select(out=tri[:, :, :], in_=tri[:, :, :], compare_op=ALU.is_ge, fill=0.0,
                                       base=-1, pattern=[[1, NE], [-1, NE]], channel_multiplier=0))
            pool.memset(VX[:, :, :, :].rearrange("p a b c -> p (a b c)"), 0.0)
            pool.memset(VAf, 0.0)
            pool.tensor_scalar(identb[:, :], ident[:, :], 1.0, 0.0, ALU.mult, ALU.add)
            ch.link(pool.iota(iota, pattern=[[1, S]], base=0, channel_multiplier=0))
            pool.memset(VX[:, :, :, DH:DH + 1], 1.0)
            pool.memset(VA[:, :, :, DH:DH + 1], 1.0).then_inc(sig("const"), 1)
            KXf = KX[:, :, :].rearrange("p h t -> p (h t)").bitcast(F32)
            QSf = QS[:, :, :].rearrange("p h t -> p (h t)").bitcast(F32)
            pool.wait_ge(sig("const"), 1)
            ch.link(pool.memset(KSf[64:96, :], 0.0))
            ch.link(pool.memset(KSf[96:128, :], 0.0))
            ch.link(pool.memset(QS[64:96, :, :], 1.0))
            pool.memset(QSf[96:128, :], 0.0).then_inc(sig("stack_clear"), 1)
            pool.wait_ge(sig("stack_clear"), 1)
            ch.link(pool.memset(KXf[64:96, :], 0.0))
            pool.memset(KX[96:128, :, :], 1.0).then_inc(sig("stack_clear"), 1)
            pool.wait_ge(sig("stack_clear"), 2)
            pool.wait_ge(sig("lens_in"), 16)
            pool.tensor_scalar(lensf[:, :], lens[:, :], 1.0, 0.0, ALU.mult, ALU.add)
            ch.link(pool.tensor_scalar(iotaf, iota, 1.0, 0.0, ALU.mult, ALU.add))
            context_keys_pool(pool, ch, 0, NEG_X0)
            if last_stage >= 4:
                x_ready(pool, 2)
                pool.memset(QSf[96:128, :], 0.0).then_inc(sig("stack_clear"), 1)
                pool.wait_ge(sig("stack_clear"), 3)
                pool.wait_ge(sig("fside_in"), 16)
                pool.wait_ge(sig("w_quantised"), 2)
                rest = KXR.rearrange("p (w n) -> p w n", w=4)
                ch.link(pool.tensor_scalar(FPART[:, :, 0, :], FRAW, 1.0, 0.0, ALU.mult, ALU.add))
                ch.link(pool.tensor_tensor(rest, FRAW, FPART[:, :, 0, :], ALU.subtract))
                ch.link(pool.tensor_scalar(FPART[:, :, 1, :], rest, 1.0, 0.0, ALU.mult, ALU.add))
                pool.tensor_tensor(FPART[:, :, 2, :], rest, FPART[:, :, 1, :], ALU.subtract).then_inc(sig("bias_parts"), 1)
                pool.wait_ge(sig("bias_parts"), 1)
                context_keys_pool(pool, ch, 1, NEG_X1)
                pool.wait_ge(sig("stack_k"), 16 * 24)
                scan_pool(pool)

        @block.tensor
        def _(pe):
            pe.wait_ge(sig("const"), 1)
            context_tensor(pe, 0)
            norm_turn(pe, XN, 0)
            self_tensor(pe)
            if last_stage >= 2:
                norm_turn(pe, XN, 1)
                cross_tensor(pe, 0)
            if last_stage >= 3:
                norm_turn(pe, ZN, 2)
                experts_tensor(pe, 0)
                pe.wait_ge(sig("gated"), UPS)
                context_tensor(pe, 1)
                pe.wait_ge(sig("mixed"), UPS // 2)
                pe.wait_ge(sig("w_sums"), 1)
                pe.matmul(bank(6)[:, 0:2], onesf[:, :], wscale[:, :], start=True, stop=True).then_inc(sig("w_total"), 1)
                norm_turn(pe, ZN, 3)
                pe.wait_ge(sig("vx_ready"), 2)
                experts_tensor(pe, 1)
            if last_stage >= 4:
                norm_turn(pe, XN, 4)
                scan_tensor(pe)
            if last_stage >= 5:
                norm_turn(pe, XN, 5)
                cross_tensor(pe, 1)
            if last_stage >= 6:
                feed_tensor(pe)

        @block.scalar
        def _(act):
            ch = Chain(act, "act_step")
            context_scalar(act, 0)
            norm_root(act, ch, 0)
            norm_take(act, 0)
            self_scalar(act, ch)
            if last_stage >= 2:
                norm_root(act, ch, 1)
                norm_take(act, 1)
                cross_scalar(act, ch, 0)
            if last_stage >= 3:
                norm_root(act, ch, 2)
                act.wait_ge(sig("router_in"), 32)
                for r in range(LOOPS):
                    norm_root(act, ch, 3 + r)
                    norm_take(act, 2 + r, normw[:, 0:1])
                    experts_scalar(act, r)
                    if r == 0:
                        context_scalar(act, 1)
            if last_stage >= 4:
                norm_root(act, ch, 5)
                norm_take(act, 4)
                scan_scalar(act, ch)
            if last_stage >= 5:
                norm_root(act, ch, 6)
                norm_take(act, 5)
                cross_scalar(act, ch, 1)
            if last_stage >= 6:
                norm_root(act, ch, 7)
                feed_scalar(act, ch)

        @block.vector
        def _(dve):
            ch = Chain(dve, "dve_step")
            dve.wait_ge(sig("x_in"), 16)

            def layer_norm(k):
                norm_stats(dve, ch, X, k, 1e-5)
                norm_refine(dve, ch, k)

            layer_norm(0)
            norm_apply(dve, XN, X)
            self_vector(dve, ch)
            if last_stage >= 2:
                x_ready(dve, 1)
                layer_norm(1)
                norm_apply(dve, XN, X)
                cross_vector(dve, ch, 0)
            if last_stage >= 3:
                x_ready(dve, 2)
                layer_norm(2)
                for j in range(NT):
                    ins = dve.tensor_scalar(XN[:, j, :], X[:, j, :], mv[:, j, 0:1], rstd[:, j:j + 1],
                                            ALU.subtract, ALU.mult)
                ch.link(ins)
                for r in range(LOOPS):
                    norm_stats(dve, ch, XN, 3 + r, 1e-6, mean_square=True)
                    norm_refine(dve, ch, 3 + r)
                    for j in range(NT):
                        ins = dve.tensor_scalar(ZN[:, j, :], XN[:, j, :], rstd[:, j:j + 1], None, ALU.mult)
                        if j % 4 == 3:
                            ins.then_inc(sig("xn"), 1)
                    experts_vector(dve, ch, r)
                    if r == 0:
                        feed_vector_weights(dve, ch)
                x = X[:, :, :].rearrange("p j d -> p (j d)")
                dve.tensor_tensor(x, x, XN1, ALU.add).then_inc(sig("x_res"), 1)
            if last_stage >= 4:
                x_ready(dve, 3)
                layer_norm(5)
                norm_apply(dve, XN, X)
                scan_vector(dve, ch)
            if last_stage >= 5:
                x_ready(dve, 4)
                layer_norm(6)
                norm_apply(dve, XN, X)
                cross_vector(dve, ch, 1)
            if last_stage >= 6:
                x_ready(dve, 5)
                layer_norm(7)
                norm_apply(dve, XN, X)
                feed_vector(dve, ch)


def kernel(**inputs):
    import numpy as np
    import concourse.bacc as bacc
    from concourse import mybir as mb
    from concourse.bass_utils import run_bass_kernel_spmd

    a = {k: np.asarray(v) for k, v in inputs.items()}

    def by_feature(w):
        return w.reshape(H, DH, D).transpose(2, 1, 0).reshape(D, D)

    def padded(w):
        full = np.zeros((NG, HG, 32, D), w.dtype)
        full[:, :, 0:DH] = w.T.reshape(NG, HG, DH, D)
        return full.reshape(NG, P, D)

    arrays = {
        "x": a["x"].reshape(T, D),
        "ctxT": a["ctx_1024"].reshape(T, D).T,
        "w_self": np.stack([by_feature(a["L0_attn_Wq"]), by_feature(a["L0_attn_Wk"]), by_feature(a["L0_attn_Wg"]),
                            a["L0_attn_Wv"].T]),
        "bg": a["L0_attn_bg"].reshape(H, DH).T.reshape(D),
        "w_x": np.stack([np.stack([by_feature(a["L0_xattn_W_q"]), by_feature(a["L0_xattn_W_k"]), a["L0_xattn_W_v"].T]),
                         np.stack([by_feature(a["L1_xattn_Wq"]), by_feature(a["L1_xattn_Wk"]), a["L1_xattn_Wv"].T])]),
        "w_out": np.stack([padded(a["L0_attn_Wo"]), padded(a["L0_xattn_W_o"]), padded(a["L1_xattn_Wo"])]),
        "lens": a["mask_B_ik0"],
        "pad": a["mask_BxS2_bk0"].reshape(T),
        "fside": np.concatenate([a["fside_SxS2_0"].reshape(QT, P, S), a["fside_SxS2_0"].T.reshape(QT, P, S)]),
        "bqk": np.stack([a["L1_xattn_bq"].reshape(H, DH).T.reshape(D), a["L1_xattn_bk"].reshape(H, DH).T.reshape(D)], 1),
        "brow": np.stack([a["L1_xattn_bv"], a["L1_xattn_bo"]]),
        "router": a["L0_ffn_router_w"],
        "normw": a["L0_ffn_norm_w"],
        "w1": a["L0_ffn_w1"], "w3": a["L0_ffn_w3"], "w2": a["L0_ffn_w2"],
        "w_ssm": a["L1_attn_W_xproj"], "w_dt": a["L1_attn_W_dt"], "b_dt": a["L1_attn_b_dt"],
        "Dskip": a["L1_attn_D"], "A_log": a["L1_attn_A_log"],
        "w1T": a["L1_ffn_w1"].T, "w2T": a["L1_ffn_w2"].T, "b1": a["L1_ffn_b1"], "b2": a["L1_ffn_b2"],
    }
    nc = bacc.Bacc("TRN2", target_bir_lowering=False, num_devices=1)
    arrays = {k: np.ascontiguousarray(v) for k, v in arrays.items()}
    inp = {k: nc.dram_tensor("in_" + k, v.shape, mb.dt.from_np(v.dtype), kind="ExternalInput").ap()
           for k, v in arrays.items()}
    out = nc.dram_tensor("out_x", (T, D), mb.dt.float32, kind="ExternalOutput").ap()
    build(nc, inp, out)
    r = run_bass_kernel_spmd(nc, [{"in_" + k: v for k, v in arrays.items()}], core_ids=[0])
    return r.results[0]["out_x"].reshape(B, S, D)
```

```python
from contextlib import ExitStack

import numpy as np

import concourse.bass as bass
from concourse import mybir

F32 = mybir.dt.float32
BF16 = mybir.dt.bfloat16
I32 = mybir.dt.int32
U8 = mybir.dt.uint8
ALU = mybir.AluOpType
ACT = mybir.ActivationFunctionType
AX = mybir.AxisListType.X

P = 128
B, S, D = 4, 256, 128
T = B * S
NT = T // P
QT = S // P
H = 16
DH = D // H
HG = 4
NG = H // HG
NE, FE = 8, 256
NS = 16
DTR = 64
FF = 512
HALF = 512
PAIRS = H // 2
UNITS = B * PAIRS
ONES_PAIR = 1.0019378662109375
ROUND = 12582912.0
CLAMP_EXP = 485165195.40979
LOG_TINY = -87.3
NEG_X0 = 1.0e6
NEG_X1 = 1.0e30
MAX_ROW = 96
NEG_ROW = 72


def bf16_parts(v):
    parts = []
    for _ in range(3):
        bits = int(np.float32(v).view(np.uint32))
        bits = (bits + 0x7FFF + ((bits >> 16) & 1)) & 0xFFFF0000
        part = float(np.uint32(bits).view(np.float32))
        parts.append(part)
        v = v - part
    return parts


def build(nc, inp, out, last_stage=6):
    ctx = ExitStack()
    with ctx:
        def sb(name, shape, dt=F32):
            return ctx.enter_context(nc.sbuf_tensor(name, shape, dt))

        signals = {}

        def sig(name):
            if name not in signals:
                signals[name] = ctx.enter_context(nc.semaphore(name))
            return signals[name]

        PS = ctx.enter_context(nc.psum_tensor("PS", [P, 8, HALF], F32))

        X = sb("X", [P, NT, D])
        XN = sb("XN", [P, NT, D])
        XNT = sb("XNT", [P, T])
        QS = sb("QS", [P, H, T], BF16)
        KSA = sb("KSA", [P, H, T], BF16)
        KX = sb("KX", [P, H, T], BF16)
        VA = sb("VA", [P, NT, H, 32])
        VX = sb("VX", [P, NT, H, 32])
        SCR = sb("SCR", [P, 4, T])
        OT = sb("OT", [P, NG, T])
        E = sb("E", [P, 3, 2, HALF])
        wself = sb("wself", [P, 4, D])
        wox = sb("wox", [P, 3, NG, D])
        wx = sb("wx", [P, 2, 3, D])
        ident = sb("ident", [P, P])
        identb = sb("identb", [P, P], BF16)
        masks = sb("masks", [P, 3, P])
        spread = sb("spread", [P, P])
        onesf = masks[:, 1, :]
        den_eps = sb("den_eps", [P, 1])
        bg = sb("bg", [P, 2])
        bqk = sb("bqk", [P, 3])
        brow = sb("brow", [1, D])
        st = sb("st", [P, NT, 6])
        mv = sb("mv", [P, NT, 2])
        ve = sb("ve", [P, NT])
        lnv = sb("lnv", [P, NT])
        rs = sb("rs", [P, NT])
        rt = sb("rt", [P, NT])
        rstd = sb("rstd", [P, NT])
        lens = sb("lens", [P, B], I32)
        lensf = sb("lensf", [P, B])
        mx = sb("mx", [P, 2, QT, H])
        mxr = sb("mxr", [32, 2, P])
        mxp = sb("mxp", [32, B, 3, P], BF16)

        QP = E[:, 0:2].rearrange("p a b c -> p (a b c)").bitcast(BF16)[:, 0:3 * T].rearrange("p (a t) -> p a t", a=3)
        EF = E[:, :, :, :].rearrange("p a b c -> p (a b c)").bitcast(BF16)
        KP = EF[:, 3 * T:6 * T].rearrange("p (a t) -> p a t", a=3)
        OTf = OT[:, :, :].rearrange("p g t -> p (g t)")
        KXP = OTf[:, 0:3 * T // 2].bitcast(BF16).rearrange("p (a t) -> p a t", a=3)
        KX32 = OTf[:, 3 * T // 2:5 * T // 2]
        KXR = OTf[:, 5 * T // 2:7 * T // 2]
        NEGP = OTf[:, 3 * T // 2:3 * T].bitcast(BF16).rearrange("p (a t) -> p a t", a=3)
        iota = OTf[:, 7 * T // 2:7 * T // 2 + S].bitcast(I32)
        iotaf = OTf[:, 7 * T // 2 + S:4 * T]
        VMASK = SCR[:, 2, :]
        CT = SCR[:, 3, :]
        KSf = KSA[:, :, :].rearrange("p h t -> p (h t)").bitcast(F32)
        W1 = KSf[:, 0:2048].rearrange("p (e f) -> p e f", e=NE)
        W3 = KSf[:, 2048:4096].rearrange("p (e f) -> p e f", e=NE)
        W2 = KSf[:, 4096:6144].rearrange("p (e c d) -> p e c d", e=NE, c=2)
        BIASQ = KSf[:, 6144:6144 + QT * S].rearrange("p (q n) -> p q n", q=QT)
        BIASK = KSf[:, 6144 + QT * S:6144 + QT * S + 3 * QT * S // 2].bitcast(BF16)\
            .rearrange("p (k c n) -> p k c n", k=QT, c=3)
        VAf = VA[:, :, :, :].rearrange("p a b c -> p (a b c)")
        XN1 = XN[:, :, :].rearrange("p j d -> p (j d)")
        E6 = E[:, :, :, :].rearrange("p a b c -> p (a b) c")
        PAD = SCR[:, 0, 0:T // 4].bitcast(U8)
        FRAW = SCR[:, 1, :].rearrange("p (w n) -> p w n", w=4)
        BIASED = SCR[:, 2, :].rearrange("p (s i n) -> p s i n", s=2, i=2)
        KXf = KX[:, :, :].rearrange("p h t -> p (h t)").bitcast(F32)
        QSf = QS[:, :, :].rearrange("p h t -> p (h t)").bitcast(F32)

        router = sb("router", [P, NE])
        normw = sb("normw", [P, 1])
        tri = sb("tri", [P, NE, NE])
        logits = sb("logits", [P, NT, NE])
        gates = sb("gates", [P, NT, NE])
        chosen = sb("chosen", [P, NT, NE])
        tok1 = sb("tok1", [P, NT])
        tok2 = sb("tok2", [P, NT])
        select = sb("select", [P, 2 * NS], BF16)
        wssm = sb("wssm", [P, DTR + 2 * NS])
        wdt = sb("wdt", [DTR, P])
        ssmc = sb("ssmc", [P, 3])
        amat = sb("amat", [P, NS])
        wraw = KSf[:, 6144:6144 + 2 * FF].rearrange("p (w f) -> p w f", w=2)
        wq1 = sb("wq1", [P, FF], BF16)
        wq2 = sb("wq2", [P, FF // P, D], BF16)
        b1bc = KSf[:, 0:FF]
        b2bc = KSf[:, FF:FF + D]
        bobc = KSf[:, FF + D:FF + 2 * D]
        wsum = sb("wsum", [P, 2])
        wmean = sb("wmean", [P, 2])
        wscale = sb("wscale", [P, 2])
        peak, fac, deq, sumsq = (logits[:, i, :] for i in range(4))

        block = ctx.enter_context(nc.Block())

        def bank(i):
            return PS[:, i, :]

        class Chain:
            def __init__(self, eng, name):
                self.eng, self.sem, self.n = eng, sig(name), 0

            def link(self, ins):
                ins.then_inc(self.sem, 1)
                self.n += 1
                self.eng.wait_ge(self.sem, self.n)

            def mark(self, ins):
                ins.then_inc(self.sem, 1)
                self.n += 1

            def wait(self):
                self.eng.wait_ge(self.sem, self.n)

        def norm_stats(dve, ch, src, k, eps, mean_square=False):
            if src is not None:
                for j in range(NT):
                    ins = dve.bn_stats(st[:, j, :], src[:, j, :])
                ch.link(ins)
            for j in range(NT):
                ins = dve.bn_aggr(mv[:, j, :], st[:, j, :])
            ch.link(ins)
            if mean_square:
                ch.link(dve.tensor_tensor(rt[:, :], mv[:, :, 0], mv[:, :, 0], ALU.mult))
                ch.link(dve.tensor_tensor(ve[:, :], rt[:, :], mv[:, :, 1], ALU.add))
                dve.tensor_scalar(ve[:, :], ve[:, :], eps, None, ALU.add).then_inc(sig("ve"), 1)
            else:
                dve.tensor_scalar(ve[:, :], mv[:, :, 1], eps, None, ALU.add).then_inc(sig("ve"), 1)

        def exp_and_ln(act):
            act.preload_act_table_set("natural_log_exp_and_others")

        def norm_root(act, ch, k):
            act.wait_ge(sig("ve"), k + 1)
            ch.link(act.activation(lnv[:, :], ve[:, :], ACT.Ln))
            act.activation(rs[:, :], lnv[:, :], ACT.Exp, scale=-0.5).then_inc(sig("root"), 1)

        def norm_refine(dve, ch, k):
            dve.wait_ge(sig("root"), k + 1)
            ch.link(dve.tensor_tensor(rt[:, :], rs[:, :], rs[:, :], ALU.mult))
            ch.link(dve.tensor_tensor(rt[:, :], rt[:, :], ve[:, :], ALU.mult))
            ch.link(dve.tensor_scalar(rt[:, :], rt[:, :], -0.5, 1.5, ALU.mult, ALU.add))
            ch.link(dve.tensor_tensor(rstd[:, :], rt[:, :], rs[:, :], ALU.mult))

        def norm_apply(dve, dst, src):
            for j in range(NT):
                ins = dve.tensor_scalar(dst[:, j, :], src[:, j, :], mv[:, j, 0:1], rstd[:, j:j + 1],
                                        ALU.subtract, ALU.mult)
                if j % 4 == 3:
                    ins.then_inc(sig("xn"), 1)

        def norm_turn(pe, src, o):
            for half in range(2):
                pe.wait_ge(sig("xn"), 2 * o + half + 1)
                if o == 0:
                    pe.wait_ge(sig("ident"), 1)
                for j in range(4):
                    ins = pe.transpose(bank(4 + half)[:, j * P:(j + 1) * P], src[:, 4 * half + j, :], ident[:, :])
                ins.then_inc(sig("turned"), 1)

        def norm_take(act, o, scale=None):
            for half in range(2):
                act.wait_ge(sig("turned"), 2 * o + half + 1)
                if scale is None:
                    ins = act.activation(XNT[:, half * HALF:(half + 1) * HALF], bank(4 + half), ACT.Copy)
                else:
                    ins = act.activation(XNT[:, half * HALF:(half + 1) * HALF], bank(4 + half), ACT.Copy, scale=scale)
                ins.then_inc(sig("xnt"), 1)

        def project(pe, first_bank, lhsT, rhs, signal):
            for half in range(2):
                ins = pe.matmul(bank(first_bank + half)[0:lhsT.shape[1], :], lhsT,
                                rhs[:, half * HALF:(half + 1) * HALF], start=True, stop=True)
            ins.then_inc(sig(signal), 1)

        def two(b):
            return PS[:, b:b + 2, :].rearrange("p a n -> p (a n)")

        def split(dve, ch, dst, src, tmp, signal):
            ch.link(dve.tensor_copy(dst[:, 0, :], src))
            ch.link(dve.tensor_tensor(tmp, src, dst[:, 0, :], ALU.subtract))
            ch.link(dve.tensor_copy(dst[:, 1, :], tmp))
            dve.tensor_tensor(dst[:, 2, :], tmp, dst[:, 1, :], ALU.subtract).then_inc(sig(signal), 1)

        def o_region(u):
            g = (u % PAIRS) // 2
            return bank(6)[:, (g % 2) * S:(g % 2) * S + S]

        def o_rows(u, i):
            r = 32 * ((2 * u + i) % HG)
            return slice(r, r + 32)

        NZ = UNITS // 4
        STEPS = QT * PAIRS + 1

        def out_evac(act, A, z, bias):
            act.wait_ge(sig("o_full"), A * NZ + z + 1)
            if A == 0 and z == 0:
                act.wait_ge(sig("stack_k"), 16 * 12)
            b, x = z // 2, z % 2
            dst = OT[:, 2 * x:2 * x + 2, b * S:(b + 1) * S]
            src = bank(6).rearrange("p (g t) -> p g t", g=2)
            if bias:
                ins = act.activation(dst, src, ACT.Identity, bias=den_eps[:, 0:1])
            else:
                ins = act.activation(dst, src, ACT.Copy)
            ins.then_inc(sig("o_taken"), 1)

        def den_bank(z):
            return bank(5 if z == NZ - 1 else 7)

        def scratch(z):
            s = SCR[:, 0 if z == NZ - 1 else 1, :]
            return s[:, 0:HALF], s[:, HALF:T]

        def den_spread(pe, A, z):
            pe.wait_ge(sig("o_taken"), A * NZ + z + 1)
            if z == NZ - 1:
                pe.wait_ge(sig("maxed" if A else "a_masked"), A * B * STEPS if A else UNITS)
            elif z or A:
                pe.wait_ge(sig("o_normed"), A * NZ + z)
            if z and z % 2 == 0:
                pe.wait_ge(sig("x_batch"), A * (B - 1) + z // 2)
            b, x = z // 2, z % 2
            pe.matmul(den_bank(z).rearrange("p (g t) -> p g t", g=2), spread[:, :],
                      OT[:, 2 * x:2 * x + 2, b * S:(b + 1) * S], start=True, stop=True).then_inc(sig("den"), 1)

        def invert(dve, ch, dst, den, guess):
            ch.link(dve.tensor_tensor(dst, den, guess, ALU.mult))
            ch.link(dve.scalar_tensor_tensor(dst, dst, 2.0, guess, ALU.subtract, ALU.mult, reverse0=True))

        def den_guess(act, ch, A, z):
            act.wait_ge(sig("den"), A * NZ + z + 1)
            if (z or A) and z != NZ - 1:
                act.wait_ge(sig("o_normed"), A * NZ + z)
            guess = scratch(z)[1]
            ch.link(act.activation(guess, den_bank(z), ACT.Ln))
            act.activation(guess, guess, ACT.Exp, scale=-1.0).then_inc(sig("den_guess"), 1)

        def out_norm(dve, ch, A, z):
            b, x = z // 2, z % 2
            dve.wait_ge(sig("den_guess"), A * NZ + z + 1)
            inverse, guess = scratch(z)
            invert(dve, ch, inverse, den_bank(z), guess)
            o = OT[:, 2 * x:2 * x + 2, b * S:(b + 1) * S]
            dve.tensor_tensor(o, o, inverse.rearrange("p (g t) -> p g t", g=2), ALU.mult).then_inc(sig("o_normed"), 1)

        def out_project(pe, A, b):
            pe.wait_ge(sig("o_normed"), A * NZ + 2 * b + 2)
            pe.wait_ge(sig("wox_in"), 16)
            for q in range(QT):
                o = bank(7)[:, q * P:(q + 1) * P]
                t0 = b * S + q * P
                for g in range(NG):
                    ins = pe.matmul(o, OT[:, g, t0:t0 + P], wox[:, A, g, :], start=(g == 0), stop=(g == NG - 1))
            ins.then_inc(sig("proj_out"), 1)

        def residual(dve, ch, A, b):
            dve.wait_ge(sig("proj_out"), A * B + b + 1)
            x = X[:, QT * b:QT * (b + 1), :].rearrange("p j d -> p (j d)")
            last = b == B - 1
            dve.tensor_tensor(x, x, bank(7)[:, 0:QT * P], ALU.add).then_inc(sig("x_res" if last else "x_batch"), 1)
            if last:
                dve.wait_ge(sig("x_res"), (1, 2, 5)[A])
            else:
                dve.wait_ge(sig("x_batch"), A * (B - 1) + b + 1)
            for j in range(QT * b, QT * (b + 1)):
                ins = dve.bn_stats(st[:, j, :], X[:, j, :])
            ch.link(ins)

        SPREAD, GUESSED, DIVIDE, PROJECT, ADD = ((7, 8, 8), (None, 8, 8), (10, 9, 9), (9, 10, 10), (12, 11, 11))

        def at(u, after, whole=False):
            z = (u - after) // 4
            return z if (u - after) % 4 == 0 and 0 <= z < NZ and (z % 2 or not whole) else None

        def output_tensor(pe, A, u):
            z = at(u, PROJECT[A], whole=True)
            if z is not None:
                out_project(pe, A, z // 2)
            z = at(u, SPREAD[A])
            if z is not None:
                den_spread(pe, A, z)

        def output_vector(dve, ch, A, u):
            z = at(u, DIVIDE[A])
            if z is not None:
                out_norm(dve, ch, A, z)
            z = at(u, ADD[A], whole=True)
            if z is not None:
                residual(dve, ch, A, z // 2)

        LAST = UNITS + 12

        def x_ready(eng, stage):
            eng.wait_ge(sig("x_res"), stage)

        def context_tensor(pe, L):
            if L == 0:
                pe.wait_ge(sig("ctx_in"), 16)
                pe.wait_ge(sig("wx_in"), 16)
            else:
                pe.wait_ge(sig("ctx_in"), 32)
                pe.wait_ge(sig("brow_in"), 16)
            project(pe, 0, wx[:, L, 1, :], CT, "kx_psum")
            for j in range(NT):
                o = bank(2 + j // 4)[:, (j % 4) * P:(j % 4 + 1) * P]
                ins = pe.matmul(o, CT[:, j * P:(j + 1) * P], wx[:, L, 2, :], start=True, stop=(L == 0))
                if L == 1:
                    ins = pe.matmul(o, onesf[0:1, :], brow[0:1, :], start=False, stop=True)
            ins.then_inc(sig("vx_psum"), 1)

        def take_values(act, dst, first_bank):
            for half in range(2):
                ins = act.activation(dst[:, 4 * half:4 * half + 4, :, 0:DH].rearrange("p j h e -> p (j h) e"),
                                     bank(first_bank + half).rearrange("p (a e) -> p a e", e=DH), ACT.Copy)
            return ins

        def context_scalar(act, L):
            act.wait_ge(sig("kx_psum"), L + 1)
            if L == 0:
                act.activation(KX32, two(0), ACT.Copy).then_inc(sig("kx_raw"), 1)
            else:
                act.wait_ge(sig("bqk_in"), 16)
                act.activation(KX32, two(0), ACT.Identity, bias=bqk[:, 1:2]).then_inc(sig("kx_raw"), 1)
            act.wait_ge(sig("vx_psum"), L + 1)
            take_values(act, VX, 2).then_inc(sig("vx_ready"), 1)

        def context_keys_pool(pool, ch, L, neg):
            if L == 0:
                for b in range(B):
                    ins = pool.tensor_scalar(VMASK[:, b * S:(b + 1) * S], iotaf, lensf[:, b:b + 1], None,
                                             ALU.is_lt)
                ch.link(ins)
            else:
                pool.wait_ge(sig("pad_in"), 16)
                ch.link(pool.tensor_scalar(VMASK, PAD, -1.0, 1.0, ALU.mult, ALU.add))
            pool.wait_ge(sig("kx_raw"), L + 1)
            ch.link(pool.tensor_tensor(KX32, KX32, VMASK, ALU.mult))
            ch.link(pool.tensor_scalar(KXP[:, 0, :], KX32, 1.0, 0.0, ALU.mult, ALU.add))
            ch.link(pool.tensor_tensor(KXR, KX32, KXP[:, 0, :], ALU.subtract))
            ch.link(pool.tensor_scalar(KXP[:, 1, :], KXR, 1.0, 0.0, ALU.mult, ALU.add))
            pool.tensor_tensor(KXP[:, 2, :], KXR, KXP[:, 1, :], ALU.subtract).then_inc(sig("kx_parts"), 1)
            pool.wait_ge(sig("kx_parts"), L + 1)
            for c, part in enumerate(bf16_parts(neg)):
                ins = pool.tensor_scalar(NEGP[:, c, :], VMASK, -1.0, part, ALU.add, ALU.mult)
            ins.then_inc(sig("neg_parts"), 1)

        def stack_context(eng, L):
            eng.wait_ge(sig("kx_parts"), L + 1)
            if L == 0:
                eng.wait_ge(sig("kx_clear"), 1)
            for a in range(3):
                for b in range(3):
                    r = 24 * a + 8 * b
                    eng.dma_start(KX[r:r + 8, :, :], KXP[:, b, :]).then_inc(sig("stack_k"), 16)
            eng.wait_ge(sig("neg_parts"), L + 1)
            for c in range(3):
                eng.dma_start(KX[NEG_ROW + c:NEG_ROW + c + 1, :, :], NEGP[0:H, c, :]).then_inc(sig("stack_k"), 16)

        def weighed(eng, A, v):
            if v % 4 == 3:
                eng.wait_ge(sig("o_full"), A * NZ + v // 4 + 1)
            else:
                eng.wait_ge(sig("weighed"), A * (UNITS - NZ) + v + 1 - (v + 1) // 4)

        def o_free(pe, A, u):
            if u % 4 == 0 and (A or u):
                pe.wait_ge(sig("o_taken"), A * NZ + u // 4)

        def self_tensor(pe):
            pe.wait_ge(sig("wself_in"), 16)
            pe.wait_ge(sig("xnt"), 2)
            project(pe, 6, wself[:, 2, :], XNT, "self_proj")
            pe.wait_ge(sig("kx_raw"), 1)
            project(pe, 0, wself[:, 1, :], XNT, "self_proj")
            pe.wait_ge(sig("vx_ready"), 1)
            project(pe, 2, wself[:, 0, :], XNT, "self_proj")
            for j in range(NT):
                ins = pe.matmul(bank(4 + j // 4)[:, (j % 4) * P:(j % 4 + 1) * P], XNT[:, j * P:(j + 1) * P],
                                wself[:, 3, :], start=True, stop=True)
            ins.then_inc(sig("self_proj"), 1)
            pe.wait_ge(sig("stack_a"), 16 * 18)
            pe.wait_ge(sig("ka_clear"), 1)
            pe.wait_ge(sig("q_clear"), 1)
            pe.wait_ge(sig("q_zero"), 1)
            pe.wait_ge(sig("va_const"), 1)
            pe.wait_ge(sig("va_ready"), 1)

            def scores(u):
                if u >= 3:
                    pe.wait_ge(sig("a_masked"), u - 2)
                b, hp = divmod(u, PAIRS)
                t0 = b * S
                for i in range(2):
                    h = 2 * hp + i
                    o = bank(2 * (u % 3) + i)
                    pe.matmul(o[:, 0:S], KSA[:, h, t0:t0 + P], QS[:, h, t0:t0 + S], start=True, stop=True)
                    ins = pe.matmul(o[:, S:S + P], KSA[:, h, t0 + P:t0 + S], QS[:, h, t0 + P:t0 + S],
                                    start=True, stop=True)
                ins.then_inc(sig("a_scores"), 1)

            def weigh(u):
                b, hp = divmod(u, PAIRS)
                pe.wait_ge(sig("a_masked"), u + 1)
                o_free(pe, 0, u)
                for i in range(2):
                    pe.matmul(o_region(u)[o_rows(u, i), :], VA[:, 2 * b, 2 * hp + i, :], E[:, u % 3, i, 0:S],
                              start=True, stop=False, skip_group_check=True)
                for i in range(2):
                    ins = pe.matmul(o_region(u)[o_rows(u, i), P:S], VA[:, 2 * b + 1, 2 * hp + i, :],
                                    E[:, u % 3, i, S:S + P], start=False, stop=True, skip_group_check=True)
                ins.then_inc(sig("o_full" if u % 4 == 3 else "weighed"), 1)

            scores(0)
            scores(1)
            for u in range(UNITS):
                if u + 2 < UNITS:
                    scores(u + 2)
                weigh(u)
                output_tensor(pe, 0, u)
            for u in range(UNITS, LAST):
                output_tensor(pe, 0, u)

        EG = SCR[:, 0, :]
        SPQ = SCR[:, 3, :]
        R1 = SCR[:, 1, :]

        def self_scalar(act, ch):
            act.wait_ge(sig("self_proj"), 1)
            act.wait_ge(sig("bg_neg"), 1)
            act.activation(EG, two(6), ACT.Exp, bias=bg[:, 1:2], scale=-1.0).then_inc(sig("self_gate"), 1)
            for n, dst in enumerate((XN1, SPQ)):
                act.wait_ge(sig("self_proj"), n + 2)
                ch.link(act.activation(dst, two(2 * n), ACT.Abs))
                ch.link(act.activation(dst, dst, ACT.Exp, scale=-1.0))
                act.activation(dst, dst, ACT.Ln, bias=1.0).then_inc(sig("self_sp"), 1)
                if n == 0:
                    act.wait_ge(sig("gate_den"), 1)
                    ch.link(act.activation(R1, EG, ACT.Ln))
                    act.activation(R1, R1, ACT.Exp, scale=-1.0).then_inc(sig("gate_guess"), 1)
            act.wait_ge(sig("self_proj"), 4)
            take_values(act, VA, 4).then_inc(sig("va_ready"), 1)
            act.wait_ge(sig("den_eps"), 1)
            out_evac(act, 0, 0, True)
            for z in range(NZ):
                if z + 1 < NZ:
                    out_evac(act, 0, z + 1, True)
                den_guess(act, ch, 0, z)

        def self_vector(dve, ch):
            dve.wait_ge(sig("bg_in"), 16)
            dve.tensor_scalar(bg[:, 1:2], bg[:, 0:1], -1.0, None, ALU.mult).then_inc(sig("bg_neg"), 1)
            dve.memset(QSf[96:128, :], 0.0).then_inc(sig("q_zero"), 1)
            dve.wait_ge(sig("self_gate"), 1)
            dve.tensor_scalar(EG, EG, 1e18, 1.0, ALU.min, ALU.add).then_inc(sig("gate_den"), 1)
            dve.wait_ge(sig("self_sp"), 1)
            ch.link(dve.scalar_tensor_tensor(XN1, two(0), 0.0, XN1, ALU.max, ALU.add))
            dve.wait_ge(sig("self_proj"), 4)
            split(dve, ch, KP, XN1, XNT[:, :], "ka_parts")
            dve.wait_ge(sig("gate_guess"), 1)
            invert(dve, ch, EG, EG, R1)
            dve.wait_ge(sig("self_sp"), 2)
            ch.link(dve.scalar_tensor_tensor(SPQ, two(2), 0.0, SPQ, ALU.max, ALU.add))
            ch.link(dve.scalar_tensor_tensor(SPQ, EG, 1e-6, SPQ, ALU.add, ALU.mult))
            split(dve, ch, QP, SPQ, R1, "qa_parts")
            dve.wait_ge(sig("const"), 1)
            ch.link(dve.tensor_reduce(den_eps[:, :], spread[:, :], AX, ALU.max))
            dve.tensor_scalar(den_eps[:, :], den_eps[:, :], 1e-6, None, ALU.mult).then_inc(sig("den_eps"), 1)
            mask = masks[:, :, :].rearrange("p a n -> p (a n)").unsqueeze(1).to_broadcast([P, 2, 3 * P])
            dve.wait_ge(sig("stack_a"), 16 * 18)
            for u in range(UNITS):
                bk = 2 * (u % 3)
                dve.wait_ge(sig("a_scores"), u + 1)
                if u >= 3:
                    weighed(dve, 0, u - 3)
                dve.tensor_tensor(E[:, u % 3, :, 0:3 * P], PS[:, bk:bk + 2, 0:3 * P], mask, ALU.mult)\
                    .then_inc(sig("a_masked"), 1)
                output_vector(dve, ch, 0, u)
            for u in range(UNITS, LAST):
                output_vector(dve, ch, 0, u)

        CHUNKS = (3, 3, 3, 3, 3, 2, 0, 0)

        def steps_before(u):
            b, hp = divmod(u, PAIRS)
            if b + 1 < B:
                k0 = sum(CHUNKS[:hp])
                for k in range(k0, k0 + CHUNKS[hp]):
                    yield b + 1, k

        def cross_tensor(pe, L):
            A = L + 1
            pe.wait_ge(sig("xnt"), 2 * ((1, 5)[L] + 1))
            project(pe, 0, wx[:, L, 0, :], XNT, "qx_psum")
            pe.wait_ge(sig("qx_raw"), L + 1)
            pe.wait_ge(sig("stack_q0"), 16 * 9 * (L + 1))
            pe.wait_ge(sig("stack_k"), 16 * 12 * (L + 1))
            pe.wait_ge(sig("kx_clear"), 2)
            pe.wait_ge(sig("const_late"), 1)
            pe.wait_ge(sig("q_clear"), 1 + L)
            pe.wait_ge(sig("vx_const"), 1)
            pe.wait_ge(sig("vx_ready"), L + 1)
            if L == 1:
                pe.wait_ge(sig("bias_parts"), 1)

            def max_step(b, k):
                n = b * STEPS + k
                if n >= 2 or L:
                    pe.wait_ge(sig("maxed"), L * B * STEPS + max(n - 1, 0))
                o = bank(4 + n % 2)
                if k == STEPS - 1:
                    pe.wait_ge(sig("maxed"), L * B * STEPS + n)
                    ins = pe.transpose(o[0:32, 0:P], mx[:, b % 2, :, :].rearrange("p q h -> p (q h)"), ident[:, :])
                else:
                    q, hp = divmod(k, PAIRS)
                    for i in range(2):
                        h = 2 * hp + i
                        ins = pe.matmul(o[:, i * S:(i + 1) * S], QS[:, h, b * S + q * P:b * S + (q + 1) * P],
                                        KX[:, h, b * S:(b + 1) * S], start=True, stop=True)
                ins.then_inc(sig("max_scores"), 1)

            def scores(u):
                b, hp = divmod(u, PAIRS)
                if hp == 0:
                    pe.wait_ge(sig("max_in%d" % b), 16 * 3 * QT * (L + 1))
                if u >= 2 or L:
                    pe.wait_ge(sig("x_exp"), L * UNITS + max(u - 1, 0))
                for i in range(2):
                    h = 2 * hp + i
                    o = bank(2 * (u % 2) + i)
                    if L == 1:
                        for c in range(3):
                            pe.matmul(o.rearrange("p (k n) -> p k n", k=QT), identb[:, :], BIASK[:, :, c, :],
                                      start=(c == 0), stop=False, skip_group_check=True)
                    for kt in range(QT):
                        ins = pe.matmul(o[:, kt * S:(kt + 1) * S], KX[:, h, b * S + kt * P:b * S + (kt + 1) * P],
                                        QS[:, h, b * S:(b + 1) * S], start=(L == 0), stop=True, skip_group_check=True)
                ins.then_inc(sig("x_scores"), 1)

            def weigh(u):
                b, hp = divmod(u, PAIRS)
                pe.wait_ge(sig("x_exp"), L * UNITS + u + 1)
                o_free(pe, A, u)
                for kt in range(QT):
                    for i in range(2):
                        ins = pe.matmul(o_region(u)[o_rows(u, i), :], VX[:, 2 * b + kt, 2 * hp + i, :],
                                        E[:, u % 3, i, kt * S:(kt + 1) * S], start=(kt == 0), stop=(kt == QT - 1),
                                        skip_group_check=True)
                ins.then_inc(sig("o_full" if u % 4 == 3 else "weighed"), 1)

            for k in range(STEPS):
                max_step(0, k)
            pe.wait_ge(sig("stack_q"), 16 * 9 * (L + 1))
            for u in range(UNITS):
                work = [lambda: scores(u)]
                if u:
                    work.append(lambda: weigh(u - 1))
                for b, k in steps_before(u):
                    max_step(b, k)
                    if work:
                        work.pop(0)()
                for product in work:
                    product()
                output_tensor(pe, A, u)
            weigh(UNITS - 1)
            for u in range(UNITS, LAST):
                output_tensor(pe, A, u)

        def cross_scalar(act, ch, L):
            A = L + 1
            act.wait_ge(sig("qx_psum"), L + 1)
            if L == 0:
                ins = act.activation(EG, two(0), ACT.Copy, scale=DH ** -0.5)
            else:
                act.wait_ge(sig("bq_scaled"), 1)
                ins = act.activation(EG, two(0), ACT.Identity, bias=bqk[:, 2:3], scale=DH ** -0.5)
            ins.then_inc(sig("qx_raw"), 1)
            act.wait_ge(sig("stack_q0"), 16 * 9 * (L + 1))
            act.wait_ge(sig("stack_q"), 16 * 9 * (L + 1))
            act.wait_ge(sig("stack_k"), 16 * 12 * (L + 1))
            for u in range(UNITS):
                act.wait_ge(sig("x_scores"), L * UNITS + u + 1)
                if u >= 3:
                    weighed(act, A, u - 3)
                bk = 2 * (u % 2)
                act.activation(E[:, u % 3, :, :], PS[:, bk:bk + 2, :], ACT.Exp).then_inc(sig("x_exp"), 1)
                if u % 4 == 0 and u:
                    out_evac(act, A, u // 4 - 1, False)
                if at(u, GUESSED[A]) is not None:
                    den_guess(act, ch, A, at(u, GUESSED[A]))
            out_evac(act, A, NZ - 1, False)
            for z in range(NZ):
                if 4 * z + GUESSED[A] >= UNITS:
                    den_guess(act, ch, A, z)

        def cross_vector(dve, ch, L):
            A = L + 1
            if L == 1:
                dve.wait_ge(sig("bqk_in"), 16)
                dve.tensor_scalar(bqk[:, 2:3], bqk[:, 0:1], DH ** -0.5, None, ALU.mult).then_inc(sig("bq_scaled"), 1)
            dve.wait_ge(sig("qx_raw"), L + 1)
            split(dve, ch, QP, EG, R1, "qx_parts")

            def max_step(b, k):
                n = b * STEPS + k
                dve.wait_ge(sig("max_scores"), L * B * STEPS + n + 1)
                o = bank(4 + n % 2)
                if k < STEPS - 1:
                    q, hp = divmod(k, PAIRS)
                    if L == 0:
                        ins = dve.tensor_reduce(mx[:, b % 2, q, 2 * hp:2 * hp + 2],
                                                o.rearrange("p (i n) -> p i n", i=2), AX, ALU.max, negate=True)
                    else:
                        if n >= 2:
                            dve.wait_ge(sig("maxed"), L * B * STEPS + n - 1)
                        for i in range(2):
                            h = 2 * hp + i
                            ins = dve.tensor_tensor_reduce(
                                out=BIASED[:, n % 2, i, :], in0=o[:, i * S:(i + 1) * S], in1=BIASQ[:, q, :],
                                scale=-1.0, scalar=3e38, op0=ALU.add, op1=ALU.min,
                                accum_out=mx[:, b % 2, q, h:h + 1])
                    ins.then_inc(sig("maxed"), 1)
                else:
                    o = o[0:32, 0:P]
                    ch.link(dve.tensor_copy(mxp[:, b, 0, :], o))
                    dve.tensor_tensor(mxr[:, 0, :], o, mxp[:, b, 0, :], ALU.subtract).then_inc(sig("maxed"), 1)
                    dve.wait_ge(sig("maxed"), L * B * STEPS + n + 1)
                    ch.link(dve.tensor_copy(mxp[:, b, 1, :], mxr[:, 0, :]))
                    dve.tensor_tensor(mxp[:, b, 2, :], mxr[:, 0, :], mxp[:, b, 1, :], ALU.subtract)\
                        .then_inc(sig("max_parts"), 1)

            for k in range(STEPS):
                max_step(0, k)
            for u in range(UNITS):
                for b, k in steps_before(u):
                    max_step(b, k)
                output_vector(dve, ch, A, u)
            for u in range(UNITS, LAST):
                output_vector(dve, ch, A, u)

        ZN = VAf[:, 0:T].rearrange("p (j d) -> p j d", j=NT)
        RANK = VAf[:, T:T + NT * NE * NE].rearrange("p (j a b) -> p j a b", j=NT, a=NE)
        SAME = VAf[:, T + 512:T + 1024].rearrange("p (j a b) -> p j a b", j=NT, a=NE)
        LOOPS = 2
        UPS = NE * 4

        def experts_tensor(pe, r):
            pe.wait_ge(sig("xnt"), 2 * (2 + r + 1))
            if r == 0:
                pe.wait_ge(sig("experts_in"), 16 * 3)
            for j in range(NT):
                ins = pe.matmul(bank(7)[:, j * NE:(j + 1) * NE], XNT[:, j * P:(j + 1) * P], router[:, :],
                                start=True, stop=True)
            ins.then_inc(sig("logits"), 1)

            def up(n):
                g = r * UPS + n
                e, half, c = n // 4, n // 2 % 2, n % 2
                if g >= 3:
                    pe.wait_ge(sig("gated"), g - 2)
                for w, o in ((W1, 0), (W3, 1)):
                    ins = pe.matmul(bank(2 * (g % 3) + o), w[:, e, c * P:(c + 1) * P],
                                    XNT[:, half * HALF:(half + 1) * HALF], start=True, stop=True)
                ins.then_inc(sig("up"), 1)

            def down(m):
                g = r * UPS // 2 + m
                pe.wait_ge(sig("gated"), 2 * g + 2)
                if g >= 2:
                    pe.wait_ge(sig("mixed"), g - 1)
                if m == 1:
                    pe.wait_ge(sig("logits_read"), r + 1)
                for j in range(4):
                    for c in range(2):
                        ins = pe.matmul(bank(6 + g % 2)[:, j * P:(j + 1) * P],
                                        E6[:, (2 * g + c) % 4, j * P:(j + 1) * P], W2[:, m // 2, c, :],
                                        start=(c == 0), stop=(c == 1))
                ins.then_inc(sig("down"), 1)

            for n in range(UPS):
                up(n)
                if n >= 2 and n % 2 == 0:
                    down(n // 2 - 1)
            down(UPS // 2 - 1)

        def experts_scalar(act, r):
            act.wait_ge(sig("logits_shifted"), r + 1)
            act.activation(gates[:, :, :], gates[:, :, :], ACT.Exp).then_inc(sig("gate_exp"), 1)
            for n in range(UPS):
                g = r * UPS + n
                act.wait_ge(sig("up"), g + 1)
                if g >= 2:
                    act.wait_ge(sig("gated"), g - 1)
                act.activation(E6[:, 4 + g % 2, :], bank(2 * (g % 3)), ACT.Silu).then_inc(sig("silu"), 1)

        def experts_vector(dve, ch, r):
            dve.wait_ge(sig("logits"), r + 1)
            dve.tensor_copy(logits[:, :, :], bank(7)[:, 0:NT * NE].rearrange("p (j e) -> p j e", j=NT))\
                .then_inc(sig("logits_read"), 1)
            dve.wait_ge(sig("logits_read"), r + 1)
            ch.link(dve.tensor_reduce(tok1[:, :], logits[:, :, :], AX, ALU.max))
            dve.tensor_tensor(gates[:, :, :], logits[:, :, :], tok1[:, :].unsqueeze(2).to_broadcast([P, NT, NE]),
                              ALU.subtract).then_inc(sig("logits_shifted"), 1)
            other = logits[:, :, :].unsqueeze(2).to_broadcast([P, NT, NE, NE])
            own = logits[:, :, :].unsqueeze(3).to_broadcast([P, NT, NE, NE])
            dve.tensor_tensor(RANK, other, own, ALU.is_gt)
            ch.link(dve.tensor_tensor(SAME, other, own, ALU.is_equal))
            ch.link(dve.tensor_tensor(SAME, SAME, tri[:, :, :].unsqueeze(1).to_broadcast([P, NT, NE, NE]), ALU.mult))
            ch.link(dve.tensor_tensor(RANK, RANK, SAME, ALU.add))
            ch.link(dve.tensor_reduce(chosen[:, :, :], RANK, AX, ALU.add))
            ch.link(dve.tensor_scalar(chosen[:, :, :], chosen[:, :, :], 1.5, None, ALU.is_lt))
            dve.wait_ge(sig("gate_exp"), r + 1)
            ch.link(dve.tensor_reduce(tok1[:, :], gates[:, :, :], AX, ALU.add))
            ch.link(dve.reciprocal(tok1[:, :], tok1[:, :]))
            ch.link(dve.tensor_tensor(gates[:, :, :], gates[:, :, :], chosen[:, :, :], ALU.mult))
            ch.link(dve.tensor_tensor(gates[:, :, :], gates[:, :, :],
                                      tok1[:, :].unsqueeze(2).to_broadcast([P, NT, NE]), ALU.mult))
            ch.link(dve.tensor_reduce(tok2[:, :], gates[:, :, :], AX, ALU.add))
            ch.link(dve.tensor_scalar(tok2[:, :], tok2[:, :], 1e-9, None, ALU.add))
            ch.link(dve.reciprocal(tok2[:, :], tok2[:, :]))
            ch.link(dve.tensor_tensor(gates[:, :, :], gates[:, :, :],
                                      tok2[:, :].unsqueeze(2).to_broadcast([P, NT, NE]), ALU.mult))

            def mix(m):
                g = r * UPS // 2 + m
                e, half = divmod(m, 2)
                dve.wait_ge(sig("down"), g + 1)
                if g >= 2:
                    dve.wait_ge(sig("mixed"), g - 1)
                for t in range(4):
                    j = 4 * half + t
                    ins = dve.scalar_tensor_tensor(XN[:, j, :], bank(6 + g % 2)[:, t * P:(t + 1) * P],
                                                   gates[:, j, e:e + 1], XN[:, j, :], ALU.mult, ALU.add)
                ins.then_inc(sig("mixed"), 1)

            for n in range(UPS):
                g = r * UPS + n
                dve.wait_ge(sig("silu"), g + 1)
                if g >= 4:
                    dve.wait_ge(sig("down"), (g - 4) // 2 + 1)
                dve.tensor_tensor(E6[:, g % 4, :], E6[:, 4 + g % 2, :], bank(2 * (g % 3) + 1), ALU.mult)\
                    .then_inc(sig("gated"), 1)
                if n >= 3 and n % 2 == 1:
                    mix((n - 3) // 2)
            mix(UPS // 2 - 1)
            dve.wait_ge(sig("mixed"), (r + 1) * UPS // 2)

        def tiles(ap, n):
            return [ap[:, i * T:(i + 1) * T] for i in range(n)]

        ot, va, ks, ee = tiles(OTf, 4), tiles(VAf, 4), tiles(KSf, 6), \
            tiles(E[:, :, :, :].rearrange("p a b c -> p (a b c)"), 3)
        LOGR, LAN, RR, EN = ot[0:2], ot[2:4], va[0:2], va[2:4]
        BCOL, DXB, SS, HH, HC = ee[0], ks[0:2], ks[2:4], ks[4:6], (ee[1], ee[2])
        DELTA, DX, LA, DTI = SCR[:, 1, :], SCR[:, 2, :], SCR[:, 0, :], SCR[0:DTR, 3, :]
        WW = SCR[:, 3, :]
        BC = KSf[:, 7680:8192].bitcast(BF16)
        BCR, BCM, BCL = ks[2], ks[3][:, 0:HALF].bitcast(BF16), ks[3][:, HALF:T].bitcast(BF16)
        CARRY = XN1

        def scan_tensor(pe):
            pe.wait_ge(sig("ssm_in"), 16 * 5)
            pe.wait_ge(sig("xnt"), 2 * 5)
            project(pe, 0, wssm[:, 0:DTR], XNT, "dti_psum")
            for half in range(2):
                for i in range(4):
                    ins = pe.matmul(bank(4 + half)[32 * i:32 * i + 32, :], wssm[:, DTR:DTR + 2 * NS],
                                    XNT[:, half * HALF:(half + 1) * HALF], start=True, stop=True,
                                    skip_group_check=True)
            ins.then_inc(sig("bc_psum"), 1)
            pe.wait_ge(sig("dti"), 1)
            for half in range(2):
                ins = pe.matmul(bank(2 + half), wdt[:, :], DTI[:, half * HALF:(half + 1) * HALF], start=True, stop=True)
            ins.then_inc(sig("delta_psum"), 1)

            pe.wait_ge(sig("bc_rows"), 1)

            def rows(n):
                if n >= 1:
                    pe.wait_ge(sig("b_read"), n)
                project(pe, 0, select[:, n:n + 1].to_broadcast([P, P]), BC, "b_psum")
                if n == 0:
                    pe.wait_ge(sig("delta"), 1)
                if n >= 2:
                    pe.wait_ge(sig("c_read"), n - 1)
                project(pe, 2 + 2 * (n % 2), select[:, NS + n:NS + n + 1].to_broadcast([P, P]), BC, "c_psum")

            def gather(n):
                pe.wait_ge(sig("c_read"), n + 1)
                for half in range(2):
                    ins = pe.matmul(bank(6 + half), ident[:, :], HC[n % 2][:, half * HALF:(half + 1) * HALF],
                                    start=(n == 0), stop=(n == NS - 1), skip_group_check=True)
                ins.then_inc(sig("summed"), 1)

            for n in range(NS):
                rows(n)
                if n >= 2:
                    gather(n - 2)
            gather(NS - 2)
            gather(NS - 1)
            pe.wait_ge(sig("y_ready"), 1)
            for half in range(2):
                for j in range(4):
                    t = 4 * half + j
                    ins = pe.transpose(bank(half)[:, j * P:(j + 1) * P], LA[:, t * P:(t + 1) * P], ident[:, :])
                ins.then_inc(sig("y_turned"), 1)

        def scan_scalar(act, ch):
            act.wait_ge(sig("stack_k"), 16 * 24)
            act.wait_ge(sig("dti_psum"), 1)
            act.activation(DTI, two(0)[0:DTR, :], ACT.Copy).then_inc(sig("dti"), 1)
            act.wait_ge(sig("ssm_in"), 16 * 5)
            act.activation(amat[:, :], amat[:, :], ACT.Exp).then_inc(sig("a_exp"), 1)
            act.wait_ge(sig("delta_psum"), 1)
            ch.link(act.activation(DX, two(2), ACT.Abs, bias=ssmc[:, 0:1]))
            ch.link(act.activation(DX, DX, ACT.Exp, scale=-1.0))
            act.activation(DX, DX, ACT.Ln, bias=1.0).then_inc(sig("delta_ln"), 1)

            def b_copy(n):
                act.wait_ge(sig("b_psum"), n + 1)
                if n >= 1:
                    act.wait_ge(sig("dxb"), n)
                act.activation(BCOL, two(0), ACT.Copy).then_inc(sig("b_read"), 1)

            b_copy(0)
            for n in range(NS):
                act.wait_ge(sig("logr"), n + 1)
                if n >= 2:
                    act.wait_ge(sig("state"), n - 1)
                act.activation(RR[n % 2], LOGR[n % 2], ACT.Exp).then_inc(sig("rr"), 1)
                if n >= 2:
                    act.wait_ge(sig("input"), n - 1)
                act.activation(EN[n % 2], LOGR[n % 2], ACT.Exp, scale=-1.0).then_inc(sig("en"), 1)
                if n + 1 < NS:
                    b_copy(n + 1)

        def scan_pool(pool):
            def dxb(n):
                pool.wait_ge(sig("b_read"), n + 1)
                if n == 0:
                    pool.wait_ge(sig("dx"), 1)
                if n >= 2:
                    pool.wait_ge(sig("input"), n - 1)
                pool.tensor_tensor(DXB[n % 2], DX, BCOL, ALU.mult).then_inc(sig("dxb"), 1)

            def state(n):
                pool.wait_ge(sig("s_sum"), n + 1)
                pool.wait_ge(sig("rr"), n + 1)
                if n >= 2:
                    pool.wait_ge(sig("c_read"), n - 1)
                pool.tensor_tensor(HH[n % 2], RR[n % 2], SS[n % 2], ALU.mult).then_inc(sig("state"), 1)

            dxb(0)
            dxb(1)
            for n in range(NS):
                state(n)
                if n + 2 < NS:
                    dxb(n + 2)

        def scan_vector(dve, ch):
            dve.wait_ge(sig("stack_k"), 16 * 24)
            dve.wait_ge(sig("turned"), 2 * 5)
            ch.link(dve.memset(XN1, 1.0))
            ch.link(dve.tensor_tensor(select[:, :], identb[:, 0:32], identb[:, 32:64], ALU.add))
            ch.link(dve.tensor_tensor(select[:, :], select[:, :], identb[:, 64:96], ALU.add))
            dve.memset(XN1.rearrange("p (b s) -> p b s", b=B)[:, :, 0:1], 0.0)
            dve.wait_ge(sig("a_exp"), 1)
            dve.memset(ssmc[:, 2:3], LOG_TINY)
            ch.link(dve.tensor_scalar(amat[:, :], amat[:, :], -1.0, None, ALU.mult))
            dve.wait_ge(sig("bc_psum"), 1)
            ch.link(dve.tensor_copy(BC, two(4)))
            ch.link(dve.tensor_tensor(BCR, two(4), BC, ALU.subtract))
            ch.link(dve.tensor_copy(BCM, BCR))
            dve.tensor_copy(BC[32:64, :], BCM[32:64, :])
            ch.link(dve.tensor_tensor(BCL, BCR, BCM, ALU.subtract))
            dve.tensor_copy(BC[64:96, :], BCL[64:96, :]).then_inc(sig("bc_rows"), 1)
            dve.wait_ge(sig("delta_ln"), 1)
            ch.link(dve.tensor_scalar(DELTA, two(2), ssmc[:, 0:1], 0.0, ALU.add, ALU.max))
            dve.tensor_tensor(DELTA, DELTA, DX, ALU.add).then_inc(sig("delta"), 1)
            dve.wait_ge(sig("delta"), 1)
            dve.tensor_tensor(DX, DELTA, XNT[:, :], ALU.mult).then_inc(sig("dx"), 1)

            tiny = ssmc[:, 2:3].to_broadcast([P, S])

            def decay(n):
                ch.link(dve.tensor_scalar(LAN[n % 2], DELTA, amat[:, n:n + 1], -7.0, ALU.mult, ALU.max))
                if n >= 2:
                    dve.wait_ge(sig("rr"), n - 1)
                    dve.wait_ge(sig("en"), n - 1)
                for b in range(B):
                    t = slice(b * S, (b + 1) * S)
                    ins = dve.tensor_tensor_scan(LOGR[n % 2][:, t], LAN[n % 2][:, t], tiny, 0.0, ALU.add, ALU.max)
                ins.then_inc(sig("logr"), 1)

            def accumulate(n):
                dve.wait_ge(sig("en"), n + 1)
                dve.wait_ge(sig("dxb"), n + 1)
                if n:
                    dve.wait_ge(sig("s_sum"), n)
                dve.scalar_tensor_tensor(WW, EN[n % 2], CLAMP_EXP, DXB[n % 2], ALU.min, ALU.mult)\
                    .then_inc(sig("input"), 1)
                dve.wait_ge(sig("input"), n + 1)
                if n >= 2:
                    dve.wait_ge(sig("state"), n - 1)
                dve.tensor_tensor_scan(SS[n % 2], CARRY, WW, 0.0, ALU.mult, ALU.add).then_inc(sig("s_sum"), 1)

            def output(n):
                dve.wait_ge(sig("state"), n + 1)
                dve.wait_ge(sig("c_psum"), n + 1)
                if n >= 2:
                    dve.wait_ge(sig("summed"), n - 1)
                dve.tensor_tensor(HC[n % 2], HH[n % 2], two(2 + 2 * (n % 2)), ALU.mult).then_inc(sig("c_read"), 1)

            decay(0)
            for n in range(NS):
                if n + 1 < NS:
                    decay(n + 1)
                accumulate(n)
                if n:
                    output(n - 1)
            output(NS - 1)
            dve.wait_ge(sig("summed"), NS)
            dve.scalar_tensor_tensor(LA, XNT[:, :], ssmc[:, 1:2], two(6), ALU.mult, ALU.add).then_inc(sig("y_ready"), 1)
            for half in range(2):
                dve.wait_ge(sig("y_turned"), half + 1)
                x = X[:, 4 * half:4 * half + 4, :].rearrange("p j d -> p (j d)")
                ins = dve.tensor_tensor(x, x, bank(half), ALU.add)
            ins.then_inc(sig("x_res"), 1)

        HB = OTf.rearrange("p (j f) -> p j f", j=NT)
        GG = VAf.rearrange("p (j f) -> p j f", j=NT)
        ROUNDED = SCR[:, 0, :]
        QB = SCR[:, 1, 0:T // 2].bitcast(BF16)
        QTB = SCR[:, 1, T // 2:T].bitcast(BF16)
        GQ = SCR[:, 2, 0:T // 2].bitcast(BF16).rearrange("p (s f) -> p s f", s=2)
        GQT = SCR[:, 2, T // 2:T].bitcast(BF16).rearrange("p (s f) -> p s f", s=2)
        SQ = SCR[:, 3, 0:HALF]

        def halfbank(i):
            return bank(i).bitcast(BF16)

        def feed_vector_weights(dve, ch):
            dve.wait_ge(sig("ffn_in"), 16 * 2)
            ch.link(dve.tensor_reduce(wsum[:, :], wraw[:, :, :], AX, ALU.add, apply_absolute_value=True))
            dve.tensor_copy(wscale[:, :], wsum[:, :]).then_inc(sig("w_sums"), 1)
            dve.wait_ge(sig("w_total"), 1)
            ch.link(dve.tensor_scalar(wmean[:, :], bank(6)[:, 0:2], 1.0 / (FF * D), 1e-5, ALU.mult, ALU.max))
            ch.link(dve.reciprocal(wscale[:, :], wmean[:, :]))
            for w, dst in ((0, wq1[:, :]), (1, wq2[:, :, :].rearrange("p c d -> p (c d)"))):
                raw = wraw[:, w, :]
                ch.link(dve.tensor_scalar(raw, raw, wscale[:, w:w + 1], ROUND, ALU.mult, ALU.add))
                ch.link(dve.tensor_scalar(raw, raw, -ROUND, 1.0, ALU.add, ALU.min))
                dve.tensor_scalar(dst, raw, -1.0, None, ALU.max).then_inc(sig("w_quantised"), 1)

        def quant_factors(dve, ch, w):
            ch.link(dve.tensor_tensor(peak, peak, rstd[:, :], ALU.mult))
            ch.link(dve.tensor_scalar(peak, peak, 1e-5, None, ALU.max))
            ch.link(dve.reciprocal(fac, peak))
            dve.tensor_scalar(deq, peak, 1.0 / 127.0, wmean[:, w:w + 1], ALU.mult, ALU.mult)
            ch.link(dve.scalar_tensor_tensor(fac, fac, 127.0, rstd[:, :], ALU.mult, ALU.mult))

        def feed_vector(dve, ch):
            dve.wait_ge(sig("xn"), 2 * 7)
            norm_stats(dve, ch, XN, 8, 1e-5, mean_square=True)
            ch.link(dve.tensor_reduce(peak, XN[:, :, :], AX, ALU.max, apply_absolute_value=True))
            norm_refine(dve, ch, 8)
            quant_factors(dve, ch, 0)
            for j in range(NT):
                ins = dve.tensor_scalar(ROUNDED[:, j * P:(j + 1) * P], XN[:, j, :], fac[:, j:j + 1], ROUND,
                                        ALU.mult, ALU.add)
            ch.link(ins)
            dve.tensor_scalar(QB, ROUNDED, -ROUND, 127.0, ALU.add, ALU.min).then_inc(sig("q1"), 1)
            for j in range(NT):
                dve.wait_ge(sig("h1"), j + 1)
                dve.scalar_tensor_tensor(HB[:, j, :], bank(1 + j % 2), deq[:, j:j + 1], b1bc, ALU.mult, ALU.add)\
                    .then_inc(sig("h1_read"), 1)
                if j:
                    dve.wait_ge(sig("gelu"), j)
                    dve.tensor_reduce(peak[:, j - 1:j], GG[:, j - 1, :], AX, ALU.max, apply_absolute_value=True)
            dve.wait_ge(sig("gelu"), NT)
            ch.link(dve.tensor_reduce(peak[:, NT - 1:NT], GG[:, NT - 1, :], AX, ALU.max, apply_absolute_value=True))
            dve.wait_ge(sig("sumsq"), 1)
            dve.tensor_scalar(ve[:, :], sumsq, 1.0 / FF, 1e-5, ALU.mult, ALU.add).then_inc(sig("ve"), 1)
            norm_refine(dve, ch, 9)
            quant_factors(dve, ch, 1)
            b2 = b2bc.unsqueeze(1).to_broadcast([P, NT, D])
            ch.link(dve.tensor_tensor(X[:, :, :], X[:, :, :], b2, ALU.add))

            def finish(j):
                dve.wait_ge(sig("h2"), j + 1)
                dve.scalar_tensor_tensor(X[:, j, :], bank(6 + j % 2)[:, 0:D], deq[:, j:j + 1], X[:, j, :],
                                         ALU.mult, ALU.add).then_inc(sig("x_tile"), 1)

            for j in range(NT):
                ch.link(dve.tensor_scalar(HB[:, j, :], GG[:, j, :], fac[:, j:j + 1], ROUND, ALU.mult, ALU.add))
                if j >= 2:
                    dve.wait_ge(sig("g_turned"), j - 1)
                dve.tensor_scalar(GQ[:, j % 2, :], HB[:, j, :], -ROUND, 127.0, ALU.add, ALU.min)\
                    .then_inc(sig("q2"), 1)
                if j >= 2:
                    finish(j - 2)
            finish(NT - 2)
            finish(NT - 1)

        def feed_tensor(pe):
            pe.wait_ge(sig("q1"), 1)
            for j in range(NT):
                ins = pe.transpose(halfbank(3)[:, j * P:(j + 1) * P], QB[:, j * P:(j + 1) * P], identb[:, :])
            ins.then_inc(sig("q_turned"), 1)
            pe.wait_ge(sig("qt1"), 1)
            for j in range(NT):
                if j >= 2:
                    pe.wait_ge(sig("h1_read"), j - 1)
                pe.matmul(bank(1 + j % 2), QTB[:, j * P:(j + 1) * P], wq1[:, :], start=True, stop=True)\
                    .then_inc(sig("h1"), 1)

            def second(j):
                pe.wait_ge(sig("gt"), j + 1)
                if j >= 2:
                    pe.wait_ge(sig("x_tile"), j - 1)
                for c in range(FF // P):
                    ins = pe.matmul(bank(6 + j % 2)[:, 0:D], GQT[:, j % 2, c * P:(c + 1) * P], wq2[:, c, :],
                                    start=(c == 0), stop=(c == FF // P - 1))
                ins.then_inc(sig("h2"), 1)

            for j in range(NT):
                pe.wait_ge(sig("q2"), j + 1)
                if j >= 2:
                    pe.wait_ge(sig("gt"), j - 1)
                for c in range(FF // P):
                    ins = pe.transpose(halfbank(4 + j % 2)[:, c * P:(c + 1) * P], GQ[:, j % 2, c * P:(c + 1) * P],
                                       identb[:, :])
                ins.then_inc(sig("g_turned"), 1)
                if j:
                    second(j - 1)
            second(NT - 1)

        def feed_scalar(act, ch):
            norm_root(act, ch, 8)
            act.wait_ge(sig("q_turned"), 1)
            act.activation(QTB, halfbank(3)[:, 0:T], ACT.Copy).then_inc(sig("qt1"), 1)
            for j in range(NT):
                act.wait_ge(sig("h1_read"), j + 1)
                act.activation(GG[:, j, :], HB[:, j, :], ACT.Gelu).then_inc(sig("gelu"), 1)
                act.wait_ge(sig("gelu"), j + 1)
                ins = act.activation(SQ, GG[:, j, :], ACT.Square, accum_out=sumsq[:, j:j + 1])
            ins.then_inc(sig("sumsq"), 1)
            norm_root(act, ch, 9)
            for j in range(NT):
                act.wait_ge(sig("g_turned"), j + 1)
                if j >= 2:
                    act.wait_ge(sig("h2"), j - 1)
                act.activation(GQT[:, j % 2, :], halfbank(4 + j % 2)[:, 0:FF], ACT.Copy).then_inc(sig("gt"), 1)

        @block.sync
        def _(sp):
            def load(dst, src, signal):
                sp.dma_start(dst, src).then_inc(sig(signal), 16)

            load(X[:, :, :], inp["x"].rearrange("(j p) d -> p j d", p=P), "x_in")
            load(CT, inp["ctxT"], "ctx_in")
            load(wx[:, :, :, :], inp["w_x"].rearrange("l w p d -> p l w d"), "wx_in")
            load(wself[:, :, :], inp["w_self"].rearrange("w p d -> p w d"), "wself_in")
            load(bg[:, 0:1], inp["bg"].rearrange("(p o) -> p o", o=1), "bg_in")
            load(lens[:, :], inp["lens"].partition_broadcast(P), "lens_in")
            load(wox[:, :, :, :], inp["w_out"].rearrange("l g p d -> p l g d"), "wox_in")
            load(router[:, :], inp["router"], "router_in")
            load(normw[:, :], inp["normw"].rearrange("(p o) -> p o", o=1), "router_in")
            load(bqk[:, 0:2], inp["bqk"], "bqk_in")
            load(brow[0:1, :], inp["bv"].rearrange("(o d) -> o d", o=1), "brow_in")
            load(wssm[:, :], inp["w_ssm"], "ssm_in")
            load(wdt[:, :], inp["w_dt"], "ssm_in")
            load(ssmc[:, 0:1], inp["b_dt"].rearrange("(p o) -> p o", o=1), "ssm_in")
            load(ssmc[:, 1:2], inp["Dskip"].rearrange("(p o) -> p o", o=1), "ssm_in")
            load(amat[:, :], inp["A_log"], "ssm_in")
            for parts, stack, ready in ((KP, KSA, "ka_parts"), (QP, QS, "qa_parts")):
                sp.wait_ge(sig(ready), 1)
                sp.wait_ge(sig("q_clear" if stack is QS else "ka_clear"), 1)
                for a in range(3):
                    for b in range(3):
                        r = 24 * a + 8 * b
                        part = a if stack is QS else b
                        sp.dma_start(stack[r:r + 8, :, :], parts[:, part, :]).then_inc(sig("stack_a"), 16)

            stack_context(sp, 0)

            def cross_sync(L):
                sp.wait_ge(sig("qx_parts"), L + 1)
                for t in (slice(0, S), slice(S, T)):
                    for a in range(3):
                        for b in range(3):
                            r = 24 * a + 8 * b
                            sp.dma_start(QS[r:r + 8, :, t], QP[:, a, t])\
                                .then_inc(sig("stack_q" if t.start else "stack_q0"), 16)
                for b in range(B):
                    sp.wait_ge(sig("max_parts"), L * B + b + 1)
                    for c in range(3):
                        for q in range(QT):
                            t0 = b * S + q * P
                            sp.dma_start(QS[MAX_ROW + c:MAX_ROW + c + 1, :, t0:t0 + P],
                                         mxp[16 * q:16 * q + 16, b, c, :]).then_inc(sig("max_in%d" % b), 16)

            if last_stage >= 2:
                cross_sync(0)
            if last_stage >= 3:
                load(KSf[:, 0:2048], inp["w1"].rearrange("e p f -> p e f"), "experts_in")
                load(KSf[:, 2048:4096], inp["w3"].rearrange("e p f -> p e f"), "experts_in")
                load(W2, inp["w2"].rearrange("e (c p) d -> p e c d", p=P), "experts_in")
                load(wraw[:, 0, :], inp["w1T"], "ffn_in")
                load(wraw[:, 1, :].rearrange("p (c d) -> p c d", c=FF // P),
                     inp["w2T"].rearrange("(c p) d -> p c d", p=P), "ffn_in")
                x_ready(sp, 2)
                load(CT, inp["ctxT"], "ctx_in")
                load(PAD, inp["pad"].partition_broadcast(P), "pad_in")
                load(FRAW, inp["fside"].rearrange("w p n -> p w n"), "fside_in")
            if last_stage >= 4:
                stack_context(sp, 1)
            if last_stage >= 5:
                x_ready(sp, 4)
                load(b1bc, inp["b1"].partition_broadcast(P), "bias_in")
                load(b2bc, inp["b2"].partition_broadcast(P), "bias_in")
                load(bobc, inp["bo"].partition_broadcast(P), "bias_in")
                cross_sync(1)
            if last_stage == 6:
                for j in range(NT):
                    sp.wait_ge(sig("x_tile"), j + 1)
                    sp.dma_start(out[j * P:(j + 1) * P, :], X[:, j, :]).then_inc(sig("stored"), 16)
                sp.wait_ge(sig("stored"), 16 * NT)
            else:
                x_ready(sp, last_stage)
                sp.dma_start(out.rearrange("(j p) d -> p j d", p=P), X[:, :, :]).then_inc(sig("stored"), 16)
                sp.wait_ge(sig("stored"), 16)

        @block.gpsimd
        def _(pool):
            ch = Chain(pool, "pool_step")
            ch.link(pool.memset(ident[:, :], 0.0))
            pool.affine_select(out=ident[:, :], in_=ident[:, :], compare_op=ALU.not_equal, fill=1.0,
                               base=0, pattern=[[-1, P]], channel_multiplier=1).then_inc(sig("ident"), 1)
            pool.memset(spread[:, :], 0.0)
            ch.link(pool.memset(masks[:, :, :], 1.0))
            heads = spread[:, :].rearrange("p (i e) -> p i e", i=HG)
            pool.affine_select(out=heads, in_=heads, compare_op=ALU.not_equal, fill=1.0, base=-DH,
                               pattern=[[-32, HG], [0, 32]], channel_multiplier=1)
            causal = masks[:, 0:3:2, :]
            pool.affine_select(out=causal, in_=causal, compare_op=ALU.is_ge, fill=0.0,
                               base=0, pattern=[[0, 2], [1, P]], channel_multiplier=-1).then_inc(sig("const"), 1)
            pool.wait_ge(sig("const"), 1)
            pool.memset(KSf[64:128, :], 0.0).then_inc(sig("ka_clear"), 1)
            pool.wait_ge(sig("ka_clear"), 1)
            pool.memset(QSf[64:96, :], ONES_PAIR).then_inc(sig("q_clear"), 1)
            pool.wait_ge(sig("q_clear"), 1)
            pool.memset(KXf[64:96, :], 0.0).then_inc(sig("kx_clear"), 1)
            pool.wait_ge(sig("kx_clear"), 1)
            pool.memset(VA[:, :, :, DH + 1:32], 0.0)
            pool.memset(VA[:, :, :, DH:DH + 1], 1.0).then_inc(sig("va_const"), 1)
            pool.wait_ge(sig("lens_in"), 16)
            pool.tensor_scalar(lensf[:, :], lens[:, :], 1.0, 0.0, ALU.mult, ALU.add)
            ch.link(pool.iota(iota, pattern=[[1, S]], base=0, channel_multiplier=0))
            ch.link(pool.tensor_scalar(iotaf, iota, 1.0, 0.0, ALU.mult, ALU.add))
            context_keys_pool(pool, ch, 0, NEG_X0)
            pool.wait_ge(sig("neg_parts"), 1)
            ch.link(pool.memset(KXf[96:128, :], ONES_PAIR))
            pool.memset(VX[:, :, :, DH + 1:32], 0.0).then_inc(sig("kx_clear"), 1)
            pool.memset(VX[:, :, :, DH:DH + 1], 1.0).then_inc(sig("vx_const"), 1)
            pool.tensor_scalar(identb[:, :], ident[:, :], 1.0, 0.0, ALU.mult, ALU.add)
            ch.link(pool.memset(tri[:, :, :], 1.0))
            pool.affine_select(out=tri[:, :, :], in_=tri[:, :, :], compare_op=ALU.is_ge, fill=0.0,
                               base=-1, pattern=[[1, NE], [-1, NE]], channel_multiplier=0)\
                .then_inc(sig("const_late"), 1)
            if last_stage >= 4:
                x_ready(pool, 2)
                pool.memset(QSf[96:128, :], 0.0).then_inc(sig("q_clear"), 1)
                pool.wait_ge(sig("q_clear"), 2)
                pool.wait_ge(sig("fside_in"), 16)
                pool.wait_ge(sig("w_quantised"), 2)
                pool.tensor_scalar(BIASQ, FRAW[:, 0:QT, :], 1.0, 0.0, ALU.mult, ALU.add)
                ch.link(pool.tensor_scalar(BIASK[:, :, 0, :], FRAW[:, QT:, :], 1.0, 0.0, ALU.mult, ALU.add))
                rest = KXR[:, 0:QT * S].rearrange("p (w n) -> p w n", w=QT)
                ch.link(pool.tensor_tensor(rest, FRAW[:, QT:, :], BIASK[:, :, 0, :], ALU.subtract))
                ch.link(pool.tensor_scalar(BIASK[:, :, 1, :], rest, 1.0, 0.0, ALU.mult, ALU.add))
                pool.tensor_tensor(BIASK[:, :, 2, :], rest, BIASK[:, :, 1, :], ALU.subtract)\
                    .then_inc(sig("bias_parts"), 1)
                pool.wait_ge(sig("bias_parts"), 1)
                context_keys_pool(pool, ch, 1, NEG_X1)
                pool.wait_ge(sig("stack_k"), 16 * 24)
                scan_pool(pool)

        @block.tensor
        def _(pe):
            context_tensor(pe, 0)
            norm_turn(pe, XN, 0)
            self_tensor(pe)
            if last_stage >= 2:
                norm_turn(pe, XN, 1)
                cross_tensor(pe, 0)
            if last_stage >= 3:
                norm_turn(pe, ZN, 2)
                experts_tensor(pe, 0)
                pe.wait_ge(sig("gated"), UPS)
                context_tensor(pe, 1)
                pe.wait_ge(sig("mixed"), UPS // 2)
                pe.wait_ge(sig("w_sums"), 1)
                pe.matmul(bank(6)[:, 0:2], onesf, wscale[:, :], start=True, stop=True).then_inc(sig("w_total"), 1)
                norm_turn(pe, ZN, 3)
                pe.wait_ge(sig("vx_ready"), 2)
                experts_tensor(pe, 1)
            if last_stage >= 4:
                norm_turn(pe, XN, 4)
                scan_tensor(pe)
            if last_stage >= 5:
                norm_turn(pe, XN, 5)
                cross_tensor(pe, 1)
            if last_stage >= 6:
                feed_tensor(pe)

        @block.scalar
        def _(act):
            ch = Chain(act, "act_step")
            exp_and_ln(act)
            norm_root(act, ch, 0)
            context_scalar(act, 0)
            norm_take(act, 0)
            self_scalar(act, ch)
            if last_stage >= 2:
                norm_root(act, ch, 1)
                norm_take(act, 1)
                cross_scalar(act, ch, 0)
            if last_stage >= 3:
                norm_root(act, ch, 2)
                act.wait_ge(sig("router_in"), 32)
                for r in range(LOOPS):
                    norm_root(act, ch, 3 + r)
                    norm_take(act, 2 + r, normw[:, 0:1])
                    experts_scalar(act, r)
                    exp_and_ln(act)
                    if r == 0:
                        context_scalar(act, 1)
            if last_stage >= 4:
                norm_root(act, ch, 5)
                norm_take(act, 4)
                scan_scalar(act, ch)
            if last_stage >= 5:
                norm_root(act, ch, 6)
                norm_take(act, 5)
                cross_scalar(act, ch, 1)
            if last_stage >= 6:
                norm_root(act, ch, 7)
                feed_scalar(act, ch)

        @block.vector
        def _(dve):
            ch = Chain(dve, "dve_step")
            dve.wait_ge(sig("x_in"), 16)

            def layer_norm(k):
                norm_stats(dve, ch, X if k in (0, 5, 6) else None, k, 1e-5)
                norm_refine(dve, ch, k)

            layer_norm(0)
            norm_apply(dve, XN, X)
            self_vector(dve, ch)
            if last_stage >= 2:
                dve.wait_ge(sig("const_late"), 1)
                x_ready(dve, 1)
                layer_norm(1)
                norm_apply(dve, XN, X)
                cross_vector(dve, ch, 0)
            if last_stage >= 3:
                x_ready(dve, 2)
                layer_norm(2)
                for j in range(NT):
                    ins = dve.tensor_scalar(XN[:, j, :], X[:, j, :], mv[:, j, 0:1], rstd[:, j:j + 1],
                                            ALU.subtract, ALU.mult)
                ch.link(ins)
                for r in range(LOOPS):
                    norm_stats(dve, ch, XN, 3 + r, 1e-6, mean_square=True)
                    norm_refine(dve, ch, 3 + r)
                    for j in range(NT):
                        ins = dve.tensor_scalar(ZN[:, j, :], XN[:, j, :], rstd[:, j:j + 1], None, ALU.mult)
                        if j % 4 == 3:
                            ins.then_inc(sig("xn"), 1)
                    experts_vector(dve, ch, r)
                    if r == 0:
                        feed_vector_weights(dve, ch)
                x = X[:, :, :].rearrange("p j d -> p (j d)")
                dve.tensor_tensor(x, x, XN1, ALU.add).then_inc(sig("x_res"), 1)
            if last_stage >= 4:
                x_ready(dve, 3)
                layer_norm(5)
                norm_apply(dve, XN, X)
                scan_vector(dve, ch)
            if last_stage >= 5:
                x_ready(dve, 4)
                layer_norm(6)
                norm_apply(dve, XN, X)
                dve.wait_ge(sig("xn"), 2 * 6)
                dve.wait_ge(sig("bias_in"), 16 * 3)
                ch.link(dve.tensor_tensor(X[:, :, :], X[:, :, :], bobc.unsqueeze(1).to_broadcast([P, NT, D]), ALU.add))
                cross_vector(dve, ch, 1)
            if last_stage >= 6:
                x_ready(dve, 5)
                layer_norm(7)
                norm_apply(dve, XN, X)
                feed_vector(dve, ch)


def kernel(**inputs):
    import numpy as np
    import concourse.bacc as bacc
    from concourse import mybir as mb
    from concourse.bass_utils import run_bass_kernel_spmd

    a = {k: np.asarray(v) for k, v in inputs.items()}

    def by_feature(w):
        return w.reshape(H, DH, D).transpose(2, 1, 0).reshape(D, D)

    def padded(w):
        full = np.zeros((NG, HG, 32, D), w.dtype)
        full[:, :, 0:DH] = w.T.reshape(NG, HG, DH, D)
        return full.reshape(NG, P, D)

    arrays = {
        "x": a["x"].reshape(T, D),
        "ctxT": a["ctx_1024"].reshape(T, D).T,
        "w_self": np.stack([by_feature(a["L0_attn_Wq"]), by_feature(a["L0_attn_Wk"]), by_feature(a["L0_attn_Wg"]),
                            a["L0_attn_Wv"].T]),
        "bg": a["L0_attn_bg"].reshape(H, DH).T.reshape(D),
        "w_x": np.stack([np.stack([by_feature(a["L0_xattn_W_q"]), by_feature(a["L0_xattn_W_k"]), a["L0_xattn_W_v"].T]),
                         np.stack([by_feature(a["L1_xattn_Wq"]), by_feature(a["L1_xattn_Wk"]), a["L1_xattn_Wv"].T])]),
        "w_out": np.stack([padded(a["L0_attn_Wo"]), padded(a["L0_xattn_W_o"]), padded(a["L1_xattn_Wo"])]),
        "lens": a["mask_B_ik0"],
        "pad": a["mask_BxS2_bk0"].reshape(T),
        "fside": np.concatenate([a["fside_SxS2_0"].reshape(QT, P, S), a["fside_SxS2_0"].T.reshape(QT, P, S)]),
        "bqk": np.stack([a["L1_xattn_bq"].reshape(H, DH).T.reshape(D), a["L1_xattn_bk"].reshape(H, DH).T.reshape(D)], 1),
        "bv": a["L1_xattn_bv"], "bo": a["L1_xattn_bo"],
        "router": a["L0_ffn_router_w"],
        "normw": a["L0_ffn_norm_w"],
        "w1": a["L0_ffn_w1"], "w3": a["L0_ffn_w3"], "w2": a["L0_ffn_w2"],
        "w_ssm": a["L1_attn_W_xproj"], "w_dt": a["L1_attn_W_dt"], "b_dt": a["L1_attn_b_dt"],
        "Dskip": a["L1_attn_D"], "A_log": a["L1_attn_A_log"],
        "w1T": a["L1_ffn_w1"].T, "w2T": a["L1_ffn_w2"].T, "b1": a["L1_ffn_b1"], "b2": a["L1_ffn_b2"],
    }
    nc = bacc.Bacc("TRN2", target_bir_lowering=False, num_devices=1)
    arrays = {k: np.ascontiguousarray(v) for k, v in arrays.items()}
    inp = {k: nc.dram_tensor("in_" + k, v.shape, mb.dt.from_np(v.dtype), kind="ExternalInput").ap()
           for k, v in arrays.items()}
    out = nc.dram_tensor("out_x", (T, D), mb.dt.float32, kind="ExternalOutput").ap()
    build(nc, inp, out)
    r = run_bass_kernel_spmd(nc, [{"in_" + k: v for k, v in arrays.items()}], core_ids=[0])
    return r.results[0]["out_x"].reshape(B, S, D)
```

```python
from contextlib import ExitStack

import numpy as np

import concourse.bass as bass
from concourse import mybir

F32 = mybir.dt.float32
BF16 = mybir.dt.bfloat16
I32 = mybir.dt.int32
U8 = mybir.dt.uint8
ALU = mybir.AluOpType
ACT = mybir.ActivationFunctionType
AX = mybir.AxisListType.X

P = 128
B, S, D = 4, 256, 128
T = B * S
NT = T // P
QT = S // P
H = 16
DH = D // H
HG = 4
NG = H // HG
NE, FE = 8, 256
NS = 16
DTR = 64
FF = 512
HALF = 512
PAIRS = H // 2
UNITS = B * PAIRS
ONES_PAIR = 1.0019378662109375
ROUND = 12582912.0
CLAMP_EXP = 485165195.40979
LOG_TINY = -87.3
NEG_X0 = 1.0e6
NEG_X1 = 1.0e30
MAX_ROW = 96
NEG_ROW = 72


def bf16_parts(v):
    parts = []
    for _ in range(3):
        bits = int(np.float32(v).view(np.uint32))
        bits = (bits + 0x7FFF + ((bits >> 16) & 1)) & 0xFFFF0000
        part = float(np.uint32(bits).view(np.float32))
        parts.append(part)
        v = v - part
    return parts


def build(nc, inp, out):
    ctx = ExitStack()
    with ctx:
        def sb(name, shape, dt=F32):
            return ctx.enter_context(nc.sbuf_tensor(name, shape, dt))

        signals = {}

        def sig(name):
            if name not in signals:
                signals[name] = ctx.enter_context(nc.semaphore(name))
            return signals[name]

        PS = ctx.enter_context(nc.psum_tensor("PS", [P, 8, HALF], F32))

        X = sb("X", [P, NT, D])
        XN = sb("XN", [P, NT, D])
        XNT = sb("XNT", [P, T])
        QS = sb("QS", [P, H, T], BF16)
        KSA = sb("KSA", [P, H, T], BF16)
        KX = sb("KX", [P, H, T], BF16)
        VA = sb("VA", [P, NT, H, 32])
        VX = sb("VX", [P, NT, H, 32])
        SCR = sb("SCR", [P, 4, T])
        OT = sb("OT", [P, NG, T])
        E = sb("E", [P, 3, 2, HALF])
        wself = sb("wself", [P, 4, D])
        wox = sb("wox", [P, 3, NG, D])
        wx = sb("wx", [P, 2, 3, D])
        ident = sb("ident", [P, P])
        identb = sb("identb", [P, P], BF16)
        masks = sb("masks", [P, 3, P])
        spread = sb("spread", [P, P])
        onesf = masks[:, 1, :]
        den_eps = sb("den_eps", [P, 1])
        bg = sb("bg", [P, 2])
        bqk = sb("bqk", [P, 3])
        brow = sb("brow", [1, D])
        st = sb("st", [P, NT, 6])
        mv = sb("mv", [P, NT, 2])
        ve = sb("ve", [P, NT])
        lnv = sb("lnv", [P, NT])
        rs = sb("rs", [P, NT])
        rt = sb("rt", [P, NT])
        rstd = sb("rstd", [P, NT])
        lens = sb("lens", [P, B], I32)
        lensf = sb("lensf", [P, B])
        mx = sb("mx", [P, 2, QT, H])
        mx_rest = sb("mx_rest", [P, QT, H])
        mx_parts = sb("mx_parts", [P, 2, QT, 3, H], BF16)
        mx_rows = sb("mx_rows", [3 * H, B, S], BF16)

        EF = E[:, :, :, :].rearrange("p a b c -> p (a b c)").bitcast(BF16)
        QP = [EF[:, a * T:(a + 1) * T] for a in range(3)]
        KP = [EF[:, (3 + a) * T:(4 + a) * T] for a in range(3)]
        OTf = OT[:, :, :].rearrange("p g t -> p (g t)")
        KXP = OTf[:, 0:3 * T // 2].bitcast(BF16).rearrange("p (a t) -> p a t", a=3)
        KX32 = OTf[:, 3 * T // 2:5 * T // 2]
        KXR = OTf[:, 5 * T // 2:7 * T // 2]
        NEGP = OTf[:, 3 * T // 2:3 * T].bitcast(BF16).rearrange("p (a t) -> p a t", a=3)
        iota = OTf[:, 7 * T // 2:7 * T // 2 + S].bitcast(I32)
        iotaf = OTf[:, 7 * T // 2 + S:4 * T]
        VMASK = SCR[:, 2, :]
        CT = SCR[:, 3, :]
        KSf = KSA[:, :, :].rearrange("p h t -> p (h t)").bitcast(F32)
        W1 = KSf[:, 0:2048].rearrange("p (e f) -> p e f", e=NE)
        W3 = KSf[:, 2048:4096].rearrange("p (e f) -> p e f", e=NE)
        W2 = KSf[:, 4096:6144].rearrange("p (e c d) -> p e c d", e=NE, c=2)
        BIASQ = KSf[:, 6144:6144 + QT * S].rearrange("p (q n) -> p q n", q=QT)
        BIASK = KSf[:, 6144 + QT * S:6144 + QT * S + 3 * QT * S // 2].bitcast(BF16)\
            .rearrange("p (k c n) -> p k c n", k=QT, c=3)
        VAf = VA[:, :, :, :].rearrange("p a b c -> p (a b c)")
        XN1 = XN[:, :, :].rearrange("p j d -> p (j d)")
        XNh = XN1.bitcast(BF16)
        QPA = [XNh[:, 0:T], XNh[:, T:2 * T], XNT[:, 0:T // 2].bitcast(BF16)]
        E6 = E[:, :, :, :].rearrange("p a b c -> p (a b) c")
        PAD = SCR[:, 0, 0:T // 4].bitcast(U8)
        FRAW = SCR[:, 1, :].rearrange("p (w n) -> p w n", w=4)
        BIASED = SCR[:, 2, :].rearrange("p (s i n) -> p s i n", s=2, i=2)
        KXf = KX[:, :, :].rearrange("p h t -> p (h t)").bitcast(F32)
        QSf = QS[:, :, :].rearrange("p h t -> p (h t)").bitcast(F32)

        router = sb("router", [P, NE])
        normw = sb("normw", [P, 1])
        tri = sb("tri", [P, NE, NE])
        logits = sb("logits", [P, NT, NE])
        gates = sb("gates", [P, NT, NE])
        chosen = sb("chosen", [P, NT, NE])
        tok1 = sb("tok1", [P, NT])
        tok2 = sb("tok2", [P, NT])
        select = sb("select", [P, 2 * NS], BF16)
        wssm = sb("wssm", [P, DTR + 2 * NS])
        wdt = sb("wdt", [DTR, P])
        ssmc = sb("ssmc", [P, 3])
        amat = sb("amat", [P, NS])
        wraw = KSf[:, 6144:6144 + 2 * FF].rearrange("p (w f) -> p w f", w=2)
        wq1 = sb("wq1", [P, FF], BF16)
        wq2 = sb("wq2", [P, FF // P, D], BF16)
        b1bc = KSf[:, 0:FF]
        b2bc = KSf[:, FF:FF + D]
        bobc = KSf[:, FF + D:FF + 2 * D]
        BIASF = KSf[:, 2 * FF:2 * FF + QT * S]
        wsum = sb("wsum", [P, 2])
        wmean = sb("wmean", [P, 2])
        wscale = sb("wscale", [P, 2])
        peak, fac, deq, sumsq = (logits[:, i, :] for i in range(4))

        block = ctx.enter_context(nc.Block())

        def bank(i):
            return PS[:, i, :]

        def halfbank(i):
            return bank(i).bitcast(BF16)

        class Chain:
            def __init__(self, eng, name):
                self.eng, self.sem, self.n = eng, sig(name), 0

            def link(self, ins):
                ins.then_inc(self.sem, 1)
                self.n += 1
                self.eng.wait_ge(self.sem, self.n)

            def mark(self, ins):
                ins.then_inc(self.sem, 1)
                self.n += 1

            def wait(self):
                self.eng.wait_ge(self.sem, self.n)

        def norm_stats(dve, ch, src, k, eps, mean_square=False):
            if src is not None:
                for j in range(NT):
                    ins = dve.bn_stats(st[:, j, :], src[:, j, :])
                ch.link(ins)
            for j in range(NT):
                ins = dve.bn_aggr(mv[:, j, :], st[:, j, :])
            ch.link(ins)
            if mean_square:
                ch.link(dve.tensor_tensor(rt[:, :], mv[:, :, 0], mv[:, :, 0], ALU.mult))
                ch.link(dve.tensor_tensor(ve[:, :], rt[:, :], mv[:, :, 1], ALU.add))
                dve.tensor_scalar(ve[:, :], ve[:, :], eps, None, ALU.add).then_inc(sig("ve"), 1)
            else:
                dve.tensor_scalar(ve[:, :], mv[:, :, 1], eps, None, ALU.add).then_inc(sig("ve"), 1)

        def exp_and_ln(act):
            act.preload_act_table_set("natural_log_exp_and_others")

        def norm_root(act, ch, k, s=slice(0, NT)):
            act.wait_ge(sig("ve"), k + 1)
            ch.link(act.activation(lnv[:, s], ve[:, s], ACT.Ln))
            act.activation(rs[:, s], lnv[:, s], ACT.Exp, scale=-0.5).then_inc(sig("root"), 1)

        def norm_refine(dve, ch, k, s=slice(0, NT)):
            dve.wait_ge(sig("root"), k + 1)
            ch.link(dve.tensor_tensor(rt[:, s], rs[:, s], rs[:, s], ALU.mult))
            ch.link(dve.tensor_tensor(rt[:, s], rt[:, s], ve[:, s], ALU.mult))
            ch.link(dve.tensor_scalar(rt[:, s], rt[:, s], -0.5, 1.5, ALU.mult, ALU.add))
            ch.link(dve.tensor_tensor(rstd[:, s], rt[:, s], rs[:, s], ALU.mult))

        def norm_apply(dve, dst, src):
            for j in range(NT):
                ins = dve.tensor_scalar(dst[:, j, :], src[:, j, :], mv[:, j, 0:1], rstd[:, j:j + 1],
                                        ALU.subtract, ALU.mult)
                if j % 4 == 3:
                    ins.then_inc(sig("xn"), 1)

        def norm_turn(pe, src, o):
            for half in range(2):
                pe.wait_ge(sig("xn"), 2 * o + half + 1)
                if o == 0:
                    pe.wait_ge(sig("ident"), 1)
                for j in range(4):
                    ins = pe.transpose(bank(4 + half)[:, j * P:(j + 1) * P], src[:, 4 * half + j, :], ident[:, :])
                ins.then_inc(sig("turned"), 1)

        def norm_take(act, o):
            for half in range(2):
                act.wait_ge(sig("turned"), 2 * o + half + 1)
                act.activation(XNT[:, half * HALF:(half + 1) * HALF], bank(4 + half), ACT.Copy)\
                    .then_inc(sig("xnt"), 1)

        def project(pe, first_bank, lhsT, rhs, signal):
            for half in range(2):
                ins = pe.matmul(bank(first_bank + half)[0:lhsT.shape[1], :], lhsT,
                                rhs[:, half * HALF:(half + 1) * HALF], start=True, stop=True)
            ins.then_inc(sig(signal), 1)

        def two(b):
            return PS[:, b:b + 2, :].rearrange("p a n -> p (a n)")

        def split(dve, ch, dst, src, tmp, signal, t=slice(0, T)):
            hi, mid, lo = (part[:, t] for part in dst)
            src, tmp = src[:, t], tmp[:, t]
            ch.link(dve.tensor_copy(hi, src))
            ch.link(dve.tensor_tensor(tmp, src, hi, ALU.subtract))
            ch.link(dve.tensor_copy(mid, tmp))
            dve.tensor_tensor(lo, tmp, mid, ALU.subtract).then_inc(sig(signal), 1)

        def stack_rows(eng, stack, parts, pick, signal, mine, t=slice(0, T)):
            for i in mine:
                r = 8 * i
                eng.dma_start(stack[r:r + 8, :, t], parts[pick(*divmod(i, 3))][:, t]).then_inc(sig(signal), 16)

        FIRST, REST = slice(0, S), slice(S, T)

        def stack_queries(eng, L, mine):
            for n, t in enumerate((FIRST, REST)):
                eng.wait_ge(sig("qx_parts"), 2 * L + n + 1)
                stack_rows(eng, QS, QP, lambda a, b: a, ("stack_q0", "stack_q")[n], mine, t)

        def stack_self(eng, mine, between=None):
            eng.wait_ge(sig("ka_parts"), 1)
            eng.wait_ge(sig("ka_clear"), 1)
            stack_rows(eng, KSA, KP, lambda a, b: b, "stack_ka", mine)
            eng.wait_ge(sig("q_clear"), 1)
            for n, t in enumerate((FIRST, REST)):
                eng.wait_ge(sig("qa_parts"), n + 1)
                stack_rows(eng, QS, QPA, lambda a, b: a, ("stack_qa0", "stack_qa")[n], mine, t)
                if n == 0 and between:
                    between()

        def o_region(u):
            g = (u % PAIRS) // 2
            return bank(6)[:, (g % 2) * S:(g % 2) * S + S]

        def o_rows(u, i):
            r = 32 * ((2 * u + i) % HG)
            return slice(r, r + 32)

        NZ = UNITS // 4
        STEPS = QT * PAIRS + 1

        def out_evac(act, A, z, bias):
            act.wait_ge(sig("o_full"), A * NZ + z + 1)
            if A == 0 and z == 0:
                act.wait_ge(sig("stack_k"), 16 * 12)
            b, x = z // 2, z % 2
            dst = OT[:, 2 * x:2 * x + 2, b * S:(b + 1) * S]
            src = bank(6).rearrange("p (g t) -> p g t", g=2)
            if bias:
                ins = act.activation(dst, src, ACT.Identity, bias=den_eps[:, 0:1])
            else:
                ins = act.activation(dst, src, ACT.Copy)
            ins.then_inc(sig("o_taken"), 1)

        def den_bank(z):
            return bank(5 if z == NZ - 1 else 7)

        def scratch(z):
            s = SCR[:, 0 if z == NZ - 1 else 1, :]
            return s[:, 0:HALF], s[:, HALF:T]

        def den_spread(pe, A, z):
            pe.wait_ge(sig("o_taken"), A * NZ + z + 1)
            if z == NZ - 1:
                pe.wait_ge(sig("maxed" if A else "a_masked"), A * B * STEPS if A else UNITS)
            elif z or A:
                pe.wait_ge(sig("o_normed"), A * NZ + z)
            if z and z % 2 == 0:
                pe.wait_ge(sig("x_batch"), A * (B - 1) + z // 2)
            b, x = z // 2, z % 2
            pe.matmul(den_bank(z).rearrange("p (g t) -> p g t", g=2), spread[:, :],
                      OT[:, 2 * x:2 * x + 2, b * S:(b + 1) * S], start=True, stop=True).then_inc(sig("den"), 1)

        def invert(dve, ch, dst, den, guess):
            ch.link(dve.tensor_tensor(dst, den, guess, ALU.mult))
            ch.link(dve.scalar_tensor_tensor(dst, dst, 2.0, guess, ALU.subtract, ALU.mult, reverse0=True))

        def den_guess(act, ch, A, z):
            act.wait_ge(sig("den"), A * NZ + z + 1)
            if (z or A) and z != NZ - 1:
                act.wait_ge(sig("o_normed"), A * NZ + z)
            guess = scratch(z)[1]
            ch.link(act.activation(guess, den_bank(z), ACT.Ln))
            act.activation(guess, guess, ACT.Exp, scale=-1.0).then_inc(sig("den_guess"), 1)

        def out_norm(dve, ch, A, z):
            b, x = z // 2, z % 2
            dve.wait_ge(sig("den_guess"), A * NZ + z + 1)
            inverse, guess = scratch(z)
            invert(dve, ch, inverse, den_bank(z), guess)
            o = OT[:, 2 * x:2 * x + 2, b * S:(b + 1) * S]
            dve.tensor_tensor(o, o, inverse.rearrange("p (g t) -> p g t", g=2), ALU.mult).then_inc(sig("o_normed"), 1)

        def out_project(pe, A, b):
            pe.wait_ge(sig("o_normed"), A * NZ + 2 * b + 2)
            pe.wait_ge(sig("wox_in"), 16)
            for q in range(QT):
                o = bank(7)[:, q * P:(q + 1) * P]
                t0 = b * S + q * P
                for g in range(NG):
                    ins = pe.matmul(o, OT[:, g, t0:t0 + P], wox[:, A, g, :], start=(g == 0), stop=(g == NG - 1))
            ins.then_inc(sig("proj_out"), 1)

        def residual(dve, ch, A, b):
            dve.wait_ge(sig("proj_out"), A * B + b + 1)
            x = X[:, QT * b:QT * (b + 1), :].rearrange("p j d -> p (j d)")
            last = b == B - 1
            dve.tensor_tensor(x, x, bank(7)[:, 0:QT * P], ALU.add).then_inc(sig("x_res" if last else "x_batch"), 1)
            if last:
                dve.wait_ge(sig("x_res"), (1, 2, 5)[A])
            else:
                dve.wait_ge(sig("x_batch"), A * (B - 1) + b + 1)
            for j in range(QT * b, QT * (b + 1)):
                ins = dve.bn_stats(st[:, j, :], X[:, j, :])
            ch.link(ins)

        SPREAD, GUESSED, DIVIDE, PROJECT, ADD = ((7, 8, 8), (None, 8, 8), (10, 9, 9), (10, 11, 11), (12, 12, 12))

        def at(u, after, whole=False):
            z = (u - after) // 4
            return z if (u - after) % 4 == 0 and 0 <= z < NZ and (z % 2 or not whole) else None

        def output_tensor(pe, A, u):
            z = at(u, PROJECT[A], whole=True)
            if z is not None:
                out_project(pe, A, z // 2)
            z = at(u, SPREAD[A])
            if z is not None:
                den_spread(pe, A, z)

        def output_vector(dve, ch, A, u):
            z = at(u, DIVIDE[A])
            if z is not None:
                out_norm(dve, ch, A, z)
            z = at(u, ADD[A], whole=True)
            if z is not None:
                residual(dve, ch, A, z // 2)

        LAST = UNITS + 12

        def x_ready(eng, stage):
            eng.wait_ge(sig("x_res"), stage)

        def context_tensor(pe):
            pe.wait_ge(sig("ctx_in"), 16)
            pe.wait_ge(sig("wx_in"), 16)
            project(pe, 0, wx[:, 0, 1, :], CT, "kx_psum")
            for j in range(NT):
                ins = pe.matmul(bank(2 + j // 4)[:, (j % 4) * P:(j % 4 + 1) * P], CT[:, j * P:(j + 1) * P],
                                wx[:, 0, 2, :], start=True, stop=True)
            ins.then_inc(sig("vx_psum"), 1)

        def take_values(act, dst, first_bank):
            for half in range(2):
                ins = act.activation(dst[:, 4 * half:4 * half + 4, :, 0:DH].rearrange("p j h e -> p (j h) e"),
                                     bank(first_bank + half).rearrange("p (a e) -> p a e", e=DH), ACT.Copy)
            return ins

        def context_scalar(act):
            act.wait_ge(sig("kx_psum"), 1)
            act.activation(KX32, two(0), ACT.Copy).then_inc(sig("kx_raw"), 1)
            act.wait_ge(sig("vx_psum"), 1)
            take_values(act, VX, 2).then_inc(sig("vx_ready"), 1)

        def context_keys_pool(pool, ch, L, neg):
            if L == 0:
                for b in range(B):
                    ins = pool.tensor_scalar(VMASK[:, b * S:(b + 1) * S], iotaf, lensf[:, b:b + 1], None,
                                             ALU.is_lt)
                ch.link(ins)
            else:
                pool.wait_ge(sig("pad_in"), 16)
                ch.link(pool.tensor_scalar(VMASK, PAD, -1.0, 1.0, ALU.mult, ALU.add))
            pool.wait_ge(sig("kx_raw"), L + 1)
            ch.link(pool.tensor_tensor(KX32, KX32, VMASK, ALU.mult))
            ch.link(pool.tensor_scalar(KXP[:, 0, :], KX32, 1.0, 0.0, ALU.mult, ALU.add))
            ch.link(pool.tensor_tensor(KXR, KX32, KXP[:, 0, :], ALU.subtract))
            ch.link(pool.tensor_scalar(KXP[:, 1, :], KXR, 1.0, 0.0, ALU.mult, ALU.add))
            pool.tensor_tensor(KXP[:, 2, :], KXR, KXP[:, 1, :], ALU.subtract).then_inc(sig("kx_parts"), 1)
            pool.wait_ge(sig("kx_parts"), L + 1)
            for c, part in enumerate(bf16_parts(neg)):
                ins = pool.tensor_scalar(NEGP[:, c, :], VMASK, -1.0, part, ALU.add, ALU.mult)
            ins.then_inc(sig("neg_parts"), 1)

        def stack_context(eng, L):
            eng.wait_ge(sig("kx_parts"), L + 1)
            if L == 0:
                eng.wait_ge(sig("kx_zero"), 1)
            for a in range(3):
                for b in range(3):
                    r = 24 * a + 8 * b
                    eng.dma_start(KX[r:r + 8, :, :], KXP[:, b, :]).then_inc(sig("stack_k"), 16)
            eng.wait_ge(sig("neg_parts"), L + 1)
            for c in range(3):
                eng.dma_start(KX[NEG_ROW + c:NEG_ROW + c + 1, :, :], NEGP[0:H, c, :]).then_inc(sig("stack_k"), 16)

        def weighed(eng, A, v):
            if v % 4 == 3:
                eng.wait_ge(sig("o_full"), A * NZ + v // 4 + 1)
            else:
                eng.wait_ge(sig("weighed"), A * (UNITS - NZ) + v + 1 - (v + 1) // 4)

        def o_free(pe, A, u):
            if u % 4 == 0 and (A or u):
                pe.wait_ge(sig("o_taken"), A * NZ + u // 4)

        def self_tensor(pe):
            pe.wait_ge(sig("wself_in"), 16)
            pe.wait_ge(sig("xnt"), 2)
            project(pe, 6, wself[:, 2, :], XNT, "self_proj")
            pe.wait_ge(sig("kx_raw"), 1)
            project(pe, 0, wself[:, 1, :], XNT, "self_proj")
            pe.wait_ge(sig("vx_ready"), 1)
            project(pe, 2, wself[:, 0, :], XNT, "self_proj")
            for j in range(NT):
                ins = pe.matmul(bank(4 + j // 4)[:, (j % 4) * P:(j % 4 + 1) * P], XNT[:, j * P:(j + 1) * P],
                                wself[:, 3, :], start=True, stop=True)
            ins.then_inc(sig("self_proj"), 1)
            pe.wait_ge(sig("stack_ka"), 16 * 9)
            pe.wait_ge(sig("stack_qa0"), 16 * 9)
            pe.wait_ge(sig("ka_clear"), 1)
            pe.wait_ge(sig("q_clear"), 1)
            pe.wait_ge(sig("q_zero"), 1)
            pe.wait_ge(sig("va_const"), 1)
            pe.wait_ge(sig("va_ready"), 1)

            def scores(u):
                if u >= 3:
                    pe.wait_ge(sig("a_masked"), u - 2)
                b, hp = divmod(u, PAIRS)
                if u == PAIRS:
                    pe.wait_ge(sig("stack_qa"), 16 * 9)
                t0 = b * S
                for i in range(2):
                    h = 2 * hp + i
                    o = bank(2 * (u % 3) + i)
                    pe.matmul(o[:, 0:S], KSA[:, h, t0:t0 + P], QS[:, h, t0:t0 + S], start=True, stop=True)
                    ins = pe.matmul(o[:, S:S + P], KSA[:, h, t0 + P:t0 + S], QS[:, h, t0 + P:t0 + S],
                                    start=True, stop=True)
                ins.then_inc(sig("a_scores"), 1)

            def weigh(u):
                b, hp = divmod(u, PAIRS)
                pe.wait_ge(sig("a_masked"), u + 1)
                o_free(pe, 0, u)
                for i in range(2):
                    pe.matmul(o_region(u)[o_rows(u, i), :], VA[:, 2 * b, 2 * hp + i, :], E[:, u % 3, i, 0:S],
                              start=True, stop=False, skip_group_check=True)
                for i in range(2):
                    ins = pe.matmul(o_region(u)[o_rows(u, i), P:S], VA[:, 2 * b + 1, 2 * hp + i, :],
                                    E[:, u % 3, i, S:S + P], start=False, stop=True, skip_group_check=True)
                ins.then_inc(sig("o_full" if u % 4 == 3 else "weighed"), 1)

            scores(0)
            scores(1)
            for u in range(UNITS):
                if u + 2 < UNITS:
                    scores(u + 2)
                weigh(u)
                output_tensor(pe, 0, u)
            for u in range(UNITS, LAST):
                output_tensor(pe, 0, u)

        EG = SCR[:, 0, :]
        SPQ = SCR[:, 3, :]
        R1 = SCR[:, 1, :]

        def self_scalar(act, ch):
            act.wait_ge(sig("self_proj"), 1)
            act.wait_ge(sig("bg_neg"), 1)
            act.activation(EG, two(6), ACT.Exp, bias=bg[:, 1:2], scale=-1.0).then_inc(sig("self_gate"), 1)
            for n, dst in enumerate((XN1, SPQ)):
                act.wait_ge(sig("self_proj"), n + 2)
                ch.link(act.activation(dst, two(2 * n), ACT.Abs))
                ch.link(act.activation(dst, dst, ACT.Exp, scale=-1.0))
                act.activation(dst, dst, ACT.Ln, bias=1.0).then_inc(sig("self_sp"), 1)
                if n == 0:
                    act.wait_ge(sig("gate_den"), 1)
                    ch.link(act.activation(R1, EG, ACT.Ln))
                    act.activation(R1, R1, ACT.Exp, scale=-1.0).then_inc(sig("gate_guess"), 1)
            act.wait_ge(sig("self_proj"), 4)
            take_values(act, VA, 4).then_inc(sig("va_ready"), 1)
            stack_self(act, range(1, 9, 2))
            act.wait_ge(sig("den_eps"), 1)
            out_evac(act, 0, 0, True)
            for z in range(NZ):
                if z + 1 < NZ:
                    out_evac(act, 0, z + 1, True)
                den_guess(act, ch, 0, z)

        def self_vector(dve, ch):
            dve.wait_ge(sig("bg_in"), 16)
            dve.tensor_scalar(bg[:, 1:2], bg[:, 0:1], -1.0, None, ALU.mult).then_inc(sig("bg_neg"), 1)
            dve.memset(QSf[96:128, :], 0.0).then_inc(sig("q_zero"), 1)
            dve.wait_ge(sig("self_gate"), 1)
            dve.tensor_scalar(EG, EG, 1e18, 1.0, ALU.min, ALU.add).then_inc(sig("gate_den"), 1)
            dve.wait_ge(sig("self_sp"), 1)
            ch.link(dve.scalar_tensor_tensor(XN1, two(0), 0.0, XN1, ALU.max, ALU.add))
            dve.wait_ge(sig("self_proj"), 4)
            split(dve, ch, KP, XN1, XNT[:, :], "ka_parts")
            dve.wait_ge(sig("gate_guess"), 1)
            invert(dve, ch, EG, EG, R1)
            dve.wait_ge(sig("self_sp"), 2)
            ch.link(dve.scalar_tensor_tensor(SPQ, two(2), 0.0, SPQ, ALU.max, ALU.add))
            ch.link(dve.scalar_tensor_tensor(SPQ, EG, 1e-6, SPQ, ALU.add, ALU.mult))
            for t in (FIRST, REST):
                split(dve, ch, QPA, SPQ, R1, "qa_parts", t)
            dve.wait_ge(sig("const"), 1)
            ch.link(dve.tensor_reduce(den_eps[:, :], spread[:, :], AX, ALU.max))
            dve.tensor_scalar(den_eps[:, :], den_eps[:, :], 1e-6, None, ALU.mult).then_inc(sig("den_eps"), 1)
            mask = masks[:, :, :].rearrange("p a n -> p (a n)").unsqueeze(1).to_broadcast([P, 2, 3 * P])
            dve.wait_ge(sig("stack_ka"), 16 * 9)
            for u in range(UNITS):
                bk = 2 * (u % 3)
                dve.wait_ge(sig("a_scores"), u + 1)
                if u >= 3:
                    weighed(dve, 0, u - 3)
                dve.tensor_tensor(E[:, u % 3, :, 0:3 * P], PS[:, bk:bk + 2, 0:3 * P], mask, ALU.mult)\
                    .then_inc(sig("a_masked"), 1)
                output_vector(dve, ch, 0, u)
            for u in range(UNITS, LAST):
                output_vector(dve, ch, 0, u)

        CHUNKS = (3, 2, 2, 2, 2, 2, 2, 2)

        def steps_before(u):
            b, hp = divmod(u, PAIRS)
            if b + 1 < B:
                k0 = sum(CHUNKS[:hp])
                for k in range(k0, k0 + CHUNKS[hp]):
                    yield b + 1, k

        def vector_bias(L, u):
            return L == 1 and u % 2 == 1

        def cross_tensor(pe, L):
            A = L + 1
            pe.wait_ge(sig("xnt"), 2 * ((1, 5)[L] + 1))
            project(pe, 0, wx[:, L, 0, :], XNT, "qx_psum")
            pe.wait_ge(sig("qx_raw"), L + 1)
            pe.wait_ge(sig("stack_q0"), 16 * 9 * (L + 1))
            pe.wait_ge(sig("stack_k"), 16 * 12 * (L + 1))
            pe.wait_ge(sig("kx_clear"), 1)
            pe.wait_ge(sig("const_late"), 1)
            pe.wait_ge(sig("q_clear"), 1 + L)
            pe.wait_ge(sig("vx_const"), 1)
            pe.wait_ge(sig("vx_ready"), L + 1)
            if L == 1:
                pe.wait_ge(sig("bias_parts"), 1)

            def max_step(b, k):
                n = b * STEPS + k
                if n >= 2 or L:
                    pe.wait_ge(sig("maxed"), L * B * STEPS + max(n - 1, 0))
                o = bank(4 + n % 2)
                if k == STEPS - 1:
                    pe.wait_ge(sig("max_split"), L * B + b + 1)
                    for q in range(QT):
                        ins = pe.transpose(halfbank(4 + n % 2)[0:3 * H, q * P:(q + 1) * P],
                                           mx_parts[:, b % 2, q, :, :].rearrange("p c h -> p (c h)"), identb[:, :])
                else:
                    q, hp = divmod(k, PAIRS)
                    for i in range(2):
                        h = 2 * hp + i
                        ins = pe.matmul(o[:, i * S:(i + 1) * S], QS[:, h, b * S + q * P:b * S + (q + 1) * P],
                                        KX[:, h, b * S:(b + 1) * S], start=True, stop=True)
                ins.then_inc(sig("max_scores"), 1)

            def scores(u):
                b, hp = divmod(u, PAIRS)
                if hp == 0:
                    pe.wait_ge(sig("max_in%d" % b), 16 * (L + 1))
                if u >= 2 or L:
                    pe.wait_ge(sig("x_exp"), L * UNITS + max(u - 1, 0))
                for i in range(2):
                    h = 2 * hp + i
                    o = bank(2 * (u % 2) + i)
                    parts_of_bias = L == 1 and not vector_bias(L, u)
                    if parts_of_bias:
                        for c in range(3):
                            pe.matmul(o.rearrange("p (k n) -> p k n", k=QT), identb[:, :], BIASK[:, :, c, :],
                                      start=(c == 0), stop=False, skip_group_check=True)
                    for kt in range(QT):
                        ins = pe.matmul(o[:, kt * S:(kt + 1) * S], KX[:, h, b * S + kt * P:b * S + (kt + 1) * P],
                                        QS[:, h, b * S:(b + 1) * S], start=not parts_of_bias, stop=True,
                                        skip_group_check=True)
                ins.then_inc(sig("x_scores"), 1)

            def weigh(u):
                b, hp = divmod(u, PAIRS)
                pe.wait_ge(sig("x_exp"), L * UNITS + u + 1)
                o_free(pe, A, u)
                for kt in range(QT):
                    for i in range(2):
                        ins = pe.matmul(o_region(u)[o_rows(u, i), :], VX[:, 2 * b + kt, 2 * hp + i, :],
                                        E[:, u % 3, i, kt * S:(kt + 1) * S], start=(kt == 0), stop=(kt == QT - 1),
                                        skip_group_check=True)
                ins.then_inc(sig("o_full" if u % 4 == 3 else "weighed"), 1)

            for k in range(STEPS):
                max_step(0, k)
            pe.wait_ge(sig("stack_q"), 16 * 9 * (L + 1))
            for u in range(UNITS):
                steps = list(steps_before(u))
                for i in range(max(2, len(steps))):
                    if i < len(steps):
                        max_step(*steps[i])
                    if i == 0:
                        scores(u)
                    elif i == 1 and u:
                        weigh(u - 1)
                output_tensor(pe, A, u)
            weigh(UNITS - 1)
            for u in range(UNITS, LAST):
                output_tensor(pe, A, u)

        def cross_scalar(act, ch, L):
            A = L + 1
            act.wait_ge(sig("qx_psum"), L + 1)
            if L == 0:
                ins = act.activation(EG, two(0), ACT.Copy, scale=DH ** -0.5)
            else:
                act.wait_ge(sig("bq_scaled"), 1)
                ins = act.activation(EG, two(0), ACT.Identity, bias=bqk[:, 2:3], scale=DH ** -0.5)
            ins.then_inc(sig("qx_raw"), 1)
            stack_queries(act, L, range(1, 9, 2))
            act.wait_ge(sig("stack_q0"), 16 * 9 * (L + 1))
            act.wait_ge(sig("stack_q"), 16 * 9 * (L + 1))
            act.wait_ge(sig("stack_k"), 16 * 12 * (L + 1))
            for u in range(UNITS):
                act.wait_ge(sig("x_scores"), L * UNITS + u + 1)
                if vector_bias(L, u):
                    act.wait_ge(sig("biased"), u // 2 + 1)
                if u >= 3:
                    weighed(act, A, u - 3)
                bk = 2 * (u % 2)
                act.activation(E[:, u % 3, :, :], PS[:, bk:bk + 2, :], ACT.Exp).then_inc(sig("x_exp"), 1)
                if u % 4 == 0 and u:
                    out_evac(act, A, u // 4 - 1, False)
                if at(u, GUESSED[A]) is not None:
                    den_guess(act, ch, A, at(u, GUESSED[A]))
            out_evac(act, A, NZ - 1, False)
            for z in range(NZ):
                if 4 * z + GUESSED[A] >= UNITS:
                    den_guess(act, ch, A, z)

        def cross_vector(dve, ch, L):
            A = L + 1
            if L == 1:
                dve.wait_ge(sig("bqk_in"), 16)
                dve.tensor_scalar(bqk[:, 2:3], bqk[:, 0:1], DH ** -0.5, None, ALU.mult).then_inc(sig("bq_scaled"), 1)
            dve.wait_ge(sig("qx_raw"), L + 1)
            for t in (FIRST, REST):
                split(dve, ch, QP, EG, R1, "qx_parts", t)

            def max_step(b, k):
                n = b * STEPS + k
                dve.wait_ge(sig("max_scores"), L * B * STEPS + n + 1)
                o = bank(4 + n % 2)
                if k < STEPS - 1:
                    q, hp = divmod(k, PAIRS)
                    if L == 0:
                        ins = dve.tensor_reduce(mx[:, b % 2, q, 2 * hp:2 * hp + 2],
                                                o.rearrange("p (i n) -> p i n", i=2), AX, ALU.max, negate=True)
                    else:
                        if n >= 2:
                            dve.wait_ge(sig("maxed"), L * B * STEPS + n - 1)
                        for i in range(2):
                            h = 2 * hp + i
                            ins = dve.tensor_tensor_reduce(
                                out=BIASED[:, n % 2, i, :], in0=o[:, i * S:(i + 1) * S], in1=BIASQ[:, q, :],
                                scale=-1.0, scalar=3e38, op0=ALU.add, op1=ALU.min,
                                accum_out=mx[:, b % 2, q, h:h + 1])
                    ins.then_inc(sig("maxed"), 1)
                    if k == STEPS - 2:
                        dve.wait_ge(sig("maxed"), L * B * STEPS + n + 1)
                        m, hi, mid, lo = [mx[:, b % 2, :, :]] + [mx_parts[:, b % 2, :, c, :] for c in range(3)]
                        ch.link(dve.tensor_copy(hi, m))
                        ch.link(dve.tensor_tensor(mx_rest[:, :, :], m, hi, ALU.subtract))
                        ch.link(dve.tensor_copy(mid, mx_rest[:, :, :]))
                        dve.tensor_tensor(lo, mx_rest[:, :, :], mid, ALU.subtract).then_inc(sig("max_split"), 1)
                else:
                    dve.tensor_copy(mx_rows[:, b, :], halfbank(4 + n % 2)[0:3 * H, 0:S]).then_inc(sig("maxed"), 1)

            for k in range(STEPS):
                max_step(0, k)
            for u in range(UNITS):
                for b, k in steps_before(u):
                    max_step(b, k)
                if vector_bias(L, u):
                    dve.wait_ge(sig("x_scores"), L * UNITS + u + 1)
                    o = PS[:, 2 * (u % 2):2 * (u % 2) + 2, :]
                    dve.tensor_tensor(o, o, BIASF.unsqueeze(1).to_broadcast([P, 2, QT * S]), ALU.add)\
                        .then_inc(sig("biased"), 1)
                output_vector(dve, ch, A, u)
            for u in range(UNITS, LAST):
                output_vector(dve, ch, A, u)

        ZN = VAf[:, 0:T].rearrange("p (j d) -> p j d", j=NT)
        RANK = VAf[:, T:T + 4 * NE * NE].rearrange("p (j a b) -> p j a b", j=4, a=NE)
        SAME = VAf[:, T + 4 * NE * NE:T + 8 * NE * NE].rearrange("p (j a b) -> p j a b", j=4, a=NE)
        LOOPS = 2

        PASSES = 2 * LOOPS
        UPS = NE * 2
        UNITS_MOE = PASSES * UPS
        QUARTERS = (10, 12, 14, 15)

        def tiles_of(p):
            return slice(4 * (p % 2), 4 * (p % 2) + 4)

        def tokens_of(p):
            return slice(HALF * (p % 2), HALF * (p % 2 + 1))

        def pass_turn(pe, p):
            pe.wait_ge(sig("xn"), 4 + p + 1)
            if p:
                pe.wait_ge(sig("logits_read"), p)
            if p == 2:
                pe.wait_ge(sig("vx_ready"), 2)
            if p == 3:
                pe.wait_ge(sig("w_quantised"), 1)
            for t in range(4):
                ins = pe.transpose(bank(7)[:, t * P:(t + 1) * P], ZN[:, tiles_of(p), :][:, t, :], ident[:, :])
            ins.then_inc(sig("turned"), 1)

        def pass_logits(pe, p):
            pe.wait_ge(sig("xnt"), 4 + p + 1)
            for t in range(4):
                ins = pe.matmul(bank(7)[:, t * NE:(t + 1) * NE], XNT[:, tokens_of(p)][:, t * P:(t + 1) * P],
                                router[:, :], start=True, stop=True)
            ins.then_inc(sig("logits"), 1)

        def context_quarter_tensor(pe, i):
            if i == 0:
                pe.wait_ge(sig("ctx_in"), 32)
                pe.wait_ge(sig("brow_in"), 16)
                pe.wait_ge(sig("logits_read"), 2)
            elif i == 2:
                pe.wait_ge(sig("kx_raw"), 2)
            else:
                pe.wait_ge(sig("quarter_read"), (i + 1) // 2)
            half = i % 2
            if i < 2:
                ins = pe.matmul(bank(7), wx[:, 1, 1, :], CT[:, half * HALF:(half + 1) * HALF], start=True, stop=True)
            else:
                for t in range(4):
                    j = 4 * half + t
                    o = bank(7)[:, t * P:(t + 1) * P]
                    pe.matmul(o, CT[:, j * P:(j + 1) * P], wx[:, 1, 2, :], start=True, stop=False)
                    ins = pe.matmul(o, onesf[0:1, :], brow[0:1, :], start=False, stop=True)
            ins.then_inc(sig("quarter"), 1)

        def context_quarter_scalar(act, i):
            act.wait_ge(sig("quarter"), i + 1)
            half = i % 2
            if i < 2:
                act.wait_ge(sig("bqk_in"), 16)
                ins = act.activation(KX32[:, half * HALF:(half + 1) * HALF], bank(7), ACT.Identity, bias=bqk[:, 1:2])
            else:
                ins = act.activation(VX[:, 4 * half:4 * half + 4, :, 0:DH].rearrange("p j h e -> p (j h) e"),
                                     bank(7).rearrange("p (a e) -> p a e", e=DH), ACT.Copy)
            ins.then_inc(sig({1: "kx_raw", 3: "vx_ready"}.get(i, "quarter_read")), 1)

        def experts_tensor(pe):
            pe.wait_ge(sig("experts_in"), 16 * 3)

            def up(g):
                p, n = divmod(g, UPS)
                e, c = divmod(n, 2)
                if g >= 3:
                    pe.wait_ge(sig("gated"), g - 2)
                for w, o in ((W1, 0), (W3, 1)):
                    ins = pe.matmul(bank(2 * (g % 3) + o), w[:, e, c * P:(c + 1) * P], XNT[:, tokens_of(p)],
                                    start=True, stop=True)
                ins.then_inc(sig("up"), 1)

            def down(m):
                pe.wait_ge(sig("gated"), 2 * m + 2)
                if m:
                    pe.wait_ge(sig("mixed"), m)
                for t in range(4):
                    for c in range(2):
                        ins = pe.matmul(bank(6)[:, t * P:(t + 1) * P], E6[:, (2 * m + c) % 4, t * P:(t + 1) * P],
                                        W2[:, m % NE, c, :], start=(c == 0), stop=(c == 1))
                ins.then_inc(sig("down"), 1)

            pass_turn(pe, 0)
            pass_logits(pe, 0)
            for g in range(UNITS_MOE):
                p, n = divmod(g, UPS)
                up(g)
                if g >= 2 and g % 2 == 0:
                    down(g // 2 - 1)
                if p + 1 < PASSES and n == 6:
                    pass_turn(pe, p + 1)
                if p + 1 < PASSES and n == 8:
                    pass_logits(pe, p + 1)
                if p == 0 and n in QUARTERS:
                    context_quarter_tensor(pe, QUARTERS.index(n))
                if p == 1 and n == 13:
                    pe.wait_ge(sig("logits_read"), 3)
                    pe.wait_ge(sig("w_sums"), 1)
                    pe.matmul(bank(7)[:, 0:2], onesf, wscale[:, :], start=True, stop=True).then_inc(sig("w_total"), 1)
                if p == 3 and n == 10:
                    pe.wait_ge(sig("logits_read"), 4)
                    half_turn(pe, 0, 7)
            down(UNITS_MOE // 2 - 1)

        def pass_scalar(act, p):
            act.wait_ge(sig("turned"), 4 + p + 1)
            act.activation(XNT[:, tokens_of(p)], bank(7), ACT.Copy, scale=normw[:, 0:1]).then_inc(sig("xnt"), 1)

        def pass_gates(act, p):
            act.wait_ge(sig("logits_shifted"), p + 1)
            g = gates[:, tiles_of(p), :]
            act.activation(g, g, ACT.Exp).then_inc(sig("gate_exp"), 1)

        def experts_scalar(act, ch):
            act.wait_ge(sig("router_in"), 32)
            norm_root(act, ch, 3, tiles_of(0))
            pass_scalar(act, 0)
            pass_gates(act, 0)
            for g in range(UNITS_MOE):
                p, n = divmod(g, UPS)
                act.wait_ge(sig("up"), g + 1)
                if g >= 2:
                    act.wait_ge(sig("gated"), g - 1)
                act.activation(E6[:, 4 + g % 2, :], bank(2 * (g % 3)), ACT.Silu).then_inc(sig("silu"), 1)
                if p + 1 < PASSES and n == 3:
                    exp_and_ln(act)
                    norm_root(act, ch, 3 + p + 1, tiles_of(p + 1))
                if p + 1 < PASSES and n == 6:
                    pass_scalar(act, p + 1)
                if p + 1 < PASSES and n == 9:
                    pass_gates(act, p + 1)
                if p == 0 and n in QUARTERS:
                    context_quarter_scalar(act, QUARTERS.index(n))
                if p == 3 and n == 6:
                    exp_and_ln(act)
                    norm_root(act, ch, 7, tiles_of(0))
                if p == 3 and n == 11:
                    half_take(act, 0, 7)
            exp_and_ln(act)

        def pass_stats(dve, ch, p):
            s = tiles_of(p)
            if p >= 2:
                dve.wait_ge(sig("mixed"), UPS // 2 * (p - 1))
            for j in range(s.start, s.stop):
                ins = dve.bn_stats(st[:, j, :], XN[:, j, :])
            ch.link(ins)
            for j in range(s.start, s.stop):
                ins = dve.bn_aggr(mv[:, j, :], st[:, j, :])
            ch.link(ins)
            ch.link(dve.tensor_tensor(rt[:, s], mv[:, s, 0], mv[:, s, 0], ALU.mult))
            ch.link(dve.tensor_tensor(ve[:, s], rt[:, s], mv[:, s, 1], ALU.add))
            dve.tensor_scalar(ve[:, s], ve[:, s], 1e-6, None, ALU.add).then_inc(sig("ve"), 1)

        def pass_norm(dve, ch, p):
            norm_refine(dve, ch, 3 + p, tiles_of(p))
            s = tiles_of(p)
            for j in range(s.start, s.stop):
                ins = dve.tensor_scalar(ZN[:, j, :], XN[:, j, :], rstd[:, j:j + 1], None, ALU.mult)
            ins.then_inc(sig("xn"), 1)

        def pass_rank(dve, ch, p):
            s = tiles_of(p)
            l, g, c, m = logits[:, s, :], gates[:, s, :], chosen[:, s, :], tok1[:, s]
            dve.wait_ge(sig("logits"), p + 1)
            dve.tensor_copy(l, bank(7)[:, 0:4 * NE].rearrange("p (j e) -> p j e", j=4)).then_inc(sig("logits_read"), 1)
            dve.wait_ge(sig("logits_read"), p + 1)
            ch.link(dve.tensor_reduce(m, l, AX, ALU.max))
            dve.tensor_tensor(g, l, m.unsqueeze(2).to_broadcast([P, 4, NE]), ALU.subtract)\
                .then_inc(sig("logits_shifted"), 1)
            other = l.unsqueeze(2).to_broadcast([P, 4, NE, NE])
            own = l.unsqueeze(3).to_broadcast([P, 4, NE, NE])
            dve.tensor_tensor(RANK, other, own, ALU.is_gt)
            ch.link(dve.tensor_tensor(SAME, other, own, ALU.is_equal))
            ch.link(dve.tensor_tensor(SAME, SAME, tri[:, :, :].unsqueeze(1).to_broadcast([P, 4, NE, NE]), ALU.mult))
            ch.link(dve.tensor_tensor(RANK, RANK, SAME, ALU.add))
            ch.link(dve.tensor_reduce(c, RANK, AX, ALU.add))
            ch.link(dve.tensor_scalar(c, c, 1.5, None, ALU.is_lt))

        def pass_share(dve, ch, p):
            s = tiles_of(p)
            g, c, total, share = gates[:, s, :], chosen[:, s, :], tok1[:, s], tok2[:, s]
            dve.wait_ge(sig("gate_exp"), p + 1)
            ch.link(dve.tensor_reduce(total, g, AX, ALU.add))
            ch.link(dve.reciprocal(total, total))
            ch.link(dve.tensor_tensor(g, g, c, ALU.mult))
            ch.link(dve.tensor_tensor(g, g, total.unsqueeze(2).to_broadcast([P, 4, NE]), ALU.mult))
            ch.link(dve.tensor_reduce(share, g, AX, ALU.add))
            ch.link(dve.tensor_scalar(share, share, 1e-9, None, ALU.add))
            ch.link(dve.reciprocal(share, share))
            ch.link(dve.tensor_tensor(g, g, share.unsqueeze(2).to_broadcast([P, 4, NE]), ALU.mult))

        def half_residual(dve, ch, half):
            x = X[:, 4 * half:4 * half + 4, :]
            dve.wait_ge(sig("mixed"), UPS // 2 * (3 + half))
            ins = dve.tensor_tensor(x, x, XN[:, 4 * half:4 * half + 4, :], ALU.add)
            if half == 0:
                ch.link(ins)
            else:
                ins.then_inc(sig("x_res"), 1)
                dve.wait_ge(sig("x_res"), 3)
            s = tiles_of(half)
            for j in range(s.start, s.stop):
                ins = dve.bn_stats(st[:, j, :], X[:, j, :])
            ch.link(ins)
            for j in range(s.start, s.stop):
                ins = dve.bn_aggr(mv[:, j, :], st[:, j, :])
            ch.link(ins)
            dve.tensor_scalar(ve[:, s], mv[:, s, 1], 1e-5, None, ALU.add).then_inc(sig("ve"), 1)

        def half_norm(dve, ch, half):
            s = tiles_of(half)
            norm_refine(dve, ch, 7 + half, s)
            for j in range(s.start, s.stop):
                ins = dve.tensor_scalar(XN[:, j, :], X[:, j, :], mv[:, j, 0:1], rstd[:, j:j + 1],
                                        ALU.subtract, ALU.mult)
            ins.then_inc(sig("xn"), 1)

        def half_turn(pe, half, bk):
            pe.wait_ge(sig("xn"), 2 * 4 + half + 1)
            for t in range(4):
                ins = pe.transpose(bank(bk)[:, t * P:(t + 1) * P], XN[:, 4 * half + t, :], ident[:, :])
            ins.then_inc(sig("turned"), 1)

        def half_take(act, half, bk):
            act.wait_ge(sig("turned"), 2 * 4 + half + 1)
            act.activation(XNT[:, tokens_of(half)], bank(bk), ACT.Copy).then_inc(sig("xnt"), 1)

        def experts_vector(dve, ch):
            pass_stats(dve, ch, 0)
            pass_norm(dve, ch, 0)
            pass_rank(dve, ch, 0)
            pass_share(dve, ch, 0)

            def mix(m):
                p, e = divmod(m, NE)
                dve.wait_ge(sig("down"), m + 1)
                if m:
                    dve.wait_ge(sig("mixed"), m)
                for t in range(4):
                    j = 4 * (p % 2) + t
                    ins = dve.scalar_tensor_tensor(XN[:, j, :], bank(6)[:, t * P:(t + 1) * P],
                                                   gates[:, j, e:e + 1], XN[:, j, :], ALU.mult, ALU.add)
                ins.then_inc(sig("mixed"), 1)

            for g in range(UNITS_MOE):
                p, n = divmod(g, UPS)
                dve.wait_ge(sig("silu"), g + 1)
                if g >= 4:
                    dve.wait_ge(sig("down"), (g - 4) // 2 + 1)
                dve.tensor_tensor(E6[:, g % 4, :], E6[:, 4 + g % 2, :], bank(2 * (g % 3) + 1), ALU.mult)\
                    .then_inc(sig("gated"), 1)
                if g >= 2 and g % 2 == 0:
                    mix(g // 2 - 1)
                if p + 1 < PASSES:
                    if n == 2:
                        pass_stats(dve, ch, p + 1)
                    if n == 4:
                        pass_norm(dve, ch, p + 1)
                    if n == 8:
                        pass_rank(dve, ch, p + 1)
                    if n == 10:
                        pass_share(dve, ch, p + 1)
                if p == 1 and n == 11:
                    feed_weight_sums(dve, ch)
                if p == 1 and n == 14:
                    feed_weights(dve, ch)
                if p == 3 and n == 5:
                    half_residual(dve, ch, 0)
                if p == 3 and n == 8:
                    half_norm(dve, ch, 0)
            mix(UNITS_MOE // 2 - 1)
            half_residual(dve, ch, 1)

        def tiles(ap, n):
            return [ap[:, i * T:(i + 1) * T] for i in range(n)]

        ot, va, ks, ee = tiles(OTf, 4), tiles(VAf, 4), tiles(KSf, 6), \
            tiles(E[:, :, :, :].rearrange("p a b c -> p (a b c)"), 3)
        LOGR, LAN, RR, EN = ot[0:2], ot[2:4], va[0:2], va[2:4]
        BCOL, DXB, SS, HH, HC = ee[0], ks[0:2], ks[2:4], ks[4:6], (ee[1], ee[2])
        DELTA, DX, LA, DTI = SCR[:, 1, :], SCR[:, 2, :], SCR[:, 0, :], SCR[0:DTR, 3, :]
        WW = SCR[:, 3, :]
        BC = KSf[:, 7680:8192].bitcast(BF16)
        BCR, BCM, BCL = ks[2], ks[3][:, 0:HALF].bitcast(BF16), ks[3][:, HALF:T].bitcast(BF16)
        CARRY = XN1

        def scan_tensor(pe):
            pe.wait_ge(sig("ssm_in"), 16 * 5)
            for half in range(2):
                pe.wait_ge(sig("xnt"), 2 * 4 + half + 1)
                ins = pe.matmul(bank(half)[0:DTR, :], wssm[:, 0:DTR], XNT[:, half * HALF:(half + 1) * HALF],
                                start=True, stop=True)
            ins.then_inc(sig("dti_psum"), 1)
            for half in range(2):
                for i in range(4):
                    ins = pe.matmul(bank(4 + half)[32 * i:32 * i + 32, :], wssm[:, DTR:DTR + 2 * NS],
                                    XNT[:, half * HALF:(half + 1) * HALF], start=True, stop=True,
                                    skip_group_check=True)
            ins.then_inc(sig("bc_psum"), 1)
            pe.wait_ge(sig("dti"), 1)
            for half in range(2):
                ins = pe.matmul(bank(2 + half), wdt[:, :], DTI[:, half * HALF:(half + 1) * HALF], start=True, stop=True)
            ins.then_inc(sig("delta_psum"), 1)

            pe.wait_ge(sig("bc_rows"), 1)

            def rows(n):
                if n >= 1:
                    pe.wait_ge(sig("b_read"), n)
                project(pe, 0, select[:, n:n + 1].to_broadcast([P, P]), BC, "b_psum")
                if n == 0:
                    pe.wait_ge(sig("delta"), 1)
                if n >= 2:
                    pe.wait_ge(sig("c_read"), n - 1)
                project(pe, 2 + 2 * (n % 2), select[:, NS + n:NS + n + 1].to_broadcast([P, P]), BC, "c_psum")

            def gather(n):
                pe.wait_ge(sig("c_read"), n + 1)
                for half in range(2):
                    ins = pe.matmul(bank(6 + half), ident[:, :], HC[n % 2][:, half * HALF:(half + 1) * HALF],
                                    start=(n == 0), stop=(n == NS - 1), skip_group_check=True)
                ins.then_inc(sig("summed"), 1)

            for n in range(NS):
                rows(n)
                if n >= 2:
                    gather(n - 2)
            gather(NS - 2)
            gather(NS - 1)
            pe.wait_ge(sig("y_ready"), 1)
            for half in range(2):
                for j in range(4):
                    t = 4 * half + j
                    ins = pe.transpose(bank(half)[:, j * P:(j + 1) * P], LA[:, t * P:(t + 1) * P], ident[:, :])
                ins.then_inc(sig("y_turned"), 1)

        def scan_scalar(act, ch):
            act.wait_ge(sig("stack_k"), 16 * 24)
            act.wait_ge(sig("dti_psum"), 1)
            act.activation(DTI, two(0)[0:DTR, :], ACT.Copy).then_inc(sig("dti"), 1)
            act.wait_ge(sig("ssm_in"), 16 * 5)
            act.activation(amat[:, :], amat[:, :], ACT.Exp).then_inc(sig("a_exp"), 1)
            act.wait_ge(sig("delta_psum"), 1)
            ch.link(act.activation(DX, two(2), ACT.Abs, bias=ssmc[:, 0:1]))
            ch.link(act.activation(DX, DX, ACT.Exp, scale=-1.0))
            act.activation(DX, DX, ACT.Ln, bias=1.0).then_inc(sig("delta_ln"), 1)

            def b_copy(n):
                act.wait_ge(sig("b_psum"), n + 1)
                if n >= 1:
                    act.wait_ge(sig("dxb"), n)
                act.activation(BCOL, two(0), ACT.Copy).then_inc(sig("b_read"), 1)

            b_copy(0)
            for n in range(NS):
                act.wait_ge(sig("logr"), n + 1)
                if n >= 2:
                    act.wait_ge(sig("state"), n - 1)
                act.activation(RR[n % 2], LOGR[n % 2], ACT.Exp).then_inc(sig("rr"), 1)
                if n >= 2:
                    act.wait_ge(sig("input"), n - 1)
                act.activation(EN[n % 2], LOGR[n % 2], ACT.Exp, scale=-1.0).then_inc(sig("en"), 1)
                if n + 1 < NS:
                    b_copy(n + 1)

        def scan_pool(pool):
            def dxb(n):
                pool.wait_ge(sig("b_read"), n + 1)
                if n == 0:
                    pool.wait_ge(sig("dx"), 1)
                if n >= 2:
                    pool.wait_ge(sig("input"), n - 1)
                pool.tensor_tensor(DXB[n % 2], DX, BCOL, ALU.mult).then_inc(sig("dxb"), 1)

            def state(n):
                pool.wait_ge(sig("s_sum"), n + 1)
                pool.wait_ge(sig("rr"), n + 1)
                if n >= 2:
                    pool.wait_ge(sig("c_read"), n - 1)
                pool.tensor_tensor(HH[n % 2], RR[n % 2], SS[n % 2], ALU.mult).then_inc(sig("state"), 1)

            dxb(0)
            dxb(1)
            for n in range(NS):
                state(n)
                if n + 2 < NS:
                    dxb(n + 2)

        def scan_vector(dve, ch):
            dve.wait_ge(sig("stack_k"), 16 * 24)
            dve.wait_ge(sig("turned"), 2 * 5)
            ch.link(dve.memset(XN1, 1.0))
            ch.link(dve.tensor_tensor(select[:, :], identb[:, 0:32], identb[:, 32:64], ALU.add))
            ch.link(dve.tensor_tensor(select[:, :], select[:, :], identb[:, 64:96], ALU.add))
            dve.memset(XN1.rearrange("p (b s) -> p b s", b=B)[:, :, 0:1], 0.0)
            dve.wait_ge(sig("a_exp"), 1)
            dve.memset(ssmc[:, 2:3], LOG_TINY)
            ch.link(dve.tensor_scalar(amat[:, :], amat[:, :], -1.0, None, ALU.mult))
            dve.wait_ge(sig("bc_psum"), 1)
            ch.link(dve.tensor_copy(BC, two(4)))
            ch.link(dve.tensor_tensor(BCR, two(4), BC, ALU.subtract))
            ch.link(dve.tensor_copy(BCM, BCR))
            dve.tensor_copy(BC[32:64, :], BCM[32:64, :])
            ch.link(dve.tensor_tensor(BCL, BCR, BCM, ALU.subtract))
            dve.tensor_copy(BC[64:96, :], BCL[64:96, :]).then_inc(sig("bc_rows"), 1)
            dve.wait_ge(sig("delta_ln"), 1)
            ch.link(dve.tensor_scalar(DELTA, two(2), ssmc[:, 0:1], 0.0, ALU.add, ALU.max))
            dve.tensor_tensor(DELTA, DELTA, DX, ALU.add).then_inc(sig("delta"), 1)
            dve.wait_ge(sig("delta"), 1)
            dve.tensor_tensor(DX, DELTA, XNT[:, :], ALU.mult).then_inc(sig("dx"), 1)

            tiny = ssmc[:, 2:3].to_broadcast([P, S])

            def decay(n):
                ch.link(dve.tensor_scalar(LAN[n % 2], DELTA, amat[:, n:n + 1], -7.0, ALU.mult, ALU.max))
                if n >= 2:
                    dve.wait_ge(sig("rr"), n - 1)
                    dve.wait_ge(sig("en"), n - 1)
                for b in range(B):
                    t = slice(b * S, (b + 1) * S)
                    ins = dve.tensor_tensor_scan(LOGR[n % 2][:, t], LAN[n % 2][:, t], tiny, 0.0, ALU.add, ALU.max)
                ins.then_inc(sig("logr"), 1)

            def accumulate(n):
                dve.wait_ge(sig("en"), n + 1)
                dve.wait_ge(sig("dxb"), n + 1)
                if n:
                    dve.wait_ge(sig("s_sum"), n)
                dve.scalar_tensor_tensor(WW, EN[n % 2], CLAMP_EXP, DXB[n % 2], ALU.min, ALU.mult)\
                    .then_inc(sig("input"), 1)
                dve.wait_ge(sig("input"), n + 1)
                if n >= 2:
                    dve.wait_ge(sig("state"), n - 1)
                dve.tensor_tensor_scan(SS[n % 2], CARRY, WW, 0.0, ALU.mult, ALU.add).then_inc(sig("s_sum"), 1)

            def output(n):
                dve.wait_ge(sig("state"), n + 1)
                dve.wait_ge(sig("c_psum"), n + 1)
                if n >= 2:
                    dve.wait_ge(sig("summed"), n - 1)
                dve.tensor_tensor(HC[n % 2], HH[n % 2], two(2 + 2 * (n % 2)), ALU.mult).then_inc(sig("c_read"), 1)

            decay(0)
            for n in range(NS):
                if n + 1 < NS:
                    decay(n + 1)
                accumulate(n)
                if n:
                    output(n - 1)
            output(NS - 1)
            dve.wait_ge(sig("summed"), NS)
            dve.scalar_tensor_tensor(LA, XNT[:, :], ssmc[:, 1:2], two(6), ALU.mult, ALU.add).then_inc(sig("y_ready"), 1)
            for half in range(2):
                dve.wait_ge(sig("y_turned"), half + 1)
                x = X[:, 4 * half:4 * half + 4, :].rearrange("p j d -> p (j d)")
                ins = dve.tensor_tensor(x, x, bank(half), ALU.add)
            ins.then_inc(sig("x_res"), 1)

        HB = OTf.rearrange("p (j f) -> p j f", j=NT)
        GG = VAf.rearrange("p (j f) -> p j f", j=NT)
        ROUNDED = SCR[:, 0, :]
        QB = SCR[:, 1, 0:T // 2].bitcast(BF16)
        QTB = SCR[:, 1, T // 2:T].bitcast(BF16)
        GQ = SCR[:, 2, 0:T // 2].bitcast(BF16).rearrange("p (s f) -> p s f", s=2)
        GQT = SCR[:, 2, T // 2:T].bitcast(BF16).rearrange("p (s f) -> p s f", s=2)
        SQ = SCR[:, 3, 0:HALF]

        def feed_weight_sums(dve, ch):
            dve.wait_ge(sig("ffn_in"), 16 * 2)
            ch.link(dve.tensor_reduce(wsum[:, :], wraw[:, :, :], AX, ALU.add, apply_absolute_value=True))
            dve.tensor_copy(wscale[:, :], wsum[:, :]).then_inc(sig("w_sums"), 1)

        def feed_weights(dve, ch):
            dve.wait_ge(sig("w_total"), 1)
            ch.link(dve.tensor_scalar(wmean[:, :], bank(7)[:, 0:2], 1.0 / (FF * D), 1e-5, ALU.mult, ALU.max))
            ch.link(dve.reciprocal(wscale[:, :], wmean[:, :]))
            for w, dst in ((0, wq1[:, :]), (1, wq2[:, :, :].rearrange("p c d -> p (c d)"))):
                raw = wraw[:, w, :]
                ch.link(dve.tensor_scalar(raw, raw, wscale[:, w:w + 1], ROUND, ALU.mult, ALU.add))
                ch.link(dve.tensor_scalar(raw, raw, -ROUND, 1.0, ALU.add, ALU.min))
                dve.tensor_scalar(dst, raw, -1.0, None, ALU.max).then_inc(sig("w_quantised"), 1)

        def quant_factors(dve, ch, w):
            ch.link(dve.tensor_tensor(peak, peak, rstd[:, :], ALU.mult))
            ch.link(dve.tensor_scalar(peak, peak, 1e-5, None, ALU.max))
            ch.link(dve.reciprocal(fac, peak))
            dve.tensor_scalar(deq, peak, 1.0 / 127.0, wmean[:, w:w + 1], ALU.mult, ALU.mult)
            ch.link(dve.scalar_tensor_tensor(fac, fac, 127.0, rstd[:, :], ALU.mult, ALU.mult))

        def feed_vector(dve, ch):
            dve.wait_ge(sig("xn"), 2 * 7)
            norm_stats(dve, ch, XN, 11, 1e-5, mean_square=True)
            ch.link(dve.tensor_reduce(peak, XN[:, :, :], AX, ALU.max, apply_absolute_value=True))
            norm_refine(dve, ch, 11)
            quant_factors(dve, ch, 0)
            for j in range(NT):
                ins = dve.tensor_scalar(ROUNDED[:, j * P:(j + 1) * P], XN[:, j, :], fac[:, j:j + 1], ROUND,
                                        ALU.mult, ALU.add)
            ch.link(ins)
            dve.tensor_scalar(QB, ROUNDED, -ROUND, 127.0, ALU.add, ALU.min).then_inc(sig("q1"), 1)
            b2 = b2bc.unsqueeze(1).to_broadcast([P, NT, D])
            ch.link(dve.tensor_tensor(X[:, :, :], X[:, :, :], b2, ALU.add))
            for j in range(NT):
                dve.wait_ge(sig("h1"), j + 1)
                dve.scalar_tensor_tensor(HB[:, j, :], bank(1 + j % 2), deq[:, j:j + 1], b1bc, ALU.mult, ALU.add)\
                    .then_inc(sig("h1_read"), 1)
                if j:
                    dve.wait_ge(sig("gelu"), j)
                    dve.tensor_reduce(peak[:, j - 1:j], GG[:, j - 1, :], AX, ALU.max, apply_absolute_value=True)
            dve.wait_ge(sig("gelu"), NT)
            ch.link(dve.tensor_reduce(peak[:, NT - 1:NT], GG[:, NT - 1, :], AX, ALU.max, apply_absolute_value=True))
            dve.wait_ge(sig("sumsq"), 1)
            dve.tensor_scalar(ve[:, :], sumsq, 1.0 / FF, 1e-5, ALU.mult, ALU.add).then_inc(sig("ve"), 1)
            norm_refine(dve, ch, 12)
            quant_factors(dve, ch, 1)

            def finish(j):
                dve.wait_ge(sig("h2"), j + 1)
                dve.scalar_tensor_tensor(X[:, j, :], bank(6 + j % 2)[:, 0:D], deq[:, j:j + 1], X[:, j, :],
                                         ALU.mult, ALU.add).then_inc(sig("x_tile"), 1)

            for j in range(NT):
                ch.link(dve.tensor_scalar(HB[:, j, :], GG[:, j, :], fac[:, j:j + 1], ROUND, ALU.mult, ALU.add))
                if j >= 2:
                    dve.wait_ge(sig("g_turned"), j - 1)
                dve.tensor_scalar(GQ[:, j % 2, :], HB[:, j, :], -ROUND, 127.0, ALU.add, ALU.min)\
                    .then_inc(sig("q2"), 1)
                if j >= 2:
                    finish(j - 2)
            finish(NT - 2)
            finish(NT - 1)

        def feed_tensor(pe):
            pe.wait_ge(sig("q1"), 1)
            for j in range(NT):
                ins = pe.transpose(halfbank(3)[:, j * P:(j + 1) * P], QB[:, j * P:(j + 1) * P], identb[:, :])
            ins.then_inc(sig("q_turned"), 1)
            pe.wait_ge(sig("qt1"), 1)
            for j in range(NT):
                if j >= 2:
                    pe.wait_ge(sig("h1_read"), j - 1)
                pe.matmul(bank(1 + j % 2), QTB[:, j * P:(j + 1) * P], wq1[:, :], start=True, stop=True)\
                    .then_inc(sig("h1"), 1)

            def second(j):
                pe.wait_ge(sig("gt"), j + 1)
                if j >= 2:
                    pe.wait_ge(sig("x_tile"), j - 1)
                for c in range(FF // P):
                    ins = pe.matmul(bank(6 + j % 2)[:, 0:D], GQT[:, j % 2, c * P:(c + 1) * P], wq2[:, c, :],
                                    start=(c == 0), stop=(c == FF // P - 1))
                ins.then_inc(sig("h2"), 1)

            for j in range(NT):
                pe.wait_ge(sig("q2"), j + 1)
                if j >= 2:
                    pe.wait_ge(sig("gt"), j - 1)
                for c in range(FF // P):
                    ins = pe.transpose(halfbank(4 + j % 2)[:, c * P:(c + 1) * P], GQ[:, j % 2, c * P:(c + 1) * P],
                                       identb[:, :])
                ins.then_inc(sig("g_turned"), 1)
                if j:
                    second(j - 1)
            second(NT - 1)

        def feed_scalar(act, ch):
            norm_root(act, ch, 11)
            act.wait_ge(sig("q_turned"), 1)
            act.activation(QTB, halfbank(3)[:, 0:T], ACT.Copy).then_inc(sig("qt1"), 1)
            for j in range(NT):
                act.wait_ge(sig("h1_read"), j + 1)
                act.activation(GG[:, j, :], HB[:, j, :], ACT.Gelu).then_inc(sig("gelu"), 1)
                act.wait_ge(sig("gelu"), j + 1)
                ins = act.activation(SQ, GG[:, j, :], ACT.Square, accum_out=sumsq[:, j:j + 1])
            ins.then_inc(sig("sumsq"), 1)
            norm_root(act, ch, 12)
            for j in range(NT):
                act.wait_ge(sig("g_turned"), j + 1)
                if j >= 2:
                    act.wait_ge(sig("h2"), j - 1)
                act.activation(GQT[:, j % 2, :], halfbank(4 + j % 2)[:, 0:FF], ACT.Copy).then_inc(sig("gt"), 1)

        @block.sync
        def _(sp):
            def load(dst, src, signal):
                sp.dma_start(dst, src).then_inc(sig(signal), 16)

            load(X[:, :, :], inp["x"].rearrange("(j p) d -> p j d", p=P), "x_in")
            load(CT, inp["ctxT"], "ctx_in")
            load(wx[:, :, :, :], inp["w_x"].rearrange("l w p d -> p l w d"), "wx_in")
            load(wself[:, :, :], inp["w_self"].rearrange("w p d -> p w d"), "wself_in")
            load(bg[:, 0:1], inp["bg"].rearrange("(p o) -> p o", o=1), "bg_in")
            load(lens[:, :], inp["lens"].partition_broadcast(P), "lens_in")
            load(wox[:, :, :, :], inp["w_out"].rearrange("l g p d -> p l g d"), "wox_in")
            load(router[:, :], inp["router"], "router_in")
            load(normw[:, :], inp["normw"].rearrange("(p o) -> p o", o=1), "router_in")
            load(bqk[:, 0:2], inp["bqk"], "bqk_in")
            load(brow[0:1, :], inp["bv"].rearrange("(o d) -> o d", o=1), "brow_in")
            load(wssm[:, :], inp["w_ssm"], "ssm_in")
            load(wdt[:, :], inp["w_dt"], "ssm_in")
            load(ssmc[:, 0:1], inp["b_dt"].rearrange("(p o) -> p o", o=1), "ssm_in")
            load(ssmc[:, 1:2], inp["Dskip"].rearrange("(p o) -> p o", o=1), "ssm_in")
            load(amat[:, :], inp["A_log"], "ssm_in")
            stack_self(sp, range(0, 9, 2), between=lambda: stack_context(sp, 0))

            def cross_sync(L):
                stack_queries(sp, L, range(0, 9, 2))
                for b in range(B):
                    sp.wait_ge(sig("maxed"), (L * B + b + 1) * STEPS)
                    sp.dma_start(QS[MAX_ROW:MAX_ROW + 3, :, b * S:(b + 1) * S], mx_rows[:, b, :])\
                        .then_inc(sig("max_in%d" % b), 16)

            cross_sync(0)
            load(KSf[:, 0:2048], inp["w1"].rearrange("e p f -> p e f"), "experts_in")
            load(KSf[:, 2048:4096], inp["w3"].rearrange("e p f -> p e f"), "experts_in")
            load(W2, inp["w2"].rearrange("e (c p) d -> p e c d", p=P), "experts_in")
            load(wraw[:, 0, :], inp["w1T"], "ffn_in")
            load(wraw[:, 1, :].rearrange("p (c d) -> p c d", c=FF // P),
                 inp["w2T"].rearrange("(c p) d -> p c d", p=P), "ffn_in")
            x_ready(sp, 2)
            load(CT, inp["ctxT"], "ctx_in")
            load(PAD, inp["pad"].partition_broadcast(P), "pad_in")
            load(FRAW, inp["fside"].rearrange("w p n -> p w n"), "fside_in")
            stack_context(sp, 1)
            x_ready(sp, 4)
            load(b1bc, inp["b1"].partition_broadcast(P), "bias_in")
            load(b2bc, inp["b2"].partition_broadcast(P), "bias_in")
            load(bobc, inp["bo"].partition_broadcast(P), "bias_in")
            load(BIASF.rearrange("p (w n) -> p w n", w=QT), inp["fside"][QT:].rearrange("w p n -> p w n"), "bias_in")
            cross_sync(1)
            for j in range(NT):
                sp.wait_ge(sig("x_tile"), j + 1)
                sp.dma_start(out[j * P:(j + 1) * P, :], X[:, j, :]).then_inc(sig("stored"), 16)
            sp.wait_ge(sig("stored"), 16 * NT)

        @block.gpsimd
        def _(pool):
            ch = Chain(pool, "pool_step")
            ch.link(pool.memset(ident[:, :], 0.0))
            pool.affine_select(out=ident[:, :], in_=ident[:, :], compare_op=ALU.not_equal, fill=1.0,
                               base=0, pattern=[[-1, P]], channel_multiplier=1).then_inc(sig("ident"), 1)
            pool.memset(spread[:, :], 0.0)
            ch.link(pool.memset(masks[:, :, :], 1.0))
            heads = spread[:, :].rearrange("p (i e) -> p i e", i=HG)
            pool.affine_select(out=heads, in_=heads, compare_op=ALU.not_equal, fill=1.0, base=-DH,
                               pattern=[[-32, HG], [0, 32]], channel_multiplier=1)
            causal = masks[:, 0:3:2, :]
            pool.affine_select(out=causal, in_=causal, compare_op=ALU.is_ge, fill=0.0,
                               base=0, pattern=[[0, 2], [1, P]], channel_multiplier=-1).then_inc(sig("const"), 1)
            pool.wait_ge(sig("const"), 1)
            pool.memset(KSf[64:128, :], 0.0).then_inc(sig("ka_clear"), 1)
            pool.wait_ge(sig("ka_clear"), 1)
            pool.memset(QSf[64:96, :], ONES_PAIR).then_inc(sig("q_clear"), 1)
            pool.wait_ge(sig("q_clear"), 1)
            pool.memset(VA[:, :, :, DH + 1:32], 0.0)
            pool.memset(VA[:, :, :, DH:DH + 1], 1.0).then_inc(sig("va_const"), 1)
            pool.wait_ge(sig("lens_in"), 16)
            pool.tensor_scalar(lensf[:, :], lens[:, :], 1.0, 0.0, ALU.mult, ALU.add)
            ch.link(pool.iota(iota, pattern=[[1, S]], base=0, channel_multiplier=0))
            ch.link(pool.tensor_scalar(iotaf, iota, 1.0, 0.0, ALU.mult, ALU.add))
            context_keys_pool(pool, ch, 0, NEG_X0)
            pool.wait_ge(sig("neg_parts"), 1)
            ch.link(pool.memset(KXf[96:128, :], ONES_PAIR))
            pool.memset(VX[:, :, :, DH + 1:32], 0.0).then_inc(sig("kx_clear"), 1)
            pool.memset(VX[:, :, :, DH:DH + 1], 1.0).then_inc(sig("vx_const"), 1)
            pool.tensor_scalar(identb[:, :], ident[:, :], 1.0, 0.0, ALU.mult, ALU.add)
            ch.link(pool.memset(tri[:, :, :], 1.0))
            pool.affine_select(out=tri[:, :, :], in_=tri[:, :, :], compare_op=ALU.is_ge, fill=0.0,
                               base=-1, pattern=[[1, NE], [-1, NE]], channel_multiplier=0)\
                .then_inc(sig("const_late"), 1)
            x_ready(pool, 2)
            pool.memset(QSf[96:128, :], 0.0).then_inc(sig("q_clear"), 1)
            pool.wait_ge(sig("q_clear"), 2)
            pool.wait_ge(sig("fside_in"), 16)
            pool.wait_ge(sig("w_quantised"), 2)
            pool.tensor_scalar(BIASQ, FRAW[:, 0:QT, :], 1.0, 0.0, ALU.mult, ALU.add)
            ch.link(pool.tensor_scalar(BIASK[:, :, 0, :], FRAW[:, QT:, :], 1.0, 0.0, ALU.mult, ALU.add))
            rest = KXR[:, 0:QT * S].rearrange("p (w n) -> p w n", w=QT)
            ch.link(pool.tensor_tensor(rest, FRAW[:, QT:, :], BIASK[:, :, 0, :], ALU.subtract))
            ch.link(pool.tensor_scalar(BIASK[:, :, 1, :], rest, 1.0, 0.0, ALU.mult, ALU.add))
            pool.tensor_tensor(BIASK[:, :, 2, :], rest, BIASK[:, :, 1, :], ALU.subtract)\
                .then_inc(sig("bias_parts"), 1)
            pool.wait_ge(sig("bias_parts"), 1)
            context_keys_pool(pool, ch, 1, NEG_X1)
            pool.wait_ge(sig("stack_k"), 16 * 24)
            scan_pool(pool)

        @block.tensor
        def _(pe):
            context_tensor(pe)
            norm_turn(pe, XN, 0)
            self_tensor(pe)
            norm_turn(pe, XN, 1)
            cross_tensor(pe, 0)
            experts_tensor(pe)
            half_turn(pe, 1, 5)
            scan_tensor(pe)
            norm_turn(pe, XN, 5)
            cross_tensor(pe, 1)
            feed_tensor(pe)

        @block.scalar
        def _(act):
            ch = Chain(act, "act_step")
            act.wait_ge(sig("ident"), 1)
            cleared = KXf[64:96, :].rearrange("p (a n) -> p a n", n=P)
            zeros = ident[64:96, :].unsqueeze(1).to_broadcast([32, 32, P])
            exp_and_ln(act)
            act.activation(cleared[:, 0:32, :], zeros, ACT.Copy, scale=0.0)
            norm_root(act, ch, 0)
            act.activation(cleared[:, 32:64, :], zeros, ACT.Copy, scale=0.0).then_inc(sig("kx_zero"), 1)
            context_scalar(act)
            norm_take(act, 0)
            self_scalar(act, ch)
            norm_root(act, ch, 1)
            norm_take(act, 1)
            cross_scalar(act, ch, 0)
            norm_root(act, ch, 2)
            experts_scalar(act, ch)
            norm_root(act, ch, 8, tiles_of(1))
            half_take(act, 1, 5)
            scan_scalar(act, ch)
            norm_root(act, ch, 9)
            norm_take(act, 5)
            cross_scalar(act, ch, 1)
            norm_root(act, ch, 10)
            feed_scalar(act, ch)

        @block.vector
        def _(dve):
            ch = Chain(dve, "dve_step")
            dve.wait_ge(sig("x_in"), 16)

            def layer_norm(k):
                norm_stats(dve, ch, X if k in (0, 9) else None, k, 1e-5)
                norm_refine(dve, ch, k)

            layer_norm(0)
            norm_apply(dve, XN, X)
            self_vector(dve, ch)
            dve.wait_ge(sig("const_late"), 1)
            x_ready(dve, 1)
            layer_norm(1)
            norm_apply(dve, XN, X)
            cross_vector(dve, ch, 0)
            x_ready(dve, 2)
            layer_norm(2)
            for j in range(NT):
                ins = dve.tensor_scalar(XN[:, j, :], X[:, j, :], mv[:, j, 0:1], rstd[:, j:j + 1],
                                        ALU.subtract, ALU.mult)
            ch.link(ins)
            experts_vector(dve, ch)
            x_ready(dve, 3)
            half_norm(dve, ch, 1)
            scan_vector(dve, ch)
            x_ready(dve, 4)
            layer_norm(9)
            norm_apply(dve, XN, X)
            dve.wait_ge(sig("xn"), 2 * 6)
            dve.wait_ge(sig("bias_in"), 16 * 4)
            ch.link(dve.tensor_tensor(X[:, :, :], X[:, :, :], bobc.unsqueeze(1).to_broadcast([P, NT, D]), ALU.add))
            cross_vector(dve, ch, 1)
            x_ready(dve, 5)
            layer_norm(10)
            norm_apply(dve, XN, X)
            feed_vector(dve, ch)


def kernel(**inputs):
    import numpy as np
    import concourse.bacc as bacc
    from concourse import mybir as mb
    from concourse.bass_utils import run_bass_kernel_spmd

    a = {k: np.asarray(v) for k, v in inputs.items()}

    def by_feature(w):
        return w.reshape(H, DH, D).transpose(2, 1, 0).reshape(D, D)

    def padded(w):
        full = np.zeros((NG, HG, 32, D), w.dtype)
        full[:, :, 0:DH] = w.T.reshape(NG, HG, DH, D)
        return full.reshape(NG, P, D)

    arrays = {
        "x": a["x"].reshape(T, D),
        "ctxT": a["ctx_1024"].reshape(T, D).T,
        "w_self": np.stack([by_feature(a["L0_attn_Wq"]), by_feature(a["L0_attn_Wk"]), by_feature(a["L0_attn_Wg"]),
                            a["L0_attn_Wv"].T]),
        "bg": a["L0_attn_bg"].reshape(H, DH).T.reshape(D),
        "w_x": np.stack([np.stack([by_feature(a["L0_xattn_W_q"]), by_feature(a["L0_xattn_W_k"]), a["L0_xattn_W_v"].T]),
                         np.stack([by_feature(a["L1_xattn_Wq"]), by_feature(a["L1_xattn_Wk"]), a["L1_xattn_Wv"].T])]),
        "w_out": np.stack([padded(a["L0_attn_Wo"]), padded(a["L0_xattn_W_o"]), padded(a["L1_xattn_Wo"])]),
        "lens": a["mask_B_ik0"],
        "pad": a["mask_BxS2_bk0"].reshape(T),
        "fside": np.concatenate([a["fside_SxS2_0"].reshape(QT, P, S), a["fside_SxS2_0"].T.reshape(QT, P, S)]),
        "bqk": np.stack([a["L1_xattn_bq"].reshape(H, DH).T.reshape(D), a["L1_xattn_bk"].reshape(H, DH).T.reshape(D)], 1),
        "bv": a["L1_xattn_bv"], "bo": a["L1_xattn_bo"],
        "router": a["L0_ffn_router_w"],
        "normw": a["L0_ffn_norm_w"],
        "w1": a["L0_ffn_w1"], "w3": a["L0_ffn_w3"], "w2": a["L0_ffn_w2"],
        "w_ssm": a["L1_attn_W_xproj"], "w_dt": a["L1_attn_W_dt"], "b_dt": a["L1_attn_b_dt"],
        "Dskip": a["L1_attn_D"], "A_log": a["L1_attn_A_log"],
        "w1T": a["L1_ffn_w1"].T, "w2T": a["L1_ffn_w2"].T, "b1": a["L1_ffn_b1"], "b2": a["L1_ffn_b2"],
    }
    nc = bacc.Bacc("TRN2", target_bir_lowering=False, num_devices=1)
    arrays = {k: np.ascontiguousarray(v) for k, v in arrays.items()}
    inp = {k: nc.dram_tensor("in_" + k, v.shape, mb.dt.from_np(v.dtype), kind="ExternalInput").ap()
           for k, v in arrays.items()}
    out = nc.dram_tensor("out_x", (T, D), mb.dt.float32, kind="ExternalOutput").ap()
    build(nc, inp, out)
    r = run_bass_kernel_spmd(nc, [{"in_" + k: v for k, v in arrays.items()}], core_ids=[0])
    return r.results[0]["out_x"].reshape(B, S, D)
```
